# Optimizing a Trainium2 kernel written in Bass

```python
import numpy as np
import jax
import jax.numpy as jnp

def _softmax(x, axis=-1):
    return jax.nn.softmax(x, axis=axis)

def _gelu(x):
    return jax.nn.gelu(x, approximate=True)

def _silu(x):
    return jax.nn.silu(x)

def _sigmoid(x):
    return jax.nn.sigmoid(x)

def _layernorm(x, axis=-1, eps=1e-05):
    m = jnp.mean(x, axis=axis, keepdims=True)
    v = jnp.var(x, axis=axis, keepdims=True)
    return (x - m) / jnp.sqrt(v + eps)

def _scatter_add(tgt, idx, src, axis=0):
    return tgt.at[idx].add(src)

def _segment_sum(src, seg, n):
    return jax.ops.segment_sum(src, seg, n)
kernel_name = 'mk_xattn_ffn_d2_seqx_r4_fa2ed1'

def setup_inputs(seed: int=0):
    np.random.seed(seed)
    _w = jnp.asarray

    def _rec_inputs():
        import jax
        import jax.numpy as jnp
        _rk = jax.random.key(seed)
        x = -0.0005146 + 1 * jax.random.normal(jax.random.fold_in(_rk, 1), (4, 1024, 256), jnp.float32)
        _lenS = 1024 - jax.random.randint(jax.random.fold_in(_rk, 7), (4,), 0, max(1, 1024 // 4) + 1, jnp.int32)
        _lenS2 = 77 - jax.random.randint(jax.random.fold_in(_rk, 8), (4,), 0, max(1, 77 // 4) + 1, jnp.int32)
        _ctx_768P = jax.random.normal(jax.random.fold_in(_rk, 11), (4, 16, 192), jnp.float32)
        _ctx_768c = jax.random.dirichlet(jax.random.fold_in(_rk, 511), 0.3 * jnp.ones((16,), jnp.float32), (4, 77))
        _ctx_768t = jnp.einsum('bsk,bkd->bsd', _ctx_768c, _ctx_768P)
        _ctx_768t = _ctx_768t * jax.lax.rsqrt(jnp.mean(jnp.square(_ctx_768t)) + 1e-12) * 0.953939
        ctx_768 = -0.00040386 + 0.999972 * (_ctx_768t + 0.3 * jax.random.normal(jax.random.fold_in(_rk, 611), (4, 77, 192), jnp.float32))
        _validS = jnp.arange(1024)[None, :] < _lenS[:, None]
        _validS2 = jnp.arange(77)[None, :] < _lenS2[:, None]
        _causal = jnp.tril(jnp.ones((1024, 1024), dtype=bool))
        mask_BxS2_bk0 = jnp.logical_not(jnp.broadcast_to(_validS2[:, :], (4, 77)))
        mask_BxS2_bf1 = jnp.ones((4, 77), dtype=bool)
        return (x, ctx_768, mask_BxS2_bk0, mask_BxS2_bf1)
    x, ctx_768, mask_BxS2_bk0, mask_BxS2_bf1 = _rec_inputs()

    def _L0_xattn_setup():
        import jax, jax.numpy as jnp
        import numpy as np
        DIM_IN, DIM_LAT, DIM_HEAD = (192, 256, 64)
        INNER = max(DIM_LAT, DIM_IN)
        HEADS = INNER // DIM_HEAD
        SCALE = DIM_HEAD ** (-0.5)
        RMS_EPS = 1e-08
        LN_EPS = 1e-05

        def layernorm(x, g, b):
            mu = jnp.mean(x, axis=-1, keepdims=True)
            var = jnp.mean((x - mu) ** 2, axis=-1, keepdims=True)
            return (x - mu) * jax.lax.rsqrt(var + LN_EPS) * g + b

        def rmsnorm(x, gamma):
            norm = jnp.sqrt(jnp.sum(x * x, axis=-1, keepdims=True)) * x.shape[-1] ** (-0.5)
            return x / jnp.maximum(norm, RMS_EPS) * gamma
        key = jax.random.key(seed)
        ks = jax.random.split(key, 12)
        b, n, m = (4, 1024, 128)
        x = jax.random.normal(ks[0], (b, n, DIM_IN), jnp.float32)
        latents = jax.random.normal(ks[1], (b, m, DIM_LAT), jnp.float32)
        mask = jax.random.randint(ks[2], (b, n), 0, 2).astype(bool)
        s = lambda k, sh, fan: jax.random.normal(k, sh, jnp.float32) * fan ** (-0.5)
        return {'x': x, 'latents': latents, 'mask': mask, 'ln_x_g': jnp.ones((DIM_IN,), jnp.float32), 'ln_x_b': jnp.zeros((DIM_IN,), jnp.float32), 'ln_l_g': jnp.ones((DIM_LAT,), jnp.float32), 'ln_l_b': jnp.zeros((DIM_LAT,), jnp.float32), 'qn_g': jnp.ones((DIM_HEAD,), jnp.float32), 'kn_g': jnp.ones((DIM_HEAD,), jnp.float32), 'Wq': s(ks[3], (INNER, DIM_LAT), DIM_LAT), 'Wkv': s(ks[4], (2 * INNER, DIM_IN), DIM_IN), 'Wlkv': s(ks[5], (2 * INNER, DIM_LAT), DIM_LAT), 'Wo': s(ks[6], (DIM_LAT, INNER), INNER), 'bo': jnp.zeros((DIM_LAT,), jnp.float32)}
    _L0_xattn_all = _L0_xattn_setup()
    _L0_xattn_in = {k: v for k, v in _L0_xattn_all.items() if k in ('ln_x_g', 'ln_x_b', 'ln_l_g', 'ln_l_b', 'qn_g', 'kn_g', 'Wq', 'Wkv', 'Wlkv', 'Wo', 'bo')}
    del _L0_xattn_all

    def _L0_ffn_setup():
        import jax, jax.numpy as jnp
        import numpy as np
        B, N, C, F, E, K = (2, 512, 256, 1024, 8, 2)
        key = jax.random.key(seed)
        k = jax.random.split(key, 6)
        xavier1 = float(np.sqrt(6.0 / (C + F)))
        xavier2 = float(np.sqrt(6.0 / (F + C)))
        return {'x': jax.random.normal(k[0], (B, N, C), dtype=jnp.float32), 'router_w': jax.random.normal(k[1], (E, C), dtype=jnp.float32) * 0.01, 'w1': jax.random.uniform(k[2], (E, F, C), dtype=jnp.float32, minval=-xavier1, maxval=xavier1), 'b1': jnp.zeros((E, F), dtype=jnp.float32), 'w2': jax.random.uniform(k[3], (E, C, F), dtype=jnp.float32, minval=-xavier2, maxval=xavier2), 'b2': jnp.zeros((E, C), dtype=jnp.float32)}
    _L0_ffn_all = _L0_ffn_setup()
    _L0_ffn_in = {k: v for k, v in _L0_ffn_all.items() if k in ('router_w', 'w1', 'b1', 'w2', 'b2')}
    del _L0_ffn_all

    def _L1_xattn_setup():
        import jax, jax.numpy as jnp
        import numpy as np
        DIM = 256
        CTX_DIM = 192
        HEADS = 16
        key = jax.random.key(seed)
        ks = jax.random.split(key, 7)
        B, N, M = (4, 1024, 64)
        x = jax.random.normal(ks[0], (B, N, DIM), dtype=jnp.float32)
        context = jax.random.normal(ks[1], (B, M, CTX_DIM), dtype=jnp.float32)
        context_mask = jnp.ones((B, M), dtype=bool)
        s_d = 1.0 / np.sqrt(DIM)
        s_c = 1.0 / np.sqrt(CTX_DIM)
        Wq = jax.random.normal(ks[2], (DIM, DIM), dtype=jnp.float32) * s_d
        Wk = jax.random.normal(ks[3], (CTX_DIM, DIM), dtype=jnp.float32) * s_c
        Wv = jax.random.normal(ks[4], (CTX_DIM, DIM), dtype=jnp.float32) * s_c
        Wo = jax.random.normal(ks[5], (DIM, DIM), dtype=jnp.float32) * s_d
        return {'x': x, 'context': context, 'context_mask': context_mask, 'Wq': Wq, 'Wk': Wk, 'Wv': Wv, 'Wo': Wo}
    _L1_xattn_all = _L1_xattn_setup()
    _L1_xattn_in = {k: v for k, v in _L1_xattn_all.items() if k in ('Wq', 'Wk', 'Wv', 'Wo')}
    del _L1_xattn_all

    def _L1_ffn_setup():
        import jax, jax.numpy as jnp
        import numpy as np
        B, S, D, H, E, TOP_K = (4, 512, 256, 512, 8, 2)
        key = jax.random.key(seed)
        ks = jax.random.split(key, 5)
        scale_d = 1.0 / np.sqrt(D)
        scale_h = 1.0 / np.sqrt(H)
        return {'x': jax.random.normal(ks[0], (B, S, D), dtype=jnp.float32), 'gate_w': jax.random.normal(ks[1], (D, E), dtype=jnp.float32) * scale_d, 'w1': jax.random.normal(ks[2], (E, D, H), dtype=jnp.float32) * scale_d, 'w2': jax.random.normal(ks[3], (E, D, H), dtype=jnp.float32) * scale_d, 'w3': jax.random.normal(ks[4], (E, H, D), dtype=jnp.float32) * scale_h}
    _L1_ffn_all = _L1_ffn_setup()
    _L1_ffn_in = {k: v for k, v in _L1_ffn_all.items() if k in ('gate_w', 'w1', 'w2', 'w3')}
    del _L1_ffn_all
    return {'x': x, 'ctx_768': ctx_768, 'mask_BxS2_bk0': mask_BxS2_bk0, 'mask_BxS2_bf1': mask_BxS2_bf1, 'L0_xattn_ln_x_g': _L0_xattn_in['ln_x_g'], 'L0_xattn_ln_x_b': _L0_xattn_in['ln_x_b'], 'L0_xattn_ln_l_g': _L0_xattn_in['ln_l_g'], 'L0_xattn_ln_l_b': _L0_xattn_in['ln_l_b'], 'L0_xattn_qn_g': _L0_xattn_in['qn_g'], 'L0_xattn_kn_g': _L0_xattn_in['kn_g'], 'L0_xattn_Wq': _L0_xattn_in['Wq'], 'L0_xattn_Wkv': _L0_xattn_in['Wkv'], 'L0_xattn_Wlkv': _L0_xattn_in['Wlkv'], 'L0_xattn_Wo': _L0_xattn_in['Wo'], 'L0_xattn_bo': _L0_xattn_in['bo'], 'L0_ffn_router_w': _L0_ffn_in['router_w'], 'L0_ffn_w1': _L0_ffn_in['w1'], 'L0_ffn_b1': _L0_ffn_in['b1'], 'L0_ffn_w2': _L0_ffn_in['w2'], 'L0_ffn_b2': _L0_ffn_in['b2'], 'L1_xattn_Wq': _L1_xattn_in['Wq'], 'L1_xattn_Wk': _L1_xattn_in['Wk'], 'L1_xattn_Wv': _L1_xattn_in['Wv'], 'L1_xattn_Wo': _L1_xattn_in['Wo'], 'L1_ffn_gate_w': _L1_ffn_in['gate_w'], 'L1_ffn_w1': _L1_ffn_in['w1'], 'L1_ffn_w2': _L1_ffn_in['w2'], 'L1_ffn_w3': _L1_ffn_in['w3']}

def reference(x, ctx_768, mask_BxS2_bk0, mask_BxS2_bf1, L0_xattn_ln_x_g, L0_xattn_ln_x_b, L0_xattn_ln_l_g, L0_xattn_ln_l_b, L0_xattn_qn_g, L0_xattn_kn_g, L0_xattn_Wq, L0_xattn_Wkv, L0_xattn_Wlkv, L0_xattn_Wo, L0_xattn_bo, L0_ffn_router_w, L0_ffn_w1, L0_ffn_b1, L0_ffn_w2, L0_ffn_b2, L1_xattn_Wq, L1_xattn_Wk, L1_xattn_Wv, L1_xattn_Wo, L1_ffn_gate_w, L1_ffn_w1, L1_ffn_w2, L1_ffn_w3):
    import jax
    import jax.numpy as jnp

    def _L0_xattn_ref(x, latents, mask, ln_x_g, ln_x_b, ln_l_g, ln_l_b, qn_g, kn_g, Wq, Wkv, Wlkv, Wo, bo):
        import jax, jax.numpy as jnp
        import numpy as np
        DIM_IN, DIM_LAT, DIM_HEAD = (192, 256, 64)
        INNER = max(DIM_LAT, DIM_IN)
        HEADS = INNER // DIM_HEAD
        SCALE = DIM_HEAD ** (-0.5)
        RMS_EPS = 1e-08
        LN_EPS = 1e-05

        def layernorm(x, g, b):
            mu = jnp.mean(x, axis=-1, keepdims=True)
            var = jnp.mean((x - mu) ** 2, axis=-1, keepdims=True)
            return (x - mu) * jax.lax.rsqrt(var + LN_EPS) * g + b

        def rmsnorm(x, gamma):
            norm = jnp.sqrt(jnp.sum(x * x, axis=-1, keepdims=True)) * x.shape[-1] ** (-0.5)
            return x / jnp.maximum(norm, RMS_EPS) * gamma
        b, n, _ = x.shape
        m = latents.shape[1]
        xn = layernorm(x, ln_x_g, ln_x_b)
        ln = layernorm(latents, ln_l_g, ln_l_b)
        q = ln @ Wq.T
        kv = jnp.concatenate([xn @ Wkv.T, ln @ Wlkv.T], axis=1)
        k, v = (kv[..., :INNER], kv[..., INNER:])
        split_heads = lambda t: t.reshape(t.shape[0], t.shape[1], HEADS, DIM_HEAD).transpose(0, 2, 1, 3)
        q, k, v = (split_heads(q), split_heads(k), split_heads(v))
        qn = rmsnorm(q, qn_g) * SCALE
        kn = rmsnorm(k, kn_g)
        attn = jnp.einsum('bhid,bhjd->bhij', qn, kn)
        full_mask = jnp.pad(mask, ((0, 0), (0, m)), constant_values=True)
        attn = jnp.where(full_mask[:, None, None, :], attn, -jnp.finfo(attn.dtype).max)
        attn = jax.nn.softmax(attn, axis=-1)
        out = jnp.einsum('bhij,bhjd->bhid', attn, v)
        out = out.transpose(0, 2, 1, 3).reshape(b, m, INNER)
        return out @ Wo.T + bo

    def _L0_ffn_ref(x, router_w, w1, b1, w2, b2):
        import jax, jax.numpy as jnp
        import numpy as np
        B, N, C, F, E, K = (2, 512, 256, 1024, 8, 2)
        Bb, Nn, Cc = x.shape
        x_flat = x.reshape(-1, Cc)
        logits = jnp.einsum('tc,ec->te', x_flat, router_w)
        probs = jax.nn.softmax(logits, axis=-1)
        top_w, top_idx = jax.lax.top_k(probs, K)
        top_w = top_w / (jnp.sum(top_w, axis=-1, keepdims=True) + 1e-09)
        h = jnp.einsum('tc,efc->tef', x_flat, w1) + b1[None]
        h = jax.nn.relu(h)
        y = jnp.einsum('tef,ecf->tec', h, w2) + b2[None]
        sel = jnp.take_along_axis(y, top_idx[:, :, None], axis=1)
        out = jnp.einsum('tkc,tk->tc', sel, top_w)
        return out.reshape(Bb, Nn, Cc)

    def _L1_xattn_ref(x, context, context_mask, Wq, Wk, Wv, Wo):
        import jax, jax.numpy as jnp
        import numpy as np
        DIM = 256
        CTX_DIM = 192
        HEADS = 16
        B, N, _ = x.shape
        M = context.shape[1]
        hd = DIM // HEADS
        scale = hd ** (-0.5)
        q = (x @ Wq).reshape(B, N, HEADS, hd).transpose(0, 2, 1, 3)
        k = (context @ Wk).reshape(B, M, HEADS, hd).transpose(0, 2, 1, 3)
        v = (context @ Wv).reshape(B, M, HEADS, hd).transpose(0, 2, 1, 3)
        scores = jnp.einsum('bhid,bhjd->bhij', q, k) * scale
        max_neg = -jnp.finfo(scores.dtype).max
        scores = jnp.where(context_mask[:, None, None, :], scores, max_neg)
        attn = jax.nn.softmax(scores, axis=-1)
        out = jnp.einsum('bhij,bhjd->bhid', attn, v)
        out = out.transpose(0, 2, 1, 3).reshape(B, N, DIM)
        return out @ Wo

    def _L1_ffn_ref(x, gate_w, w1, w2, w3):
        import jax, jax.numpy as jnp
        import numpy as np
        B, S, D, H, E, TOP_K = (4, 512, 256, 512, 8, 2)
        gate_scores = jax.nn.softmax(x @ gate_w, axis=-1)
        top_vals, top_idx = jax.lax.top_k(gate_scores, TOP_K)
        mask = (jax.nn.one_hot(top_idx, E, dtype=x.dtype) * top_vals[..., None]).sum(axis=-2)
        weights = mask / (mask.sum(axis=-1, keepdims=True) + 1e-09)
        g = jax.nn.silu(jnp.einsum('bsd,edh->bseh', x, w1)) * jnp.einsum('bsd,edh->bseh', x, w2)
        expert_out = jnp.einsum('bseh,ehd->bsed', g, w3)
        return jnp.einsum('bse,bsed->bsd', weights, expert_out)
    x = x + _L0_xattn_ref(ctx_768, _layernorm(x, axis=-1), mask_BxS2_bk0, L0_xattn_ln_x_g, L0_xattn_ln_x_b, L0_xattn_ln_l_g, L0_xattn_ln_l_b, L0_xattn_qn_g, L0_xattn_kn_g, L0_xattn_Wq, L0_xattn_Wkv, L0_xattn_Wlkv, L0_xattn_Wo, L0_xattn_bo)
    x = x + _L0_ffn_ref(_layernorm(x, axis=-1), L0_ffn_router_w, L0_ffn_w1, L0_ffn_b1, L0_ffn_w2, L0_ffn_b2)
    x = x + _L1_xattn_ref(_layernorm(x, axis=-1), ctx_768, mask_BxS2_bf1, L1_xattn_Wq, L1_xattn_Wk, L1_xattn_Wv, L1_xattn_Wo)
    x = x + _L1_ffn_ref(_layernorm(x, axis=-1), L1_ffn_gate_w, L1_ffn_w1, L1_ffn_w2, L1_ffn_w3)
    return x

_drawn_inputs = setup_inputs


def setup_inputs(seed=0):
    import zlib

    import numpy as np

    out = dict(_drawn_inputs(seed))
    spreads = {'L0_xattn_ln_x_g': (1.0, 0.6),
     'L0_xattn_ln_x_b': (0.0, 0.348),
     'L0_xattn_ln_l_g': (1.0, 0.2),
     'L0_xattn_ln_l_b': (0.0, 0.1),
     'L0_xattn_qn_g': (1.0, 0.2),
     'L0_xattn_kn_g': (1.0, 0.2),
     'L0_xattn_bo': (0.0, 0.1),
     'L0_ffn_b1': (0.0, 0.1),
     'L0_ffn_b2': (0.0, 0.1)}
    factors = {}
    for name, (base, spread) in spreads.items():
        noise = np.random.default_rng([zlib.crc32(name.encode()), seed]).standard_normal(out[name].shape)
        drawn = base * np.exp(spread * noise) if base else spread * noise
        out[name] = jnp.asarray(drawn.astype(out[name].dtype))
    for name, factor in factors.items():
        out[name] = (out[name] * factor).astype(out[name].dtype)
    return out
```

```python
from contextlib import ExitStack

import concourse.bass as bass
from concourse import mybir

F32 = mybir.dt.float32
F16 = mybir.dt.float16
I32 = mybir.dt.int32
U32 = mybir.dt.uint32
U8 = mybir.dt.uint8
ALU = mybir.AluOpType
ACT = mybir.ActivationFunctionType
AX = mybir.AxisListType

P = 128
B = 4
S = 1024
T = B * S // P
TB = S // P
D = 256
DC = 192
M = 77
MP = 80
LN_EPS = 1e-5
RMS_EPS = 1e-8
MASKED = -1e30

H0, HD0 = 4, 64
SCALE0 = HD0 ** -0.5
H1, HD1 = 16, 16
SCALE1 = HD1 ** -0.5

E = 8
F0, F1 = 1024, 512
WS = 64.0


class Names:
    pass


class Mem:

    def __init__(self, nc, stack):
        self.nc, self.stack = nc, stack

    def sb(self, name, shape, dt=F32):
        return self.stack.enter_context(self.nc.sbuf_tensor(name, shape, dt))

    def ps(self, name, shape, dt=F32):
        return self.stack.enter_context(self.nc.psum_tensor(name, shape, dt))

    def sem(self, name):
        return self.stack.enter_context(self.nc.semaphore(name))


def setup(nc, mem, g, a):
    g.x = mem.sb("x_sb", [P, T, D])
    g.ident = mem.sb("ident", [P, P])
    g.ident16 = mem.sb("ident16", [P, P], F16)
    g.ones = mem.sb("ones", [P, P])
    g.neghalf = mem.sb("neghalf", [P, 64])
    g.ctxT = mem.sb("ctxT", [P, 2, B, MP])
    g.mean = mem.sb("mean", [P, T])
    g.rstd = mem.sb("rstd", [P, T])
    g.gain = mem.sb("gain", [P, HD0])
    g.shift = mem.sb("shift", [P, B + 1])
    g.pos = [mem.sb(f"pos{k}", [P, T], U32) for k in range(2)]
    g.wt = mem.sb("wt", [P, 2, T])
    g.expert = mem.sb("expert", [1, NT], I32)
    g.zeros = mem.sb("zeros", [P, 2 * D], F16)
    g.cleared = mem.sem("cleared")
    g.x_in = mem.sem("x_in")
    g.consts = mem.sem("consts")


def attention0_inputs(nc, g, a):
    with ExitStack() as st:
        m = Mem(nc, st)
        ctx = m.sb("ctx", [M, B, DC])
        zc = m.sb("zc", [M, B, DC])
        stats = m.sb("stats_c", [M, B, 6])
        mv = m.sb("mv_c", [M, B, 2])
        ve = m.sb("ve_c", [M, B])
        rstd = m.sb("rstd_c", [M, B])
        lnT = m.sb("lnT_c", [P, 2, B, M])
        gx = m.sb("gx", [P, 2])
        bx = m.sb("bx", [P, 2])
        wkv = m.sb("wkv", [P, 2, 2 * D])
        sq = m.sb("sq_c", [M, B, D])
        ss = m.sb("ss_c", [M, B * H0])
        rn = m.sb("rn_c", [M, B * H0])
        kn = m.sb("kn_c", [M, B * H0, HD0])
        khl = m.sb("khl_c", [M, B * H0, 3, HD0], F16)
        mask = m.sb("mask_c", [M, B], U8)
        gq = m.sb("gq_row", [P, HD0])
        gk = m.sb("gk_row", [P, HD0])
        gabs = m.sb("gabs", [P, 1])
        kv = m.ps("kv_c", [M, B, 2 * D])
        tr = m.ps("tr_c", [P, 4, 512])

        ld_ctx, ld_w, ld_g = m.sem("ld_ctx"), m.sem("ld_wkv"), m.sem("ld_g")
        v_step, p_step = m.sem("c_v_step"), m.sem("c_p_step")
        t_done, ev, kv_done, sq_done = m.sem("c_t_done"), m.sem("c_ev"), m.sem("c_kv"), m.sem("c_sq")
        hi_done, kt_done, kt_ev = m.sem("c_hi"), m.sem("c_ktd"), m.sem("c_ktev")
        z_zero = m.sem("z_zero")
        block = st.enter_context(nc.Block())

        @block.sync
        def _(sp):
            sp.wait_ge(z_zero, 1)
            sp.dma_start(g.zs.rearrange("(n p) d -> p n d", p=P),
                         g.zeros[:].rearrange("p (o d) -> p o d", o=1).to_broadcast([P, NT, 2 * D])).then_inc(g.cleared, 16)
            sp.dma_start(ctx[:], a["ctx"].rearrange("b m d -> m b d")).then_inc(ld_ctx, 16)
            for i in range(B):
                sp.dma_start(g.x[:, i * TB:(i + 1) * TB, :],
                             a["x"][i * S:(i + 1) * S, :].rearrange("(t p) d -> p t d", p=P)).then_inc(g.x_in, 16)

        @block.scalar
        def _(act):
            act.preload_act_table_set("natural_log_exp_and_others")
            act.dma_start(wkv[:, 0, :], a["WkvT"][0:P, :]).then_inc(ld_w, 16)
            act.dma_start(wkv[0:DC - P, 1, :], a["WkvT"][P:DC, :]).then_inc(ld_w, 16)
            for v, dst in ((a["ln_x_g"], gx), (a["ln_x_b"], bx)):
                act.dma_start(dst[:, 0:1], v[0:P].rearrange("(p o) -> p o", o=1)).then_inc(ld_g, 16)
                act.dma_start(dst[0:DC - P, 1:2], v[P:DC].rearrange("(p o) -> p o", o=1)).then_inc(ld_g, 16)
            act.dma_start(mask[:], a["mask0"].rearrange("b m -> m b"), allow_slow_non_contiguous=True).then_inc(ld_g, 16)
            act.dma_start(gq[:], a["qn_g"].partition_broadcast(P)).then_inc(ld_g, 16)
            act.dma_start(gk[:], a["kn_g"].partition_broadcast(P)).then_inc(ld_g, 16)
            act.wait_ge(t_done, 1)
            act.copy(g.ctxT[:, 0, :, 0:M], tr[:, 0, 0:B * M].rearrange("p (b m) -> p b m", b=B)).then_inc(ev, 1)
            act.copy(g.ctxT[0:DC - P, 1, :, 0:M],
                     tr[0:DC - P, 1, 0:B * M].rearrange("p (b m) -> p b m", b=B)).then_inc(ev, 1)
            act.wait_ge(t_done, 2)
            act.wait_ge(ld_g, 16 * 7)
            act.activation(lnT[:, 0], tr[:, 2, 0:B * M].rearrange("p (b m) -> p b m", b=B), ACT.Identity,
                           bias=bx[:, 0:1], scale=gx[:, 0:1]).then_inc(ev, 1)
            act.activation(lnT[0:DC - P, 1], tr[0:DC - P, 3, 0:B * M].rearrange("p (b m) -> p b m", b=B),
                           ACT.Identity, bias=bx[0:DC - P, 1:2], scale=gx[0:DC - P, 1:2]).then_inc(ev, 1)
            act.wait_ge(kv_done, 1)
            act.activation(sq[:], kv[:, :, 0:D], ACT.Square).then_inc(sq_done, 1)
            act.copy(g.vctx[:], kv[:, :, D:2 * D]).then_inc(sq_done, 1)
            act.wait_ge(v_step, 16)
            act.copy(khl[:, :, 0:3:2, :], kn[:].rearrange("p (h o) d -> p h o d", o=1).to_broadcast([M, B * H0, 2, HD0])
                     ).then_inc(hi_done, 1)
            act.wait_ge(kt_done, 1)
            t16 = tr[:].bitcast(F16)
            for n in range(4):
                act.copy(g.kctx[:, n // 2, (n % 2) * 8:(n % 2) * 8 + 8, 0:M],
                         t16[:, n, 0:8 * MP].rearrange("p (h m) -> p h m", h=8)[:, :, 0:M]).then_inc(kt_ev, 1)
            act.wait_ge(kt_ev, 4)

        @block.gpsimd
        def _(pool):
            pool.memset(g.zeros[:], 0.0).then_inc(z_zero, 1)
            pool.memset(g.ident[:], 0.0).then_inc(p_step, 1)
            pool.memset(g.ident16[:], 0.0).then_inc(p_step, 1)
            pool.memset(g.ones[:], 1.0).then_inc(g.consts, 1)
            pool.memset(g.neghalf[:], -0.5).then_inc(g.consts, 1)
            pool.wait_ge(p_step, 2)
            for t in (g.ident, g.ident16):
                pool.affine_select(out=t[:], in_=t[:], compare_op=ALU.not_equal, fill=1.0, base=0,
                                   pattern=[[-1, P]], channel_multiplier=1).then_inc(g.consts, 1)
            pool.wait_ge(g.consts, 4)
            pool.wait_ge(v_step, 9)
            pool.tensor_tensor(rstd[:], ve[:], g.neghalf[0:M, 0:B], ALU.pow).then_inc(p_step, 1)
            pool.wait_ge(v_step, 15)
            pool.tensor_tensor(rn[:], ss[:], g.neghalf[0:M, 0:B * H0], ALU.pow).then_inc(p_step, 1)
            pool.wait_ge(p_step, 4)

        @block.vector
        def _(dve):
            dve.wait_ge(ld_ctx, 16)
            for b in range(B):
                dve.bn_stats(stats[:, b, :], ctx[:, b, :]).then_inc(v_step, 1)
            dve.wait_ge(v_step, 4)
            for b in range(B):
                dve.bn_aggr(mv[:, b, :], stats[:, b, :]).then_inc(v_step, 1)
            dve.wait_ge(v_step, 8)
            dve.tensor_scalar(ve[:], mv[:, :, 1], LN_EPS, None, ALU.add).then_inc(v_step, 1)
            dve.wait_ge(p_step, 3)
            for b in range(B):
                dve.tensor_scalar(zc[:, b, :], ctx[:, b, :], mv[:, b, 0:1], rstd[:, b:b + 1],
                                  ALU.subtract, ALU.mult).then_inc(v_step, 1)
            dve.wait_ge(sq_done, 1)
            dve.tensor_reduce(ss[:], sq[:].rearrange("p b (h d) -> p (b h) d", d=HD0), AX.X,
                              ALU.add).then_inc(v_step, 1)
            dve.wait_ge(v_step, 14)
            dve.tensor_scalar(ss[:], ss[:], 1.0 / HD0, RMS_EPS ** 2, ALU.mult, ALU.max).then_inc(v_step, 1)
            dve.wait_ge(p_step, 4)
            dve.wait_ge(sq_done, 2)
            dve.tensor_tensor(kn[:].rearrange("p (b h) d -> p b h d", b=B),
                              kv[:, :, 0:D].rearrange("p b (h d) -> p b h d", d=HD0),
                              rn[:].rearrange("p (b h o) -> p b h o", b=B, o=1).to_broadcast([M, B, H0, HD0]),
                              ALU.mult).then_inc(v_step, 1)
            dve.wait_ge(ld_g, 16 * 7)
            dve.scalar_tensor_tensor(g.gain[:], gq[:], SCALE0, gk[:], ALU.mult, ALU.mult).then_inc(v_step, 1)
            dve.wait_ge(v_step, 17)
            dve.tensor_reduce(gabs[:], g.gain[:], AX.X, ALU.max, apply_absolute_value=True).then_inc(v_step, 1)
            dve.wait_ge(v_step, 18)
            dve.tensor_scalar(g.shift[:, B:B + 1], gabs[:], -float(HD0), None, ALU.mult).then_inc(v_step, 1)
            dve.tensor_scalar(g.shift[0:M, 0:B], mask[:], 1.0, -MASKED, ALU.subtract, ALU.mult).then_inc(v_step, 1)
            dve.wait_ge(v_step, 20)
            dve.tensor_scalar(g.shift[0:M, 0:B], g.shift[0:M, 0:B], g.shift[0:M, B:B + 1], None,
                              ALU.add).then_inc(v_step, 1)
            dve.wait_ge(hi_done, 1)
            dve.tensor_tensor(khl[:, :, 1, :], kn[:], khl[:, :, 0, :], ALU.subtract).then_inc(v_step, 1)
            dve.wait_ge(v_step, 22)

        @block.tensor
        def _(pe):
            pe.wait_ge(ld_ctx, 16)
            pe.wait_ge(g.consts, 4)

            def turn(src, k0):
                for b in range(B):
                    pe.transpose(tr[:, k0, b * M:(b + 1) * M], src[:, b, 0:P], g.ident[0:M, 0:M])
                    last = pe.transpose(tr[0:DC - P, k0 + 1, b * M:(b + 1) * M], src[:, b, P:DC],
                                        g.ident[0:M, 0:M])
                last.then_inc(t_done, 1)

            turn(ctx, 0)
            pe.wait_ge(v_step, 13)
            turn(zc, 2)
            pe.wait_ge(ev, 4)
            pe.wait_ge(ld_w, 32)
            for b in range(B):
                pe.matmul(kv[:, b, :], lnT[:, 0, b, :], wkv[:, 0, :], start=True, stop=False)
                last = pe.matmul(kv[:, b, :], lnT[0:DC - P, 1, b, :], wkv[0:DC - P, 1, :], start=False, stop=True)
            last.then_inc(kv_done, 1)
            pe.wait_ge(hi_done, 1)
            pe.wait_ge(v_step, 22)
            t16 = tr[:].bitcast(F16)
            for n in range(2):
                for h in range(B * H0):
                    last = pe.transpose(t16[:, 2 * n + h // 8, (h % 8) * MP:(h % 8) * MP + M],
                                        khl[:, h, n:n + 2, :].rearrange("p o d -> p (o d)"), g.ident16[0:M, 0:M])
            last.then_inc(kt_done, 1)


def token_stats(nc, g, phase, eps_twice):
    with ExitStack() as st:
        m = Mem(nc, st)
        stats = m.sb(phase + "_stats", [P, T, 6])
        tmp = m.sb(phase + "_tmp", [P, 4, T])
        ve = m.sb(phase + "_ve", [P, T])
        v_step, p_step = m.sem(phase + "_v_step"), m.sem(phase + "_p_step")
        block = st.enter_context(nc.Block())

        @block.vector
        def _(dve):
            dve.wait_ge(g.x_in, 16 * B)
            with dve.Fori(0, T) as t:
                dve.bn_stats(stats[:, bass.ds(t, 1), :], g.x[:, bass.ds(t, 1), :]).then_inc(v_step, 1)
            dve.wait_ge(v_step, T)
            dve.tensor_tensor(tmp[:, 0, :], stats[:, :, 1], stats[:, :, 4], ALU.add).then_inc(v_step, 1)
            dve.tensor_tensor(tmp[:, 1, :], stats[:, :, 1], stats[:, :, 4], ALU.subtract).then_inc(v_step, 1)
            dve.tensor_tensor(tmp[:, 2, :], stats[:, :, 2], stats[:, :, 5], ALU.add).then_inc(v_step, 1)
            dve.wait_ge(v_step, T + 3)
            dve.tensor_scalar(g.mean[:], tmp[:, 0, :], 0.5, None, ALU.mult).then_inc(v_step, 1)
            dve.tensor_tensor(tmp[:, 3, :], tmp[:, 1, :], tmp[:, 1, :], ALU.mult).then_inc(v_step, 1)
            dve.wait_ge(v_step, T + 5)
            dve.scalar_tensor_tensor(tmp[:, 0, :], tmp[:, 3, :], D / 4, tmp[:, 2, :], ALU.mult, ALU.add).then_inc(v_step, 1)
            dve.wait_ge(v_step, T + 6)
            grow, eps = (1.0 + LN_EPS, LN_EPS ** 2) if eps_twice else (1.0, LN_EPS)
            dve.tensor_scalar(ve[:], tmp[:, 0, :], grow / D, eps, ALU.mult, ALU.add).then_inc(v_step, 1)

        @block.gpsimd
        def _(pool):
            pool.wait_ge(v_step, T + 7)
            pool.tensor_tensor(g.rstd[:], ve[:], g.neghalf[:, 0:T], ALU.pow).then_inc(p_step, 1)
            pool.wait_ge(p_step, 1)


def attention0(nc, g, a):
    HALF = S // 2
    KT = TB + 1
    UNITS = 4
    STEPS = UNITS * KT
    with ExitStack() as st:
        m = Mem(nc, st)
        z = m.sb("z0", [P, 2, D])
        lnT = m.sb("lnT0", [P, 2, 2, P])
        w = m.sb("wqkv", [P, 2, 3 * D])
        gl = m.sb("gl", [P, 2])
        bl = m.sb("bl", [P, 2])
        bo = m.sb("bo_row", [P, D])
        sq = m.sb("sq0", [P, 2, 2 * D])
        ss = m.sb("ss0", [P, 2, 2 * H0])
        rn = m.sb("rn0", [P, 2, 2 * H0])
        qk = m.sb("qk0", [P, 2, 2 * H0, HD0])
        hl = m.sb("hl0", [P, 2, 2 * H0, 3, HD0], F16)
        qT = m.sb("qT", [P, H0, S], F16)
        kT = m.sb("kT", [P, 2, H0, S], F16)
        v = m.sb("v0", [P, KT, D])
        pr = m.sb("probs", [P, 4, 2, HALF])
        acc = m.sb("acc", [P, 2, 2, HALF])
        rden = m.sb("rden", [P, HALF])
        oT = m.sb("oT0", [P, 2, HALF])
        wo = m.sb("wo0", [P, 2, D])
        cshift = m.sb("cshift", [M, 1])
        lo = m.ps("lower_banks", [P, 4, 512])
        mid = m.ps("middle_banks", [P, 2, 512])
        hi = m.ps("upper_banks", [P, 2, 512])
        zT = [lo[:, i, 0:2 * P].rearrange("p (k t) -> p k t", k=2) for i in range(2)]
        pqk = [lo[:, 2 + i, :] for i in range(2)]
        pv = [mid[:, i, 0:D] for i in range(2)]
        t3 = hi[:].bitcast(F16).rearrange("p a (h t) -> p a h t", t=P)
        sc = lo[:].rearrange("p (s j) q -> p s j q", s=2)
        po = [mid[:, i, :] for i in range(2)]
        pden = hi[:, 0, :]
        py = hi[:, 1, :].rearrange("p (c d) -> p c d", c=2)

        ld = m.sem("l_ld")
        z_done, t1_done, e1_done, mm_done = m.sem("l_z"), m.sem("l_t1"), m.sem("l_e1"), m.sem("l_mm")
        sq_done, v_ev, ss_done, rn_done, qk_done = m.sem("l_sq"), m.sem("l_v"), m.sem("l_ss"), m.sem("l_rn"), m.sem("l_qk")
        hi_done, lo_done, t3_done, e3_act, e3_dve = m.sem("l_hi"), m.sem("l_lo"), m.sem("l_t3"), m.sem("l_e3a"), m.sem("l_e3v")
        n_done, bo_done, vc_done = m.sem("l_n"), m.sem("l_bo"), m.sem("l_vc")
        s_done, e_done, pv_done = m.sem("a_s"), m.sem("a_e"), m.sem("a_pv")
        acc0, acc1, den_done, r_done = m.sem("a_acc0"), m.sem("a_acc1"), m.sem("a_den"), m.sem("a_r")
        o_done, y_done, x_done = m.sem("a_o"), m.sem("a_y"), m.sem("a_x")
        block = st.enter_context(nc.Block())

        @block.sync
        def _(sp):
            for k in range(2):
                sp.dma_start(w[:, k, :], a["WqkvT"][k * P:(k + 1) * P, :]).then_inc(ld, 16)
            sp.dma_start(gl[:], a["ln_l_g"].rearrange("(k p) -> p k", p=P), allow_slow_non_contiguous=True).then_inc(ld, 16)
            sp.dma_start(bl[:], a["ln_l_b"].rearrange("(k p) -> p k", p=P), allow_slow_non_contiguous=True).then_inc(ld, 16)
            sp.dma_start(bo[:], a["bo"].partition_broadcast(P)).then_inc(ld, 16)
            sp.dma_start(wo[:], a["WoT"].rearrange("(k p) n -> p k n", p=P)).then_inc(ld, 16)
        LOADS = 6 * 16

        def rows(k):
            return P if k < TB else M

        @block.tensor
        def _(pe):
            pe.wait_ge(ld, LOADS)

            def project(t, i, second):
                pe.wait_ge(z_done, t + 1)
                if second:
                    pe.wait_ge(e1_done, t - 1)
                for k in range(2):
                    last = pe.transpose(zT[i][:, k, :], z[:, i, k * P:(k + 1) * P], g.ident[:])
                last.then_inc(t1_done, 1)
                if second:
                    pe.wait_ge(qk_done, t - 1)
                    pe.wait_ge(v_ev, t - 1)
                    pe.wait_ge(sq_done, t - 1)
                pe.wait_ge(e1_done, t + 1)
                for k in range(2):
                    pe.matmul(pqk[i], lnT[:, i, k, :], w[:, k, 0:2 * D], start=(k == 0), stop=(k == 1))
                for k in range(2):
                    last = pe.matmul(pv[i], lnT[:, i, k, :], w[:, k, 2 * D:], start=(k == 0), stop=(k == 1))
                last.then_inc(mm_done, 1)

            def turn(t, i, later):
                pe.wait_ge(hi_done, t + 1)
                pe.wait_ge(lo_done, t + 1)
                if later:
                    pe.wait_ge(e3_act, t)
                    pe.wait_ge(e3_dve, t)
                for h in range(2 * H0):
                    pe.transpose(t3[:, 0, h, :], hl[:, i, h, 0:2, :].rearrange("p o d -> p (o d)"), g.ident16[:])
                for h in range(H0):
                    last = pe.transpose(t3[:, 1, h, :], hl[:, i, H0 + h, 1:3, :].rearrange("p o d -> p (o d)"),
                                        g.ident16[:])
                last.then_inc(t3_done, 1)

            def scores(b, n, fresh):
                u, k = divmod(n, KT)
                half, pair = divmod(u, 2)
                if not fresh:
                    pe.wait_ge(e_done, STEPS * b + n - 1)
                for j in range(2):
                    h = 2 * pair + j
                    q = qT[:, h, half * HALF:(half + 1) * HALF]
                    for form in range(2):
                        if k < TB:
                            kk = kT[:, form, h, k * P:(k + 1) * P]
                        else:
                            kk = g.kctx[:, form, bass.ds(b * H0 + h, 1), 0:M]
                            kk = kk.rearrange("p o m -> p (o m)")
                        last = pe.matmul(sc[0:rows(k), n % 2, j, :], kk, q, start=(form == 0), stop=(form == 1))
                last.then_inc(s_done, 1)

            def values(b, n):
                u, k = divmod(n, KT)
                pair = u % 2
                pe.wait_ge(e_done, STEPS * b + n + 1)
                if k == 0 and u >= 2:
                    pe.wait_ge(o_done, UNITS * b + u - 1)
                for j in range(2):
                    h = 2 * pair + j
                    last = pe.matmul(po[u % 2][j * HD0:(j + 1) * HD0, :], v[0:rows(k), k, h * HD0:(h + 1) * HD0],
                                     pr[0:rows(k), n % 4, j, :], start=(k == 0), stop=(k == KT - 1))
                last.then_inc(pv_done, 1)

            def denominators(b, u):
                pe.wait_ge(acc0, TB * (UNITS * b + u + 1))
                pe.wait_ge(acc1, TB * (UNITS * b + u + 1))
                if u > 0:
                    pe.wait_ge(r_done, UNITS * b + u)
                for j in range(2):
                    last = pe.matmul(pden[j * HD0:(j + 1) * HD0, :], g.ones[:, 0:HD0], acc[:, u % 2, j, :],
                                     start=True, stop=True)
                last.then_inc(den_done, 1)

            def output(b, half):
                pe.wait_ge(o_done, UNITS * b + 2 * half + 2)
                for r in range(2):
                    i = 2 * half + r
                    if i > 0:
                        pe.wait_ge(x_done, UNITS * b + i)
                    for c in range(2):
                        tok = (2 * r + c) * P
                        for pair in range(2):
                            last = pe.matmul(py[:, c, :], oT[:, pair, tok:tok + P], wo[:, pair, :],
                                             start=(pair == 0), stop=(pair == 1))
                    last.then_inc(y_done, 1)

            with pe.Fori(0, B) as b:
                first = b * TB
                project(first, 0, False)
                project(first + 1, 1, False)
                turn(first, 0, False)
                with pe.Fori(1, TB // 2) as n:
                    project(first + 2 * n, 0, True)
                    turn(first + 2 * n - 1, 1, True)
                    project(first + 2 * n + 1, 1, True)
                    turn(first + 2 * n, 0, True)
                turn(first + TB - 1, 1, True)
                pe.wait_ge(e3_act, first + TB)
                pe.wait_ge(e3_dve, first + TB)
                pe.wait_ge(vc_done, 2 * b + 2)
                for n in range(STEPS):
                    if n == 0:
                        scores(b, 0, True)
                    if n < STEPS - 1:
                        scores(b, n + 1, n == 0)
                    values(b, n)
                    u, k = divmod(n, KT)
                    if u > 0 and k == 1:
                        denominators(b, u - 1)
                    if u == 2 and k == 6:
                        output(b, 0)
                denominators(b, UNITS - 1)
                output(b, 1)
                pe.wait_ge(x_done, UNITS * b + UNITS)

        @block.scalar
        def _(act):
            act.wait_ge(ld, LOADS)

            def first(t, i, second):
                act.wait_ge(t1_done, t + 1)
                if second:
                    act.wait_ge(mm_done, t - 1)
                for k in range(2):
                    last = act.activation(lnT[:, i, k, :], zT[i][:, k, :], ACT.Identity, bias=bl[:, k:k + 1],
                                          scale=gl[:, k:k + 1])
                last.then_inc(e1_done, 1)

            def norm(t0, l, i, second):
                t = t0 + l
                act.wait_ge(mm_done, t + 1)
                if second:
                    act.wait_ge(ss_done, 2 * t - 2)
                act.activation(sq[:, i, :], pqk[i], ACT.Square).then_inc(sq_done, 1)
                act.copy(v[:, bass.ds(l, 1), :], pv[i].rearrange("p (o d) -> p o d", o=1)).then_inc(v_ev, 1)

            def high(t, i, second):
                act.wait_ge(n_done, t + 1)
                if second:
                    act.wait_ge(t3_done, t - 1)
                act.copy(hl[:, i, :, 0:3:2, :],
                         qk[:, i].rearrange("p (h o) d -> p h o d", o=1).to_broadcast([P, 2 * H0, 2, HD0])).then_inc(hi_done, 1)

            def out(t0, l):
                t = t0 + l
                act.wait_ge(t3_done, t + 1)
                act.copy(kT[:, 1, :, bass.ds(l * P, P)], t3[:, 1, 0:H0, :]).then_inc(e3_act, 1)

            with act.Fori(0, B) as b:
                t0 = b * TB
                first(t0, 0, False)
                norm(t0, 0, 0, False)
                high(t0, 0, False)
                first(t0 + 1, 1, False)
                norm(t0, 1, 1, False)
                out(t0, 0)
                high(t0 + 1, 1, False)
                with act.Fori(1, TB // 2) as n:
                    for i in range(2):
                        first(t0 + 2 * n + i, i, True)
                        norm(t0, 2 * n + i, i, True)
                        out(t0, 2 * n + i - 1)
                        high(t0 + 2 * n + i, i, True)
                out(t0, TB - 1)
                for n in range(STEPS):
                    k = n % KT
                    act.wait_ge(s_done, STEPS * b + n + 1)
                    if n >= 4:
                        u4, k4 = divmod(n - 4, KT)
                        act.wait_ge(pv_done, STEPS * b + n - 3)
                        act.wait_ge(acc0, TB * (UNITS * b + u4) + max(k4, 1))
                        act.wait_ge(acc1, TB * (UNITS * b + u4) + max(k4, 1))
                    r = rows(k)
                    if n == TB:
                        act.wait_ge(vc_done, 2 * b + 2)
                    bias = g.shift[:, B:B + 1] if k < TB else cshift[:]
                    act.activation(pr[0:r, n % 4], sc[0:r, n % 2], ACT.Exp, bias=bias).then_inc(e_done, 1)

        def sum_up(eng, sem, j, b, n):
            u, k = divmod(n, KT)
            if k == 0:
                return
            eng.wait_ge(e_done, STEPS * b + n + 1)
            if k == 1:
                if u >= 2:
                    eng.wait_ge(den_done, UNITS * b + u - 1)
                eng.tensor_tensor(acc[:, u % 2, j, :], pr[:, (n - 1) % 4, j, :], pr[:, n % 4, j, :],
                                  ALU.add).then_inc(sem, 1)
            else:
                eng.wait_ge(sem, TB * (UNITS * b + u) + k - 1)
                r = rows(k)
                eng.tensor_tensor(acc[0:r, u % 2, j, :], acc[0:r, u % 2, j, :], pr[0:r, n % 4, j, :],
                                  ALU.add).then_inc(sem, 1)

        @block.gpsimd
        def _(pool):
            pool.wait_ge(ld, LOADS)

            def root(t, i):
                pool.wait_ge(ss_done, 2 * t + 2)
                pool.tensor_tensor(rn[:, i, :], ss[:, i, :], g.neghalf[:, 0:2 * H0], ALU.pow).then_inc(rn_done, 1)
                pool.wait_ge(z_done, t + 1)
                xt = g.x[:, bass.ds(t, 1), :].rearrange("p o d -> p (o d)")
                pool.tensor_tensor(xt, xt, bo[:], ALU.add).then_inc(bo_done, 1)

            with pool.Fori(0, B) as b:
                pool.wait_ge(mm_done, b * TB + 1)
                pool.tensor_copy(cshift[:], g.shift[0:M, bass.ds(b, 1)]).then_inc(vc_done, 1)
                pool.tensor_copy(v[0:M, TB, :], g.vctx[:, bass.ds(b, 1), :].rearrange("p o d -> p (o d)")).then_inc(vc_done, 1)
                with pool.Fori(0, TB // 2) as n:
                    for i in range(2):
                        root(b * TB + 2 * n + i, i)
                for n in range(STEPS):
                    sum_up(pool, acc1, 1, b, n)

        @block.vector
        def _(dve):
            def center(t, i, second):
                if second:
                    dve.wait_ge(t1_done, t - 1)
                dve.tensor_scalar(z[:, i:i + 1, :], g.x[:, bass.ds(t, 1), :], g.mean[:, bass.ds(t, 1)],
                                  g.rstd[:, bass.ds(t, 1)], ALU.subtract, ALU.mult).then_inc(z_done, 1)

            def norm(t, i, second):
                dve.wait_ge(sq_done, t + 1)
                dve.tensor_reduce(ss[:, i, :], sq[:, i, :].rearrange("p (h d) -> p h d", d=HD0), AX.X,
                                  ALU.add).then_inc(ss_done, 1)
                dve.wait_ge(ss_done, 2 * t + 1)
                dve.tensor_scalar(ss[:, i, :], ss[:, i, :], 1.0 / HD0, RMS_EPS ** 2, ALU.mult, ALU.max).then_inc(ss_done, 1)
                dve.wait_ge(rn_done, t + 1)
                if second:
                    dve.wait_ge(hi_done, t - 1)
                dve.tensor_tensor(qk[:, i], pqk[i].rearrange("p (h d) -> p h d", d=HD0),
                                  rn[:, i, :].rearrange("p (h o) -> p h o", o=1).to_broadcast([P, 2 * H0, HD0]),
                                  ALU.mult).then_inc(qk_done, 1)
                dve.wait_ge(qk_done, t + 1)
                dve.tensor_tensor(qk[:, i, 0:H0, :], qk[:, i, 0:H0, :],
                                  g.gain[:].rearrange("p (o d) -> p o d", o=1).to_broadcast([P, H0, HD0]),
                                  ALU.mult).then_inc(n_done, 1)
                dve.wait_ge(hi_done, t + 1)
                dve.tensor_tensor(hl[:, i, :, 1, :], qk[:, i], hl[:, i, :, 0, :], ALU.subtract).then_inc(lo_done, 1)

            def out(t0, l):
                t = t0 + l
                dve.wait_ge(t3_done, t + 1)
                dve.tensor_copy(qT[:, :, bass.ds(l * P, P)], t3[:, 0, 0:H0, :])
                dve.tensor_copy(kT[:, 0, :, bass.ds(l * P, P)], t3[:, 0, H0:, :]).then_inc(e3_dve, 1)

            def normalise(b, u):
                half, pair = divmod(u, 2)
                dve.wait_ge(den_done, UNITS * b + u + 1)
                dve.reciprocal(rden[:], pden).then_inc(r_done, 1)
                dve.wait_ge(r_done, UNITS * b + u + 1)
                dve.wait_ge(pv_done, STEPS * b + KT * (u + 1))
                dve.tensor_tensor(oT[:, pair, :], po[u % 2], rden[:], ALU.mult).then_inc(o_done, 1)

            def residual(b, half):
                for r in range(2):
                    i = 2 * half + r
                    dve.wait_ge(y_done, UNITS * b + i + 1)
                    xt = g.x[:, bass.ds(b * TB + 2 * i, 2), :]
                    dve.tensor_tensor(xt, xt, py, ALU.add).then_inc(x_done, 1)

            with dve.Fori(0, B) as b:
                t0 = b * TB
                center(t0, 0, False)
                center(t0 + 1, 1, False)
                norm(t0, 0, False)
                with dve.Fori(1, TB // 2) as n:
                    t = t0 + 2 * n
                    center(t, 0, True)
                    norm(t - 1, 1, True)
                    out(t0, 2 * n - 2)
                    center(t + 1, 1, True)
                    norm(t, 0, True)
                    out(t0, 2 * n - 1)
                norm(t0 + TB - 1, 1, True)
                out(t0, TB - 2)
                out(t0, TB - 1)
                for n in range(STEPS):
                    u, k = divmod(n, KT)
                    sum_up(dve, acc0, 0, b, n)
                    if u > 0 and k == 2:
                        normalise(b, u - 1)
                    if u == 2 and k == 7:
                        residual(b, 0)
                normalise(b, UNITS - 1)
                residual(b, 1)
            dve.wait_ge(x_done, UNITS * B)


def hold(eng, g, sem, value):
    eng.wait_ge(sem, value)
    eng.wait_ge(g.consts, 4)


NT = (2 * B * S + E * (P - 1)) // P + 1
NT += NT % 2
SLOTS = NT * P


def load_experts(nc, g, parts):
    with ExitStack() as st:
        m = Mem(nc, st)
        n_max = max(dst.shape[3] for dst, _ in parts)
        stage = m.sb(g.name("stage"), [P, 4, n_max])
        ld = [m.sem(g.name(f"w_ld{i}")) for i in range(4)]
        hi_done, lo_done = m.sem(g.name("w_hi")), m.sem(g.name("w_lo"))
        block = st.enter_context(nc.Block())
        work = [(dst, src, e) for dst, src in parts for e in range(E)]

        @block.sync
        def _(sp):
            for i, (dst, src, e) in enumerate(work):
                if i >= 4:
                    sp.wait_ge(lo_done, i - 3)
                v = src(e)
                sp.dma_start(stage[:, i % 4, 0:dst.shape[3]].rearrange("p (k n) -> p k n", k=v.shape[1]),
                             v).then_inc(ld[i % 4], 16)

        @block.scalar
        def _(act):
            for i, (dst, src, e) in enumerate(work):
                act.wait_ge(ld[i % 4], 16 * (i // 4 + 1))
                act.mul(dst[:, 0, e, :], stage[:, i % 4, 0:dst.shape[3]], WS).then_inc(hi_done, 1)

        @block.vector
        def _(dve):
            for i, (dst, src, e) in enumerate(work):
                dve.wait_ge(hi_done, i + 1)
                dve.scalar_tensor_tensor(dst[:, 1, e, :], stage[:, i % 4, 0:dst.shape[3]], WS, dst[:, 0, e, :],
                                         ALU.mult, ALU.subtract).then_inc(lo_done, 1)
            dve.wait_ge(lo_done, len(work))


def route(nc, g, a, gate):
    with ExitStack() as st:
        m = Mem(nc, st)
        nm = g.name
        z = m.sb(nm("z"), [P, 2, D])
        zhl = m.sb(nm("zhl"), [P, T, 2 * D], F16)
        zTs = m.sb(nm("zTs"), [P, 2, 2, P])
        gw = m.sb(nm("gw"), [P, 2, E])
        upper = m.sb(nm("upper"), [P, P])
        rev = m.sb(nm("rev"), [P, E])
        tiles = m.sb(nm("tiles"), [1, NT, E])
        lg, l2, oh0, oh1, wk, wk2, ex = (m.sb(nm(f"r{i}"), [P, T, E]) for i in range(7))
        m0, m1, r0, e1, sm, den, pf = (m.sb(nm(f"c{i}"), [P, T]) for i in range(7))
        cnt, cumt, base = (m.sb(nm(f"e{i}"), [P, E]) for i in range(3))
        cnti, cntj = (m.sb(nm(f"ei{i}"), [P, E], I32) for i in range(2))
        tef = m.sb(nm("tef"), [1, NT])
        pz = [m.ps(nm(f"pz{i}"), [P, 4, P]) for i in range(2)]
        plg = m.ps(nm("plg"), [P, 512])
        prk = m.ps(nm("prk"), [P, 512])
        ptot = m.ps(nm("ptot"), [P, 512])

        ld, z_done, hi_done, lo_done = m.sem(nm("ld")), m.sem(nm("z_")), m.sem(nm("hi")), m.sem(nm("lo"))
        t_done, ev, lg_done, p_step = m.sem(nm("t")), m.sem(nm("ev")), m.sem(nm("lg")), m.sem(nm("p"))
        v_step, ex_done, rk_done, sc_done = m.sem(nm("v")), m.sem(nm("ex")), m.sem(nm("rk")), m.sem(nm("sc"))
        block = st.enter_context(nc.Block())

        @block.sync
        def _(sp):
            sp.dma_start(gw[:], gate.rearrange("(k p) e -> p k e", p=P)).then_inc(ld, 16)

        @block.gpsimd
        def _(pool):
            pool.affine_select(out=upper[:], in_=g.ones[:], compare_op=ALU.is_gt, fill=0.0, base=0,
                               pattern=[[1, P]], channel_multiplier=-1).then_inc(p_step, 1)
            pool.iota(rev[:], pattern=[[-1, E]], base=E, channel_multiplier=0,
                      allow_small_or_imprecise_dtypes=True).then_inc(p_step, 1)
            pool.iota(tiles[:], pattern=[[1, NT], [0, E]], base=0, channel_multiplier=0,
                      allow_small_or_imprecise_dtypes=True).then_inc(p_step, 1)
            pool.wait_ge(v_step, ROUTED)
            pool.wait_ge(lo_done, T)
            pool.wait_ge(g.cleared, 16)
            for t in range(T):
                for pos in g.pos:
                    pool.indirect_dma_start(g.zs, bass.IndirectOffsetOnAxis(ap=pos[:, t:t + 1], axis=0),
                                            zhl[:, t, :], None).then_inc(sc_done, 16)
            pool.wait_ge(sc_done, 16 * 2 * T)

        @block.tensor
        def _(pe):
            pe.wait_ge(ld, 16)

            def turn(t, i, second):
                pe.wait_ge(z_done, t + 1)
                if second:
                    pe.wait_ge(ev, t - 1)
                for k in range(2):
                    last = pe.transpose(pz[i][:, k, :], z[:, i, k * P:(k + 1) * P], g.ident[:])
                last.then_inc(t_done, 1)

            def logits(t, i):
                pe.wait_ge(ev, t + 1)
                for k in range(2):
                    last = pe.matmul(plg[:, bass.ds(t * E, E)], zTs[:, i, k, :], gw[:, k, :],
                                     start=(k == 0), stop=(k == 1))
                last.then_inc(lg_done, 1)

            turn(0, 0, False)
            turn(1, 1, False)
            logits(0, 0)
            with pe.Fori(1, T // 2) as n:
                turn(2 * n, 0, True)
                logits(2 * n - 1, 1)
                turn(2 * n + 1, 1, True)
                logits(2 * n, 0)
            logits(T - 1, 1)
            pe.wait_ge(p_step, 3)
            pe.wait_ge(v_step, CHOSEN)
            sel = wk[:].rearrange("p t e -> p (t e)")
            pe.matmul(prk[:, 0:T * E], upper[:], sel, start=True, stop=True)
            pe.matmul(ptot[:, 0:T * E], g.ones[:], sel, start=True, stop=True).then_inc(rk_done, 1)

        @block.scalar
        def _(act):
            def high(t, i, second):
                act.wait_ge(z_done, t + 1)
                act.copy(zhl[:, bass.ds(t, 1), 0:D], z[:, i:i + 1, :]).then_inc(hi_done, 1)
                act.wait_ge(t_done, t + 1)
                if second:
                    act.wait_ge(lg_done, t - 1)
                act.copy(zTs[:, i], pz[i][:, 0:2, :]).then_inc(ev, 1)

            high(0, 0, False)
            high(1, 1, False)
            with act.Fori(1, T // 2) as n:
                for i in range(2):
                    high(2 * n + i, i, True)
            act.wait_ge(v_step, SHIFTED)
            act.activation(ex[:], l2[:], ACT.Exp).then_inc(ex_done, 1)
            act.activation(e1[:], sm[:], ACT.Exp).then_inc(ex_done, 1)

        def over_e(x):
            return x.rearrange("p (t o) -> p t o", o=1).to_broadcast([P, T, E])

        def over_t(x, n=T, p=P):
            return x.rearrange("p (o e) -> p o e", o=1).to_broadcast([p, n, E])

        @block.vector
        def _(dve):
            def center(t, i, second):
                if second:
                    dve.wait_ge(t_done, t - 1)
                    dve.wait_ge(hi_done, t - 1)
                    dve.wait_ge(lo_done, t - 1)
                dve.tensor_scalar(z[:, i:i + 1, :], g.x[:, bass.ds(t, 1), :], g.mean[:, bass.ds(t, 1)],
                                  g.rstd[:, bass.ds(t, 1)], ALU.subtract, ALU.mult).then_inc(z_done, 1)

            def low(t, i):
                dve.wait_ge(hi_done, t + 1)
                dve.tensor_tensor(zhl[:, bass.ds(t, 1), D:], z[:, i:i + 1, :], zhl[:, bass.ds(t, 1), 0:D],
                                  ALU.subtract).then_inc(lo_done, 1)

            center(0, 0, False)
            center(1, 1, False)
            low(0, 0)
            with dve.Fori(1, T // 2) as n:
                center(2 * n, 0, True)
                low(2 * n - 1, 1)
                center(2 * n + 1, 1, True)
                low(2 * n, 0)
            low(T - 1, 1)

            n = [0]

            def step(ins):
                n[0] += 1
                ins.then_inc(v_step, 1)
                dve.wait_ge(v_step, n[0])

            dve.wait_ge(lg_done, T)
            dve.wait_ge(p_step, 3)
            step(dve.tensor_copy(lg[:].rearrange("p t e -> p (t e)"), plg[:, 0:T * E]))
            for src, top, oh in ((lg, m0, oh0), (l2, m1, oh1)):
                step(dve.tensor_reduce(top[:], src[:], AX.X, ALU.max))
                step(dve.tensor_tensor(wk[:], src[:], over_e(top[:]), ALU.is_equal))
                step(dve.tensor_tensor(wk2[:], wk[:], over_t(rev[:]), ALU.mult))
                step(dve.tensor_reduce(r0[:], wk2[:], AX.X, ALU.max))
                step(dve.tensor_tensor(oh[:], over_t(rev[:]), over_e(r0[:]), ALU.is_equal))
                if src is lg:
                    step(dve.scalar_tensor_tensor(l2[:].rearrange("p t e -> p (t e)"), oh0[:].rearrange("p t e -> p (t e)"),
                                                  MASKED, lg[:].rearrange("p t e -> p (t e)"), ALU.mult, ALU.add))
            step(dve.tensor_tensor(wk[:], oh0[:], oh1[:], ALU.add))
            assert n[0] == CHOSEN
            step(dve.tensor_tensor(l2[:], lg[:], over_e(m0[:]), ALU.subtract))
            step(dve.tensor_tensor(sm[:], m1[:], m0[:], ALU.subtract))
            assert n[0] == SHIFTED
            dve.wait_ge(ex_done, 2)
            step(dve.tensor_reduce(den[:], ex[:], AX.X, ALU.add))
            step(dve.tensor_scalar(den[:], den[:], 1e-9, 1.0, ALU.mult, ALU.add))
            step(dve.tensor_tensor(den[:], den[:], e1[:], ALU.add))
            step(dve.reciprocal(g.wt[:, 0, :], den[:]))
            step(dve.tensor_tensor(g.wt[:, 1, :], g.wt[:, 0, :], e1[:], ALU.mult))
            dve.wait_ge(rk_done, 1)
            tot = ptot[:, 0:T * E].rearrange("p (t e) -> p t e", e=E)
            step(dve.tensor_copy(ex[:], tot))
            step(dve.tensor_scalar(wk2[:], ex[:], 0.0, 1.0, ALU.mult, ALU.add))
            for e in range(E):
                last = dve.tensor_tensor_scan(l2[:, :, e], wk2[:, :, e], ex[:, :, e], 0.0, ALU.mult, ALU.add)
                n[0] += 1
                last.then_inc(v_step, 1)
            dve.wait_ge(v_step, n[0])
            step(dve.tensor_scalar(cnti[:], l2[:, T - 1, :], float(P - 1), None, ALU.add))
            step(dve.tensor_scalar(cntj[:], cnti[:], P.bit_length() - 1, None, ALU.logical_shift_right))
            step(dve.tensor_copy(cnt[:], cntj[:]))
            step(dve.tensor_tensor_scan(cumt[:], wk2[:, 0, :], cnt[:], 0.0, ALU.mult, ALU.add))
            step(dve.tensor_tensor(base[:], cumt[:], cnt[:], ALU.subtract))
            step(dve.tensor_scalar(base[:], base[:], float(P), None, ALU.mult))
            step(dve.tensor_tensor(l2[:], l2[:], ex[:], ALU.subtract))
            step(dve.tensor_tensor(l2[:], l2[:], prk[:, 0:T * E].rearrange("p (t e) -> p t e", e=E), ALU.add))
            step(dve.tensor_tensor(l2[:], l2[:], over_t(base[:]), ALU.add))
            for oh, pos in zip((oh0, oh1), g.pos):
                step(dve.tensor_tensor(wk2[:], oh[:], l2[:], ALU.mult))
                step(dve.tensor_reduce(pf[:], wk2[:], AX.X, ALU.add))
                step(dve.tensor_copy(pos[:], pf[:]))
            step(dve.tensor_tensor(tiles[:], tiles[:], over_t(cumt[0:1, :], NT, 1), ALU.is_ge))
            step(dve.tensor_reduce(tef[:], tiles[:], AX.X, ALU.add))
            step(dve.tensor_scalar(tef[:], tef[:], float(E - 1), None, ALU.min))
            step(dve.tensor_copy(g.expert[:], tef[:]))
            assert n[0] == ROUTED, n[0]


CHOSEN = 13
SHIFTED = 15
ROUTED = 49


def experts(nc, g, a, layer):
    F = F0 if layer == 0 else F1
    NF = F // P
    NU = 8
    with ExitStack() as st:
        m = Mem(nc, st)
        nm = g.name
        zt = m.sb(nm("zt"), [P, 2, 2 * D], F16)
        zTs = m.sb(nm("zTt"), [P, 2, 4, P], F16)
        h32 = m.sb(nm("h32"), [P, 2, NF, P])
        gt = m.sb(nm("g32"), [P, 2, NF, P]) if layer else None
        hh = m.sb(nm("hh"), [P, 2, NF, P], F16)
        hl = m.sb(nm("hl"), [P, 2, NF, P], F16)
        ysb = m.sb(nm("ysb"), [P, 2, D])
        if layer == 0:
            b1 = m.sb(nm("b1"), [P, E, NF])
            b2 = m.sb(nm("b2"), [P, E, D])
        pz = [m.ps(nm(f"pzt{i}"), [P, 8, P], F16) for i in range(2)]
        ph = m.ps(nm("ph"), [P, 2, NU, P])
        py = [m.ps(nm(f"pyt{i}"), [P, 512]) for i in range(2)]

        ld = [m.sem(nm(f"zld{i}")) for i in range(2)]
        sto = [m.sem(nm(f"yst{i}")) for i in range(2)]
        bld, t_done, zev = m.sem(nm("bld")), m.sem(nm("tt")), m.sem(nm("zev"))
        up_done, act_done, g_done = m.sem(nm("up")), m.sem(nm("act")), m.sem(nm("gd"))
        hi_done, lo_done, dn_done, yev = m.sem(nm("hid")), m.sem(nm("lod")), m.sem(nm("dn")), m.sem(nm("yev"))
        block = st.enter_context(nc.Block())
        up_w, down_w = g.up_w, g.down_w

        def steps(eng, body):
            body(0, 0, 0)
            body(1, 1, 1)
            with eng.Fori(1, NT // 2) as n:
                body(2 * n, 0, 2)
                body(2 * n + 1, 1, 2)

        @block.sync
        def _(sp):
            if layer == 0:
                sp.dma_start(b1[:], a["b1"].rearrange("e (f p) -> p e f", p=P), allow_slow_non_contiguous=True
                             ).then_inc(bld, 16)
                sp.dma_start(b2[:], a["b2"].partition_broadcast(P)).then_inc(bld, 16)

            def load(i, s, early):
                if not early:
                    sp.wait_ge(t_done, i - 1)
                sp.dma_start(zt[:, s, :], g.zs[bass.ds(i * P, P), :]).then_inc(ld[s], 16)

            for i in range(4):
                load(i, i % 2, i < 2)
            with sp.Fori(2, NT // 2) as n:
                for s in range(2):
                    load(2 * n + s, s, False)
                    sp.wait_ge(yev, 2 * n + s - 3)
                    sp.dma_start(g.ys[bass.ds((2 * n + s - 4) * P, P), :], ysb[:, s, :]).then_inc(sto[s], 16)
            for i in range(NT - 4, NT):
                sp.wait_ge(yev, i + 1)
                sp.dma_start(g.ys[i * P:(i + 1) * P, :], ysb[:, i % 2, :]).then_inc(sto[i % 2], 16)
            for i in range(2):
                sp.wait_ge(sto[i], 16 * (NT // 2))

        @block.tensor
        def _(pe):
            def turn(i, s, half, early):
                pe.wait_ge(ld[s], 16 * half + 16)
                if not early:
                    pe.wait_ge(zev, i - 1)
                for k in range(4):
                    last = pe.transpose(pz[s][:, k, :], zt[:, s, k * P:(k + 1) * P], g.ident16[:])
                last.then_inc(t_done, 1)

            def up(i, s, early):
                e = pe.value_load(g.expert[0:1, bass.ds(i, 1)], min_val=0, max_val=E - 1)
                if not early:
                    pe.wait_ge(act_done, i - 1)
                    if layer:
                        pe.wait_ge(g_done, i - 1)
                hold(pe, g, zev, i + 1)
                for f in range(NU):
                    n = 0
                    for k in range(2):
                        for wp, zp in ((0, 0), (0, 1), (1, 0)):
                            last = pe.matmul(ph[:, s, f, :], up_w(wp, e, k, f), zTs[:, s, 2 * zp + k, :],
                                             start=(n == 0), stop=(n == 5))
                            n += 1
                last.then_inc(up_done, 1)

            def down(i, s, early):
                e = pe.value_load(g.expert[0:1, bass.ds(i, 1)], min_val=0, max_val=E - 1)
                if not early:
                    pe.wait_ge(yev, i - 1)
                pe.wait_ge(hi_done, i + 1)
                hold(pe, g, lo_done, i + 1)
                n = 0
                for f in range(NF):
                    for wp, hp in ((0, hh), (1, hh), (0, hl)):
                        last = pe.matmul(py[s][:, 0:D], hp[:, s, f, :], down_w(wp, e, f),
                                         start=(n == 0), stop=(n == 3 * NF - 1))
                        n += 1
                last.then_inc(dn_done, 1)

            if layer == 0:
                pe.wait_ge(bld, 32)
            turn(0, 0, 0, True)
            turn(1, 1, 0, True)
            up(0, 0, True)
            up(1, 1, True)
            turn(2, 0, 1, False)
            down(0, 0, True)
            up(2, 0, False)
            turn(3, 1, 1, False)
            down(1, 1, True)
            with pe.Fori(1, NT // 2 - 1) as n:
                for s in range(2):
                    i = 2 * n + s
                    up(i + 1, 1 - s, False)
                    turn(i + 2, s, n + 1, False)
                    down(i, s, False)
            up(NT - 1, 1, False)
            down(NT - 2, 0, False)
            down(NT - 1, 1, False)

        @block.scalar
        def _(act):
            if layer == 0:
                act.wait_ge(bld, 32)

                def body(i, s, early):
                    if early == 2:
                        act.wait_ge(lo_done, i - 1)
                        act.wait_ge(dn_done, i - 1)
                    e = act.value_load(g.expert[0:1, bass.ds(i, 1)], min_val=0, max_val=E - 1)
                    hold(act, g, up_done, i + 1)
                    for f in range(NF):
                        last = act.activation(h32[:, s, f, :], ph[:, s, f, :], ACT.Relu,
                                              bias=b1[:, bass.ds(e, 1), f], scale=1.0 / WS)
                    last.then_inc(act_done, 1)
                    act.wait_ge(act_done, i + 1)
                    act.copy(hh[:, s], h32[:, s]).then_inc(hi_done, 1)
            else:
                def body(i, s, early):
                    if early == 2:
                        act.wait_ge(g_done, i - 1)
                    act.wait_ge(up_done, i + 1)
                    act.activation(h32[:, s], ph[:, s, 0:NF, :], ACT.Silu, scale=1.0 / WS).then_inc(act_done, 1)
                    if early == 2:
                        act.wait_ge(dn_done, i - 1)
                    act.wait_ge(g_done, i + 1)
                    act.copy(hh[:, s], gt[:, s]).then_inc(hi_done, 1)
            steps(act, body)

        @block.vector
        def _(dve):
            if layer == 0:
                dve.wait_ge(bld, 32)

            def evacuate(i, s, early):
                dve.wait_ge(t_done, i + 1)
                if not early:
                    dve.wait_ge(up_done, i - 1)
                dve.tensor_copy(zTs[:, s], pz[s][:, 0:4, :]).then_inc(zev, 1)

            def hidden(i, s, early):
                if layer:
                    dve.wait_ge(act_done, i + 1)
                    if not early:
                        dve.wait_ge(lo_done, i - 1)
                    dve.scalar_tensor_tensor(gt[:, s].rearrange("p f t -> p (f t)"),
                                             ph[:, s, NF:, :].rearrange("p f t -> p (f t)"), 1.0 / WS,
                                             h32[:, s].rearrange("p f t -> p (f t)"), ALU.mult, ALU.mult
                                             ).then_inc(g_done, 1)
                if not early:
                    dve.wait_ge(dn_done, i - 1)
                dve.wait_ge(hi_done, i + 1)
                dve.tensor_tensor(hl[:, s], gt[:, s] if layer else h32[:, s], hh[:, s], ALU.subtract
                                  ).then_inc(lo_done, 1)

            def result(i, s, half, early):
                dve.wait_ge(dn_done, i + 1)
                if not early:
                    dve.wait_ge(sto[s], 16 * half)
                if layer == 0:
                    e = dve.value_load(g.expert[0:1, bass.ds(i, 1)], min_val=0, max_val=E - 1)
                    dve.scalar_tensor_tensor(ysb[:, s:s + 1, :], py[s][:, 0:D].rearrange("p (o d) -> p o d", o=1),
                                             1.0 / WS, b2[:, bass.ds(e, 1), :], ALU.mult, ALU.add).then_inc(yev, 1)
                else:
                    dve.tensor_scalar(ysb[:, s, :], py[s][:, 0:D], 1.0 / WS, None, ALU.mult).then_inc(yev, 1)

            evacuate(0, 0, True)
            evacuate(1, 1, True)
            hidden(0, 0, True)
            evacuate(2, 0, False)
            result(0, 0, 0, True)
            hidden(1, 1, True)
            evacuate(3, 1, False)
            result(1, 1, 0, True)
            with dve.Fori(1, NT // 2 - 1) as n:
                for s in range(2):
                    i = 2 * n + s
                    hidden(i, s, False)
                    evacuate(i + 2, s, False)
                    result(i, s, n, False)
            hidden(NT - 2, 0, False)
            result(NT - 2, 0, NT // 2 - 1, False)
            hidden(NT - 1, 1, False)
            result(NT - 1, 1, NT // 2 - 1, False)
            dve.wait_ge(yev, NT)


def combine(nc, g):
    with ExitStack() as st:
        m = Mem(nc, st)
        nm = g.name
        R = 4
        rows = m.sb(nm("rows"), [P, R, 2, D])
        got = [m.sem(nm(f"got{i}")) for i in range(R)]
        added = m.sem(nm("added"))
        block = st.enter_context(nc.Block())

        @block.gpsimd
        def _(pool):
            for t in range(T):
                if t >= R:
                    pool.wait_ge(added, 2 * (t - R) + 2)
                for k in range(2):
                    pool.indirect_dma_start(rows[:, t % R, k, :], None, g.ys,
                                            bass.IndirectOffsetOnAxis(ap=g.pos[k][:, t:t + 1], axis=0)
                                            ).then_inc(got[t % R], 16)

        @block.vector
        def _(dve):
            for t in range(T):
                dve.wait_ge(got[t % R], 32 * (t // R + 1))
                for k in range(2):
                    if k:
                        dve.wait_ge(added, 2 * t + 1)
                    dve.scalar_tensor_tensor(g.x[:, t, :], rows[:, t % R, k, :], g.wt[:, k, t:t + 1], g.x[:, t, :],
                                             ALU.mult, ALU.add).then_inc(added, 1)
            dve.wait_ge(added, 2 * T)


def attention1_context(nc, g, a, at):
    with ExitStack() as st:
        m = Mem(nc, st)
        wk = m.sb("wk1", [P, 2, D])
        wv = m.sb("wv1", [P, 2, D])
        mask8 = m.sb("mask8", [P, B, M], U8)
        mask = m.sb("mask1f", [P, B, M])
        own = m.sb("own", [P, 8])
        own2 = m.sb("own2", [P, 8])
        kT = m.sb("kT1", [P, 2, B, M])
        pk = m.ps("pk1", [P, 2, 512])
        pv = m.ps("pv1", [M, B, 512])
        ld, pool_done, mm_done, v_step, v_ev = m.sem("k_ld"), m.sem("k_pool"), m.sem("k_mm"), m.sem("k_v"), m.sem("k_vev")
        kbd_done, wo_ld = m.sem("k_bd"), m.sem("k_wo")
        block = st.enter_context(nc.Block())

        @block.sync
        def _(sp):
            for w, src in ((wk, a["Wk1"]), (wv, a["Wv1"])):
                sp.dma_start(w[:, 0, :], src[0:P, :]).then_inc(ld, 16)
                sp.dma_start(w[0:DC - P, 1, :], src[P:DC, :]).then_inc(ld, 16)
            sp.dma_start(mask8[:], a["mask1"].partition_broadcast(P)).then_inc(ld, 16)
            sp.dma_start(at.wq[:], a["Wq1"].rearrange("(k p) n -> p k n", p=P)).then_inc(ld, 16)
            sp.wait_ge(pool_done, 2)
            for h in range(H1):
                r = 32 * (h % 4)
                sp.dma_start(at.wo[r:r + HD1, h // 4, :], a["Wo1"][h * HD1:(h + 1) * HD1, :]).then_inc(wo_ld, 16)
            sp.wait_ge(wo_ld, 16 * H1)

        @block.gpsimd
        def _(pool):
            pool.memset(at.v[:], 0.0).then_inc(pool_done, 1)
            pool.memset(at.wo[:], 0.0).then_inc(pool_done, 1)
            pool.affine_select(out=own2[:], in_=g.ones[:, 0:8], compare_op=ALU.is_ge, fill=0.0, base=0,
                               pattern=[[-HD1, 8]], channel_multiplier=1).then_inc(pool_done, 1)
            pool.wait_ge(pool_done, 3)
            pool.affine_select(out=own[:], in_=own2[:], compare_op=ALU.is_ge, fill=0.0, base=HD1 - 1,
                               pattern=[[HD1, 8]], channel_multiplier=-1).then_inc(pool_done, 1)

        @block.tensor
        def _(pe):
            pe.wait_ge(ld, 16 * 6)
            for hg in range(2):
                for k, r in ((0, P), (1, DC - P)):
                    pe.matmul(pk[:, hg, 0:B * M], wk[0:r, k, hg * P:(hg + 1) * P], g.ctxT[0:r, k, :, 0:M],
                              start=(k == 0), stop=(k == 1))
            for b in range(B):
                for k, r in ((0, P), (1, DC - P)):
                    last = pe.matmul(pv[:, b, 0:D], g.ctxT[0:r, k, b, 0:M], wv[0:r, k, :],
                                     start=(k == 0), stop=(k == 1))
            last.then_inc(mm_done, 1)

        @block.scalar
        def _(act):
            act.wait_ge(mm_done, 1)
            act.wait_ge(pool_done, 1)
            for b in range(B):
                act.copy(at.v[:, b, :, 0:HD1], pv[:, b, 0:D].rearrange("p (h d) -> p h d", d=HD1)).then_inc(v_ev, 1)
            act.wait_ge(v_ev, B)

        @block.vector
        def _(dve):
            dve.wait_ge(ld, 16 * 6)
            dve.tensor_copy(mask[:], mask8[:]).then_inc(v_step, 1)
            dve.wait_ge(v_step, 1)
            dve.tensor_scalar(at.bias[:], mask[:], 1.0, -MASKED, ALU.subtract, ALU.mult).then_inc(v_step, 1)
            dve.wait_ge(mm_done, 1)
            for hg in range(2):
                dve.scalar_tensor_tensor(kT[:, hg].rearrange("p b m -> p (b m)"), pk[:, hg, 0:B * M], SCALE1,
                                         mask[:].rearrange("p b m -> p (b m)"), ALU.mult, ALU.mult).then_inc(v_step, 1)
            dve.wait_ge(v_step, 4)
            dve.wait_ge(pool_done, 4)
            for b in range(B):
                for hg in range(2):
                    dve.tensor_tensor(at.k[:, b, hg], kT[:, hg, b:b + 1, :].to_broadcast([P, 8, M]),
                                      own[:].rearrange("p (j o) -> p j o", o=1).to_broadcast([P, 8, M]),
                                      ALU.mult).then_inc(kbd_done, 1)
            dve.wait_ge(kbd_done, 2 * B)


def attention1(nc, g, a, at):
    LAG = 3
    SLOT = 4
    C = 4
    with ExitStack() as st:
        m = Mem(nc, st)
        z = m.sb("z1", [P, 2, D])
        zT = m.sb("zT1", [P, 2, P])
        qT = m.sb("qT1", [P, 2, P])
        s = m.sb("s1", [P, SLOT, H1, M])
        mx = m.sb("mx1", [P, SLOT, H1])
        sm = m.sb("sm1", [P, SLOT, H1])
        rs = m.sb("rs1", [P, SLOT, H1])
        pT = m.sb("pT1", [M, 2, H1, P])
        oT = m.sb("oT1", [P, C, P])
        v = m.sb("vcur", [M, H1, 32])
        psc = m.ps("psc1", [P, C, 512])
        pt = m.ps("pt1", [M, 2, 4, P])
        front = m.ps("front1", [P, 4, P])
        back = m.ps("back1", [P, 512])

        z_done, t_done, zT_ev, q_done, q_ev = (m.sem("b_" + n) for n in ("z", "t", "zTev", "q", "qev"))
        s_done, add_done, max_done, sub_done, e_done = (m.sem("b_" + n) for n in ("s", "add", "max", "sub", "e"))
        sum_done, r_done, n_done = (m.sem("b_" + n) for n in ("sum", "r", "n"))
        pt_done, pt_ev, v_done, o_done, o_ev, y_done, x_done = (
            m.sem("b_" + n) for n in ("pt", "ptev", "v", "o", "oev", "y", "x"))
        block = st.enter_context(nc.Block())

        def steps(eng, body):
            head = LAG + 1
            for c in range(head):
                body(0, 0, c, lambda x: 0 <= x)
            with eng.Fori(0, B - 1) as n:
                for r in range(TB):
                    body(n * TB, n, head + r, lambda x: True)
            last = (B - 1) * TB
            for c in range(head, TB + LAG + 1):
                body(last, B - 1, c, lambda x: x < TB)

        @block.tensor
        def _(pe):
            def body(base, b0, c, live):
                if live(c):
                    t = base + c
                    if c > 0:
                        pe.wait_ge(q_ev, t)
                    pe.wait_ge(z_done, t + 1)
                    for k in range(2):
                        last = pe.transpose(front[:, k, :], z[:, c % 2, k * P:(k + 1) * P], g.ident[:])
                    last.then_inc(t_done, 1)
                d = c - LAG
                if live(d):
                    t = base + d
                    pe.wait_ge(n_done, t + 1)
                    for n in range(4):
                        if d > 0 or n >= 2:
                            pe.wait_ge(pt_ev, 4 * t + n - 1)
                        for h in range(4 * n, 4 * n + 4):
                            last = pe.transpose(pt[:, n % 2, h % 4, :], s[:, d % SLOT, h, :], g.ident[:])
                        last.then_inc(pt_done, 1)
                if live(c):
                    t = base + c
                    pe.wait_ge(zT_ev, t + 1)
                    for hg in range(2):
                        for k in range(2):
                            last = pe.matmul(front[:, 2 + hg, :], at.wq[:, k, hg * P:(hg + 1) * P], zT[:, k, :],
                                             start=(k == 0), stop=(k == 1))
                    last.then_inc(q_done, 1)
                if live(d):
                    t = base + d
                    if d % TB == 0:
                        pe.wait_ge(v_done, b0 + d // TB + 1)
                    if d > 0:
                        pe.wait_ge(x_done, t)
                    pe.wait_ge(pt_ev, 4 * t + 4)
                    for h in range(H1):
                        r = 32 * (h % 4)
                        last = pe.matmul(back[r:r + 32, (h // 4) * P:(h // 4 + 1) * P], v[:, h, :], pT[:, d % 2, h, :],
                                         start=True, stop=True)
                    last.then_inc(o_done, 1)
                if live(c):
                    t = base + c
                    if c > 0:
                        pe.wait_ge(add_done, t)
                    pe.wait_ge(q_ev, t + 1)
                    for n in range(C):
                        last = pe.matmul(psc[:, n, 0:4 * M], qT[:, n // 2, :],
                                         at.k[:, bass.ds(b0 + c // TB, 1), n // 2, 4 * (n % 2):4 * (n % 2) + 4, :]
                                         .rearrange("p o j m -> p (o j m)"), start=True, stop=True)
                    last.then_inc(s_done, 1)
                if live(d):
                    pe.wait_ge(o_ev, base + d + 1)
                    for n in range(C):
                        last = pe.matmul(back[:, 0:D], oT[:, n, :], at.wo[:, n, :], start=(n == 0), stop=(n == C - 1))
                    last.then_inc(y_done, 1)

            steps(pe, body)

        @block.scalar
        def _(act):
            def body(base, b0, c, live):
                if live(c):
                    t = base + c
                    act.wait_ge(t_done, t + 1)
                    act.copy(zT[:], front[:, 0:2, :]).then_inc(zT_ev, 1)
                d = c - LAG
                if live(d):
                    t = base + d
                    for n in range(4):
                        act.wait_ge(pt_done, 4 * t + n + 1)
                        act.copy(pT[:, d % 2, 4 * n:4 * n + 4, :], pt[:, n % 2]).then_inc(pt_ev, 1)
                if live(c):
                    t = base + c
                    act.wait_ge(q_done, t + 1)
                    act.copy(qT[:], front[:, 2:4, :]).then_inc(q_ev, 1)
                if live(c - 1):
                    t = base + c - 1
                    act.wait_ge(sub_done, t + 1)
                    act.activation(s[:, (c - 1) % SLOT], s[:, (c - 1) % SLOT], ACT.Exp).then_inc(e_done, 1)
                if live(d):
                    act.wait_ge(o_done, base + d + 1)
                    act.copy(oT[:].rearrange("p n t -> p (n t)"), back[:]).then_inc(o_ev, 1)

            steps(act, body)

        def per_key(x):
            return x.rearrange("p (h o) -> p h o", o=1).to_broadcast([P, H1, M])

        @block.gpsimd
        def _(pool):
            def body(base, b0, c, live):
                d = c - LAG
                if live(d) and d % TB == 0:
                    b = b0 + d // TB
                    if d > 0:
                        pool.wait_ge(o_done, base + d)
                    pool.tensor_copy(v[:].rearrange("p (o h) d -> p o h d", o=1), at.v[:, bass.ds(b, 1)]
                                     ).then_inc(v_done, 1)
                if live(c - 2):
                    i = (c - 2) % SLOT
                    pool.wait_ge(r_done, base + c - 1)
                    pool.tensor_tensor(s[:, i], s[:, i], per_key(rs[:, i, :]), ALU.mult).then_inc(n_done, 1)
                if live(c - 1):
                    i = (c - 1) % SLOT
                    pool.wait_ge(max_done, base + c)
                    pool.tensor_tensor(s[:, i], s[:, i], per_key(mx[:, i, :]), ALU.subtract).then_inc(sub_done, 1)

            steps(pool, body)

        @block.vector
        def _(dve):
            def center(base, c):
                t = base + c
                if c > 1:
                    dve.wait_ge(t_done, t - 1)
                dve.tensor_scalar(z[:, c % 2:c % 2 + 1, :], g.x[:, bass.ds(t, 1), :], g.mean[:, bass.ds(t, 1)],
                                  g.rstd[:, bass.ds(t, 1)], ALU.subtract, ALU.mult).then_inc(z_done, 1)

            def body(base, b0, c, live):
                if c == 0:
                    center(base, 0)
                if live(c - 2):
                    i, t = (c - 2) % SLOT, base + c - 2
                    dve.wait_ge(e_done, t + 1)
                    dve.tensor_reduce(sm[:, i, :], s[:, i], AX.X, ALU.add).then_inc(sum_done, 1)
                    dve.wait_ge(sum_done, t + 1)
                    dve.reciprocal(rs[:, i, :], sm[:, i, :]).then_inc(r_done, 1)
                if live(c - 1):
                    i, t = (c - 1) % SLOT, base + c - 1
                    if c - 1 >= SLOT:
                        dve.wait_ge(pt_done, 4 * (t - SLOT) + 4)
                    dve.wait_ge(s_done, t + 1)
                    dve.tensor_tensor(s[:, i].rearrange("p (n j) m -> p n j m", n=C),
                                      psc[:, :, 0:4 * M].rearrange("p n (j m) -> p n j m", m=M),
                                      at.bias[:, bass.ds(b0 + (c - 1) // TB, 1), :].rearrange("p (n o) m -> p n o m", n=1)
                                      .to_broadcast([P, C, 4, M]), ALU.add).then_inc(add_done, 1)
                    dve.wait_ge(add_done, t + 1)
                    dve.tensor_reduce(mx[:, i, :], s[:, i], AX.X, ALU.max).then_inc(max_done, 1)
                if live(c + 1):
                    center(base, c + 1)
                d = c - LAG
                if live(d):
                    t = base + d
                    dve.wait_ge(y_done, t + 1)
                    xt = g.x[:, bass.ds(t, 1), :]
                    dve.tensor_tensor(xt, xt, back[:, 0:D].rearrange("p (o d) -> p o d", o=1), ALU.add).then_inc(x_done, 1)

            steps(dve, body)
            dve.wait_ge(x_done, T)


def host_arrays(i):
    import numpy as np

    n = {k: np.asarray(v) for k, v in i.items()}
    c = np.ascontiguousarray
    return {
        "x": n["x"].reshape(B * S, D),
        "ctx": n["ctx_768"],
        "mask0": n["mask_BxS2_bk0"],
        "mask1": n["mask_BxS2_bf1"],
        "ln_x_g": n["L0_xattn_ln_x_g"], "ln_x_b": n["L0_xattn_ln_x_b"],
        "ln_l_g": n["L0_xattn_ln_l_g"], "ln_l_b": n["L0_xattn_ln_l_b"],
        "qn_g": n["L0_xattn_qn_g"], "kn_g": n["L0_xattn_kn_g"],
        "WqkvT": c(np.concatenate([n["L0_xattn_Wq"].T, n["L0_xattn_Wlkv"].T], axis=1)),
        "WkvT": c(n["L0_xattn_Wkv"].T),
        "WoT": c(n["L0_xattn_Wo"].T), "bo": n["L0_xattn_bo"],
        "routerT": c(n["L0_ffn_router_w"].T),
        "w1T": c(n["L0_ffn_w1"].transpose(0, 2, 1)), "b1": n["L0_ffn_b1"],
        "w2T": c(n["L0_ffn_w2"].transpose(0, 2, 1)), "b2": n["L0_ffn_b2"],
        "Wq1": n["L1_xattn_Wq"], "Wk1": n["L1_xattn_Wk"], "Wv1": n["L1_xattn_Wv"], "Wo1": n["L1_xattn_Wo"],
        "gate": n["L1_ffn_gate_w"],
        "u1": n["L1_ffn_w1"], "u2": n["L1_ffn_w2"], "u3": n["L1_ffn_w3"],
    }


def program(nc, a, out, start=0, stages=4):
    g = Names()
    g.phase = "e0_"
    g.name = lambda x: g.phase + x
    g.zs = nc.dram_tensor("sorted_tokens", [SLOTS, 2 * D], F16, kind="Internal").ap()
    g.ys = nc.dram_tensor("sorted_results", [SLOTS, D], F32, kind="Internal").ap()
    with ExitStack() as whole:
        mem = Mem(nc, whole)
        setup(nc, mem, g, a)
        with ExitStack() as st:
            m = Mem(nc, st)
            g.kctx = m.sb("kctx", [P, 2, B * H0, MP], F16)
            g.vctx = m.sb("vctx", [M, B, D])
            attention0_inputs(nc, g, a)
            if start < 1 <= stages:
                token_stats(nc, g, "n0", True)
                attention0(nc, g, a)
        wA = mem.sb("weights_a", [P, 2, E, 2 * F0], F16)
        if start < 2 <= stages:
            token_stats(nc, g, "n1", False)
            route(nc, g, a, a["routerT"])
            with ExitStack() as st:
                wB = Mem(nc, st).sb("weights_b", [P, 2, E, (F0 // P) * D], F16)
                g.up_w = lambda part, e, k, f: wA[:, part, bass.ds(e, 1), k * F0 + f * P:k * F0 + f * P + P].rearrange("p o n -> p (o n)")
                g.down_w = lambda part, e, f: wB[:, part, bass.ds(e, 1), f * D:(f + 1) * D].rearrange("p o n -> p (o n)")
                load_experts(nc, g, [(wA, lambda e: a["w1T"][e].rearrange("(k p) f -> p k f", p=P)),
                                     (wB, lambda e: a["w2T"][e].rearrange("(k p) f -> p k f", p=P))])
                experts(nc, g, a, 0)
            combine(nc, g)
        if start < 3 <= stages:
            with ExitStack() as st:
                m = Mem(nc, st)
                at = Names()
                at.k = m.sb("kbd", [P, B, 2, 8, M])
                at.v = m.sb("vpad", [M, B, H1, 32])
                at.bias = m.sb("bias1", [P, B, M])
                at.wq = m.sb("wq1", [P, 2, D])
                at.wo = m.sb("wo1", [P, 4, D])
                attention1_context(nc, g, a, at)
                token_stats(nc, g, "n2", False)
                attention1(nc, g, a, at)
        if start < 4 <= stages:
            g.phase = "e1_"
            token_stats(nc, g, "n3", False)
            route(nc, g, a, a["gate"])
            with ExitStack() as st:
                w3 = Mem(nc, st).sb("weights_3", [P, 2, E, (F1 // P) * D], F16)
                parts = [wA[:, :, :, i * 2 * F1:(i + 1) * 2 * F1] for i in range(2)]
                g.up_w = lambda part, e, k, f: parts[f // 4][:, part, bass.ds(e, 1), k * F1 + (f % 4) * P:k * F1 + (f % 4) * P + P].rearrange("p o n -> p (o n)")
                g.down_w = lambda part, e, f: w3[:, part, bass.ds(e, 1), f * D:(f + 1) * D].rearrange("p o n -> p (o n)")
                load_experts(nc, g, [(parts[0], lambda e: a["u1"][e].rearrange("(k p) f -> p k f", p=P)),
                                     (parts[1], lambda e: a["u2"][e].rearrange("(k p) f -> p k f", p=P)),
                                     (w3, lambda e: a["u3"][e].rearrange("(k p) f -> p k f", p=P))])
                experts(nc, g, a, 1)
            combine(nc, g)
        finish(nc, g, out)


def finish(nc, g, out):
    with ExitStack() as st:
        m = Mem(nc, st)
        done = m.sem("stored")
        block = st.enter_context(nc.Block())

        @block.sync
        def _(sp):
            sp.dma_start(out.rearrange("(t p) d -> p t d", p=P), g.x[:]).then_inc(done, 16)
            sp.wait_ge(done, 16)


def kernel(**inputs):
    import concourse.bacc as bacc
    from concourse.bass_utils import run_bass_kernel_spmd
    nc = bacc.Bacc("TRN2", target_bir_lowering=False, num_devices=1)
    arrays = {f"in_{name}": array for name, array in host_arrays(inputs).items()}
    views = {name[3:]: nc.dram_tensor(name, array.shape, mybir.dt.from_np(array.dtype), kind="ExternalInput").ap()
             for name, array in arrays.items()}
    out = nc.dram_tensor("out_dram", (B, S, D), F32, kind="ExternalOutput").ap()
    program(nc, views, out.rearrange("b s d -> (b s) d"))
    return run_bass_kernel_spmd(nc, [arrays], core_ids=[0]).results[0]["out_dram"]
```

```python
from contextlib import ExitStack

import concourse.bass as bass
from concourse import mybir

F32 = mybir.dt.float32
F16 = mybir.dt.float16
I32 = mybir.dt.int32
U32 = mybir.dt.uint32
U8 = mybir.dt.uint8
ALU = mybir.AluOpType
ACT = mybir.ActivationFunctionType
AX = mybir.AxisListType

P = 128
B = 4
S = 1024
T = B * S // P
TB = S // P
D = 256
DC = 192
M = 77
MP = 80
LN_EPS = 1e-5
RMS_EPS = 1e-8
MASKED = -1e30

H0, HD0 = 4, 64
SCALE0 = HD0 ** -0.5
H1, HD1 = 16, 16
SCALE1 = HD1 ** -0.5

E = 8
F0, F1 = 1024, 512
WS = 64.0


class Names:
    pass


class Mem:

    def __init__(self, nc, stack):
        self.nc, self.stack = nc, stack

    def sb(self, name, shape, dt=F32):
        return self.stack.enter_context(self.nc.sbuf_tensor(name, shape, dt))

    def ps(self, name, shape, dt=F32):
        return self.stack.enter_context(self.nc.psum_tensor(name, shape, dt))

    def sem(self, name):
        return self.stack.enter_context(self.nc.semaphore(name))


def setup(nc, mem, g, a):
    g.x = mem.sb("x_sb", [P, T, D])
    g.ident = mem.sb("ident", [P, P])
    g.ident16 = mem.sb("ident16", [P, P], F16)
    g.ones = mem.sb("ones", [P, P])
    g.neghalf = mem.sb("neghalf", [P, 64])
    g.ctxT = mem.sb("ctxT", [P, 2, B, MP])
    g.stats = mem.sb("stats", [P, T, 6])
    g.mean = mem.sb("mean", [P, T])
    g.rstd = mem.sb("rstd", [P, T])
    g.gain = mem.sb("gain", [P, HD0])
    g.shift = mem.sb("shift", [P, B + 1])
    g.pos = [mem.sb(f"pos{k}", [P, T], U32) for k in range(2)]
    g.wt = mem.sb("wt", [P, 2, T])
    g.expert = mem.sb("expert", [1, NT], I32)
    g.cleared = mem.sem("cleared")
    g.x_in = mem.sem("x_in")
    g.consts = mem.sem("consts")
    g.stat_steps, g.stat_roots = mem.sem("stat_steps"), mem.sem("stat_roots")
    g.stat_seen = g.stat_runs = 0


def attention0_inputs(nc, g, a):
    with ExitStack() as st:
        m = Mem(nc, st)
        ctx = m.sb("ctx", [M, B, DC])
        zc = m.sb("zc", [M, B, DC])
        stats = m.sb("stats_c", [M, B, 6])
        mv = m.sb("mv_c", [M, B, 2])
        ve = m.sb("ve_c", [M, B])
        rstd = m.sb("rstd_c", [M, B])
        lnT = m.sb("lnT_c", [P, 2, B, M])
        gx = m.sb("gx", [P, 2])
        bx = m.sb("bx", [P, 2])
        wkv = m.sb("wkv", [P, 2, 2 * D])
        sq = m.sb("sq_c", [M, B, D])
        ss = m.sb("ss_c", [M, B * H0])
        rn = m.sb("rn_c", [M, B * H0])
        kn = m.sb("kn_c", [M, B * H0, HD0])
        khl = m.sb("khl_c", [M, B * H0, 3, HD0], F16)
        mask = m.sb("mask_c", [M, B], U8)
        gq = m.sb("gq_row", [P, HD0])
        gk = m.sb("gk_row", [P, HD0])
        gabs = m.sb("gabs", [P, 1])
        kv = m.ps("kv_c", [M, B, 2 * D])
        tr = m.ps("tr_c", [P, 4, 512])

        ld_ctx, ld_w, ld_g = m.sem("ld_ctx"), m.sem("ld_wkv"), m.sem("ld_g")
        v_step, p_step = m.sem("c_v_step"), m.sem("c_p_step")
        t_done, ev, kv_done, sq_done = m.sem("c_t_done"), m.sem("c_ev"), m.sem("c_kv"), m.sem("c_sq")
        x_step = m.sem("c_x")
        hi_done, kt_done, kt_ev = m.sem("c_hi"), m.sem("c_ktd"), m.sem("c_ktev")
        block = st.enter_context(nc.Block())

        @block.sync
        def _(sp):
            sp.dma_start(ctx[:], a["ctx"].rearrange("b m d -> m b d")).then_inc(ld_ctx, 16)
            sp.wait_ge(ld_w, 32)
            for i in range(B):
                sp.dma_start(g.x[:, i * TB:(i + 1) * TB, :],
                             a["x"][i * S:(i + 1) * S, :].rearrange("(t p) d -> p t d", p=P)).then_inc(g.x_in, 16)
            sp.wait_ge(p_step, 1)
            sp.wait_ge(g.x_in, 16 * B)
            sp.dma_start(g.zs.rearrange("(n p) d -> p n d", p=P),
                         g.zeros[:].rearrange("p (o d) -> p o d", o=1).to_broadcast([P, C * NT, 2 * D])).then_inc(g.cleared, 16)

        @block.scalar
        def _(act):
            act.preload_act_table_set("natural_log_exp_and_others")
            act.dma_start(wkv[:, 0, :], a["WkvT"][0:P, :]).then_inc(ld_w, 16)
            act.dma_start(wkv[0:DC - P, 1, :], a["WkvT"][P:DC, :]).then_inc(ld_w, 16)
            for v, dst in ((a["ln_x_g"], gx), (a["ln_x_b"], bx)):
                act.dma_start(dst[:, 0:1], v[0:P].rearrange("(p o) -> p o", o=1)).then_inc(ld_g, 16)
                act.dma_start(dst[0:DC - P, 1:2], v[P:DC].rearrange("(p o) -> p o", o=1)).then_inc(ld_g, 16)
            act.dma_start(mask[:], a["mask0"].rearrange("b m -> m b"), allow_slow_non_contiguous=True).then_inc(ld_g, 16)
            act.dma_start(gq[:], a["qn_g"].partition_broadcast(P)).then_inc(ld_g, 16)
            act.dma_start(gk[:], a["kn_g"].partition_broadcast(P)).then_inc(ld_g, 16)
            act.wait_ge(t_done, 1)
            act.copy(g.ctxT[:, 0, :, 0:M], tr[:, 0, 0:B * M].rearrange("p (b m) -> p b m", b=B)).then_inc(ev, 1)
            act.copy(g.ctxT[0:DC - P, 1, :, 0:M],
                     tr[0:DC - P, 1, 0:B * M].rearrange("p (b m) -> p b m", b=B)).then_inc(ev, 1)
            act.wait_ge(t_done, 2)
            act.wait_ge(ld_g, 16 * 7)
            act.activation(lnT[:, 0], tr[:, 2, 0:B * M].rearrange("p (b m) -> p b m", b=B), ACT.Identity,
                           bias=bx[:, 0:1], scale=gx[:, 0:1]).then_inc(ev, 1)
            act.activation(lnT[0:DC - P, 1], tr[0:DC - P, 3, 0:B * M].rearrange("p (b m) -> p b m", b=B),
                           ACT.Identity, bias=bx[0:DC - P, 1:2], scale=gx[0:DC - P, 1:2]).then_inc(ev, 1)
            act.wait_ge(kv_done, 1)
            act.activation(sq[:], kv[:, :, 0:D], ACT.Square).then_inc(sq_done, 1)
            act.copy(g.vctx[:], kv[:, :, D:2 * D]).then_inc(sq_done, 1)
            act.wait_ge(v_step, 16)
            act.copy(khl[:, :, 0:3:2, :], kn[:].rearrange("p (h o) d -> p h o d", o=1).to_broadcast([M, B * H0, 2, HD0])
                     ).then_inc(hi_done, 1)
            act.wait_ge(kt_done, 1)
            t16 = tr[:].bitcast(F16)
            for n in range(4):
                act.copy(g.kctx[:, n // 2, (n % 2) * 8:(n % 2) * 8 + 8, 0:M],
                         t16[:, n, 0:8 * MP].rearrange("p (h m) -> p h m", h=8)[:, :, 0:M]).then_inc(kt_ev, 1)
            act.wait_ge(kt_ev, 4)

        @block.gpsimd
        def _(pool):
            pool.memset(g.zeros[:], 0.0).then_inc(p_step, 1)
            pool.memset(g.ident[:], 0.0).then_inc(p_step, 1)
            pool.memset(g.ident16[:], 0.0).then_inc(p_step, 1)
            pool.memset(g.ones[:], 1.0).then_inc(g.consts, 1)
            pool.memset(g.neghalf[:], -0.5).then_inc(g.consts, 1)
            pool.wait_ge(p_step, 3)
            for t in (g.ident, g.ident16):
                pool.affine_select(out=t[:], in_=t[:], compare_op=ALU.not_equal, fill=1.0, base=0,
                                   pattern=[[-1, P]], channel_multiplier=1).then_inc(g.consts, 1)
            pool.wait_ge(g.consts, 4)
            pool.wait_ge(v_step, 9)
            pool.tensor_tensor(rstd[:], ve[:], g.neghalf[0:M, 0:B], ALU.pow).then_inc(p_step, 1)
            pool.wait_ge(v_step, 15)
            pool.tensor_tensor(rn[:], ss[:], g.neghalf[0:M, 0:B * H0], ALU.pow).then_inc(p_step, 1)
            pool.wait_ge(p_step, 5)

        @block.vector
        def _(dve):
            def token_rows(t0, t1):
                if t0 == 0:
                    dve.wait_ge(g.x_in, 16 * B)
                for t in range(t0, t1):
                    dve.bn_stats(g.stats[:, t, :], g.x[:, t, :]).then_inc(x_step, 1)

            dve.wait_ge(ld_ctx, 16)
            for b in range(B):
                dve.bn_stats(stats[:, b, :], ctx[:, b, :]).then_inc(v_step, 1)
            dve.wait_ge(v_step, 4)
            for b in range(B):
                dve.bn_aggr(mv[:, b, :], stats[:, b, :]).then_inc(v_step, 1)
            dve.wait_ge(v_step, 8)
            dve.tensor_scalar(ve[:], mv[:, :, 1], LN_EPS, None, ALU.add).then_inc(v_step, 1)
            dve.wait_ge(p_step, 4)
            for b in range(B):
                dve.tensor_scalar(zc[:, b, :], ctx[:, b, :], mv[:, b, 0:1], rstd[:, b:b + 1],
                                  ALU.subtract, ALU.mult).then_inc(v_step, 1)
            token_rows(0, T // 4)
            dve.wait_ge(sq_done, 1)
            dve.tensor_reduce(ss[:], sq[:].rearrange("p b (h d) -> p (b h) d", d=HD0), AX.X,
                              ALU.add).then_inc(v_step, 1)
            dve.wait_ge(v_step, 14)
            dve.tensor_scalar(ss[:], ss[:], 1.0 / HD0, RMS_EPS ** 2, ALU.mult, ALU.max).then_inc(v_step, 1)
            token_rows(T // 4, T // 2)
            dve.wait_ge(p_step, 5)
            dve.wait_ge(sq_done, 2)
            dve.tensor_tensor(kn[:].rearrange("p (b h) d -> p b h d", b=B),
                              kv[:, :, 0:D].rearrange("p b (h d) -> p b h d", d=HD0),
                              rn[:].rearrange("p (b h o) -> p b h o", b=B, o=1).to_broadcast([M, B, H0, HD0]),
                              ALU.mult).then_inc(v_step, 1)
            dve.wait_ge(ld_g, 16 * 7)
            dve.scalar_tensor_tensor(g.gain[:], gq[:], SCALE0, gk[:], ALU.mult, ALU.mult).then_inc(v_step, 1)
            dve.wait_ge(v_step, 17)
            dve.tensor_reduce(gabs[:], g.gain[:], AX.X, ALU.max, apply_absolute_value=True).then_inc(v_step, 1)
            dve.wait_ge(v_step, 18)
            dve.tensor_scalar(g.shift[:, B:B + 1], gabs[:], -float(HD0), None, ALU.mult).then_inc(v_step, 1)
            dve.tensor_scalar(g.shift[0:M, 0:B], mask[:], 1.0, -MASKED, ALU.subtract, ALU.mult).then_inc(v_step, 1)
            dve.wait_ge(v_step, 20)
            dve.tensor_scalar(g.shift[0:M, 0:B], g.shift[0:M, 0:B], g.shift[0:M, B:B + 1], None,
                              ALU.add).then_inc(v_step, 1)
            token_rows(T // 2, T - T // 4)
            dve.wait_ge(hi_done, 1)
            dve.tensor_tensor(khl[:, :, 1, :], kn[:], khl[:, :, 0, :], ALU.subtract).then_inc(v_step, 1)
            token_rows(T - T // 4, T)
            dve.wait_ge(x_step, T)
            dve.wait_ge(v_step, 22)

        @block.tensor
        def _(pe):
            pe.wait_ge(ld_ctx, 16)
            pe.wait_ge(g.consts, 4)

            def turn(src, k0):
                for b in range(B):
                    pe.transpose(tr[:, k0, b * M:(b + 1) * M], src[:, b, 0:P], g.ident[0:M, 0:M])
                    last = pe.transpose(tr[0:DC - P, k0 + 1, b * M:(b + 1) * M], src[:, b, P:DC],
                                        g.ident[0:M, 0:M])
                last.then_inc(t_done, 1)

            turn(ctx, 0)
            pe.wait_ge(v_step, 13)
            turn(zc, 2)
            pe.wait_ge(ev, 4)
            pe.wait_ge(ld_w, 32)
            for b in range(B):
                pe.matmul(kv[:, b, :], lnT[:, 0, b, :], wkv[:, 0, :], start=True, stop=False)
                last = pe.matmul(kv[:, b, :], lnT[0:DC - P, 1, b, :], wkv[0:DC - P, 1, :], start=False, stop=True)
            last.then_inc(kv_done, 1)
            pe.wait_ge(hi_done, 1)
            pe.wait_ge(v_step, 22)
            t16 = tr[:].bitcast(F16)
            for n in range(2):
                for h in range(B * H0):
                    last = pe.transpose(t16[:, 2 * n + h // 8, (h % 8) * MP:(h % 8) * MP + M],
                                        khl[:, h, n:n + 2, :].rearrange("p o d -> p (o d)"), g.ident16[0:M, 0:M])
            last.then_inc(kt_done, 1)


def token_stats(nc, g, phase, first, twice=False):
    with ExitStack() as st:
        m = Mem(nc, st)
        stats = g.stats
        tmp = m.sb(phase + "_tmp", [P, 4, T])
        ve = m.sb(phase + "_ve", [P, T])
        v_step, p_step = g.stat_steps, g.stat_roots
        seen = g.stat_seen + (T if first else 0)
        g.stat_seen = seen + 7
        g.stat_runs += 1
        runs = g.stat_runs
        block = st.enter_context(nc.Block())

        @block.vector
        def _(dve):
            if first:
                dve.wait_ge(g.x_in, 16 * B)
                with dve.Fori(0, T) as t:
                    dve.bn_stats(stats[:, bass.ds(t, 1), :], g.x[:, bass.ds(t, 1), :]).then_inc(v_step, 1)
                dve.wait_ge(v_step, seen)
            dve.tensor_tensor(tmp[:, 0, :], stats[:, :, 1], stats[:, :, 4], ALU.add).then_inc(v_step, 1)
            dve.tensor_tensor(tmp[:, 1, :], stats[:, :, 1], stats[:, :, 4], ALU.subtract).then_inc(v_step, 1)
            dve.tensor_tensor(tmp[:, 2, :], stats[:, :, 2], stats[:, :, 5], ALU.add).then_inc(v_step, 1)
            dve.wait_ge(v_step, seen + 3)
            dve.tensor_scalar(g.mean[:], tmp[:, 0, :], 0.5, None, ALU.mult).then_inc(v_step, 1)
            dve.tensor_tensor(tmp[:, 3, :], tmp[:, 1, :], tmp[:, 1, :], ALU.mult).then_inc(v_step, 1)
            dve.wait_ge(v_step, seen + 5)
            dve.scalar_tensor_tensor(tmp[:, 0, :], tmp[:, 3, :], D / 4, tmp[:, 2, :], ALU.mult, ALU.add).then_inc(v_step, 1)
            dve.wait_ge(v_step, seen + 6)
            grow, eps = (1.0 + LN_EPS, LN_EPS ** 2) if twice else (1.0, LN_EPS)
            dve.tensor_scalar(ve[:], tmp[:, 0, :], grow / D, eps, ALU.mult, ALU.add).then_inc(v_step, 1)

        @block.gpsimd
        def _(pool):
            pool.wait_ge(v_step, seen + 7)
            pool.tensor_tensor(g.rstd[:], ve[:], g.neghalf[:, 0:T], ALU.pow).then_inc(p_step, 1)
            pool.wait_ge(p_step, runs)


def attention0(nc, g, a):
    HALF = S // 2
    KT = TB + 1
    UNITS = 4
    STEPS = UNITS * KT
    with ExitStack() as st:
        m = Mem(nc, st)
        z = m.sb("z0", [P, 2, D])
        lnT = m.sb("lnT0", [P, 2, 2, P])
        w = m.sb("wqkv", [P, 2, 3 * D])
        gl = m.sb("gl", [P, 2])
        bl = m.sb("bl", [P, 2])
        bo = m.sb("bo_row", [P, D])
        sq = m.sb("sq0", [P, 2, 2 * D])
        ss = m.sb("ss0", [P, 2, 2 * H0])
        rn = m.sb("rn0", [P, 2, 2 * H0])
        qk = m.sb("qk0", [P, 2, 2 * H0, HD0])
        hl = m.sb("hl0", [P, 2, 2 * H0, 3, HD0], F16)
        qT = m.sb("qT", [P, H0, S], F16)
        kT = m.sb("kT", [P, 2, H0, S], F16)
        v = m.sb("v0", [P, KT, D])
        pr = m.sb("probs", [P, 4, 2, HALF])
        acc = m.sb("acc", [P, 2, 2, HALF])
        oT = m.sb("oT0", [P, 2, HALF])
        rden = m.sb("rden", [P, HALF])
        wo = m.sb("wo0", [P, 2, D])
        cshift = m.sb("cshift", [M, 1])
        lo = m.ps("lower_banks", [P, 4, 512])
        mid = m.ps("middle_banks", [P, 2, 512])
        hi = m.ps("upper_banks", [P, 2, 512])
        zT = [lo[:, i, 0:2 * P].rearrange("p (k t) -> p k t", k=2) for i in range(2)]
        pqk = [lo[:, 2 + i, :] for i in range(2)]
        pv = [mid[:, i, 0:D] for i in range(2)]
        t3 = hi[:].bitcast(F16).rearrange("p a (h t) -> p a h t", t=P)
        sc = lo[:].rearrange("p (s j) q -> p s j q", s=2)
        po = [mid[:, i, :] for i in range(2)]
        pden = hi[:, 0, :]
        py = hi[:, 1, :].rearrange("p (c d) -> p c d", c=2)

        ld = m.sem("l_ld")
        z_done, t1_done, e1_done, mm_done = m.sem("l_z"), m.sem("l_t1"), m.sem("l_e1"), m.sem("l_mm")
        sq_done, v_ev, ss_done, rn_done, qk_done = m.sem("l_sq"), m.sem("l_v"), m.sem("l_ss"), m.sem("l_rn"), m.sem("l_qk")
        hi_done, lo_done, t3_done, e3_act, e3_dve = m.sem("l_hi"), m.sem("l_lo"), m.sem("l_t3"), m.sem("l_e3a"), m.sem("l_e3v")
        n_done, bo_done, vc_done = m.sem("l_n"), m.sem("l_bo"), m.sem("l_vc")
        s_done, e_done, pv_done = m.sem("a_s"), m.sem("a_e"), m.sem("a_pv")
        acc0, acc1, den_done, r_done = m.sem("a_acc0"), m.sem("a_acc1"), m.sem("a_den"), m.sem("a_r")
        o_done, y_done, x_done, st_done = m.sem("a_o"), m.sem("a_y"), m.sem("a_x"), m.sem("a_st")
        block = st.enter_context(nc.Block())

        @block.sync
        def _(sp):
            for k in range(2):
                sp.dma_start(w[:, k, :], a["WqkvT"][k * P:(k + 1) * P, :]).then_inc(ld, 16)
            sp.dma_start(gl[:], a["ln_l_g"].rearrange("(k p) -> p k", p=P), allow_slow_non_contiguous=True).then_inc(ld, 16)
            sp.dma_start(bl[:], a["ln_l_b"].rearrange("(k p) -> p k", p=P), allow_slow_non_contiguous=True).then_inc(ld, 16)
            sp.dma_start(bo[:], a["bo"].partition_broadcast(P)).then_inc(ld, 16)
            sp.dma_start(wo[:], a["WoT"].rearrange("(k p) n -> p k n", p=P)).then_inc(ld, 16)
            sp.wait_ge(g.cleared, 16)
        LOADS = 6 * 16

        def rows(k):
            return P if k < TB else M

        LAG = 4

        def pipeline(stages):
            for s in range(-1, TB + LAG):
                for stage, lag in stages:
                    if 0 <= s - lag < TB:
                        stage(s - lag)

        @block.tensor
        def _(pe):
            pe.wait_ge(ld, LOADS)

            def turn_z(first, l):
                t, i = first + l, l % 2
                pe.wait_ge(z_done, t + 1)
                if l >= 2:
                    pe.wait_ge(e1_done, t - 1)
                for k in range(2):
                    last = pe.transpose(zT[i][:, k, :], z[:, i, k * P:(k + 1) * P], g.ident[:])
                last.then_inc(t1_done, 1)

            def project(first, l):
                t, i = first + l, l % 2
                if l >= 2:
                    pe.wait_ge(qk_done, t - 1)
                    pe.wait_ge(v_ev, t - 1)
                    pe.wait_ge(sq_done, t - 1)
                pe.wait_ge(e1_done, t + 1)
                for k in range(2):
                    pe.matmul(pqk[i], lnT[:, i, k, :], w[:, k, 0:2 * D], start=(k == 0), stop=(k == 1))
                for k in range(2):
                    last = pe.matmul(pv[i], lnT[:, i, k, :], w[:, k, 2 * D:], start=(k == 0), stop=(k == 1))
                last.then_inc(mm_done, 1)

            def turn_parts(first, l):
                t, i = first + l, l % 2
                pe.wait_ge(hi_done, t + 1)
                pe.wait_ge(lo_done, t + 1)
                if l >= 1:
                    pe.wait_ge(e3_act, t)
                    pe.wait_ge(e3_dve, t)
                for h in range(H0):
                    pe.transpose(t3[:, 0, h, :], hl[:, i, h, 0:2, :].rearrange("p o d -> p (o d)"), g.ident16[:])
                for form in range(2):
                    for h in range(H0):
                        last = pe.transpose(t3[:, 1, form * H0 + h, :],
                                            hl[:, i, H0 + h, form:form + 2, :].rearrange("p o d -> p (o d)"), g.ident16[:])
                last.then_inc(t3_done, 1)

            def scores(b, n, fresh):
                u, k = divmod(n, KT)
                half, pair = divmod(u, 2)
                if not fresh:
                    pe.wait_ge(e_done, STEPS * b + n - 1)
                for j in range(2):
                    h = 2 * pair + j
                    q = qT[:, h, half * HALF:(half + 1) * HALF]
                    for form in range(2):
                        if k < TB:
                            kk = kT[:, form, h, k * P:(k + 1) * P]
                        else:
                            kk = g.kctx[:, form, bass.ds(b * H0 + h, 1), 0:M]
                            kk = kk.rearrange("p o m -> p (o m)")
                        last = pe.matmul(sc[0:rows(k), n % 2, j, :], kk, q, start=(form == 0), stop=(form == 1))
                last.then_inc(s_done, 1)

            def values(b, n):
                u, k = divmod(n, KT)
                pair = u % 2
                pe.wait_ge(e_done, STEPS * b + n + 1)
                if k == 0 and u >= 2:
                    pe.wait_ge(o_done, UNITS * b + u - 1)
                for j in range(2):
                    h = 2 * pair + j
                    last = pe.matmul(po[u % 2][j * HD0:(j + 1) * HD0, :], v[0:rows(k), k, h * HD0:(h + 1) * HD0],
                                     pr[0:rows(k), n % 4, j, :], start=(k == 0), stop=(k == KT - 1))
                last.then_inc(pv_done, 1)

            def denominators(b, u):
                pe.wait_ge(acc0, TB * (UNITS * b + u + 1))
                pe.wait_ge(acc1, TB * (UNITS * b + u + 1))
                if u > 0:
                    pe.wait_ge(r_done, UNITS * b + u)
                for j in range(2):
                    last = pe.matmul(pden[j * HD0:(j + 1) * HD0, :], g.ones[:, 0:HD0], acc[:, u % 2, j, :],
                                     start=True, stop=True)
                last.then_inc(den_done, 1)

            def output(b, half):
                pe.wait_ge(o_done, UNITS * b + 2 * half + 2)
                for r in range(2):
                    i = 2 * half + r
                    if i > 0:
                        pe.wait_ge(x_done, UNITS * b + i)
                    for c in range(2):
                        tok = (2 * r + c) * P
                        for pair in range(2):
                            last = pe.matmul(py[:, c, :], oT[:, pair, tok:tok + P], wo[:, pair, :],
                                             start=(pair == 0), stop=(pair == 1))
                    last.then_inc(y_done, 1)

            with pe.Fori(0, B) as b:
                first = b * TB
                pipeline([(lambda l: turn_z(first, l), 0), (lambda l: project(first, l), 1),
                          (lambda l: turn_parts(first, l), 4)])
                pe.wait_ge(e3_act, first + TB)
                pe.wait_ge(e3_dve, first + TB)
                pe.wait_ge(vc_done, 2 * b + 2)
                for n in range(STEPS):
                    if n == 0:
                        scores(b, 0, True)
                    if n < STEPS - 1:
                        scores(b, n + 1, n == 0)
                    values(b, n)
                    u, k = divmod(n, KT)
                    if u > 0 and k == 1:
                        denominators(b, u - 1)
                    if u == 2 and k == 6:
                        output(b, 0)
                denominators(b, UNITS - 1)
                output(b, 1)
                pe.wait_ge(x_done, UNITS * b + UNITS)

        @block.scalar
        def _(act):
            act.wait_ge(ld, LOADS)

            def gain_and_shift(first, l):
                t, i = first + l, l % 2
                act.wait_ge(t1_done, t + 1)
                if l >= 2:
                    act.wait_ge(mm_done, t - 1)
                for k in range(2):
                    last = act.activation(lnT[:, i, k, :], zT[i][:, k, :], ACT.Identity, bias=bl[:, k:k + 1],
                                          scale=gl[:, k:k + 1])
                last.then_inc(e1_done, 1)

            def squares(first, l):
                t, i = first + l, l % 2
                act.wait_ge(mm_done, t + 1)
                if l >= 2:
                    act.wait_ge(ss_done, 2 * t - 2)
                act.activation(sq[:, i, :], pqk[i], ACT.Square).then_inc(sq_done, 1)
                act.copy(v[:, l, :], pv[i]).then_inc(v_ev, 1)

            def high(first, l):
                t, i = first + l, l % 2
                act.wait_ge(n_done, t + 1)
                if l >= 2:
                    act.wait_ge(t3_done, t - 1)
                act.copy(hl[:, i, :, 0:3:2, :],
                         qk[:, i].rearrange("p (h o) d -> p h o d", o=1).to_broadcast([P, 2 * H0, 2, HD0])).then_inc(hi_done, 1)

            def keys_out(first, l):
                act.wait_ge(t3_done, first + l + 1)
                act.copy(kT[:, :, :, l * P:(l + 1) * P], t3[:, 1].rearrange("p (f h) t -> p f h t", f=2)
                         ).then_inc(e3_act, 1)

            with act.Fori(0, B) as b:
                first = b * TB
                pipeline([(lambda l: high(first, l), 3), (lambda l: gain_and_shift(first, l), 0),
                          (lambda l: squares(first, l), 1), (lambda l: keys_out(first, l), 4)])
                for n in range(STEPS):
                    k = n % KT
                    act.wait_ge(s_done, STEPS * b + n + 1)
                    if n >= 4:
                        u4, k4 = divmod(n - 4, KT)
                        act.wait_ge(pv_done, STEPS * b + n - 3)
                        act.wait_ge(acc0, TB * (UNITS * b + u4) + max(k4, 1))
                        act.wait_ge(acc1, TB * (UNITS * b + u4) + max(k4, 1))
                    r = rows(k)
                    if n == TB:
                        act.wait_ge(vc_done, 2 * b + 2)
                    bias = g.shift[:, B:B + 1] if k < TB else cshift[:]
                    act.activation(pr[0:r, n % 4], sc[0:r, n % 2], ACT.Exp, bias=bias).then_inc(e_done, 1)

        def sum_up(eng, sem, j, b, n):
            u, k = divmod(n, KT)
            if k == 0:
                return
            eng.wait_ge(e_done, STEPS * b + n + 1)
            if k == 1:
                if u >= 2:
                    eng.wait_ge(den_done, UNITS * b + u - 1)
                eng.tensor_tensor(acc[:, u % 2, j, :], pr[:, (n - 1) % 4, j, :], pr[:, n % 4, j, :],
                                  ALU.add).then_inc(sem, 1)
            else:
                eng.wait_ge(sem, TB * (UNITS * b + u) + k - 1)
                r = rows(k)
                eng.tensor_tensor(acc[0:r, u % 2, j, :], acc[0:r, u % 2, j, :], pr[0:r, n % 4, j, :],
                                  ALU.add).then_inc(sem, 1)

        @block.gpsimd
        def _(pool):
            pool.wait_ge(ld, LOADS)

            def root(t, i):
                pool.wait_ge(ss_done, 2 * t + 2)
                pool.tensor_tensor(rn[:, i, :], ss[:, i, :], g.neghalf[:, 0:2 * H0], ALU.pow).then_inc(rn_done, 1)
                pool.wait_ge(z_done, t + 1)
                xt = g.x[:, bass.ds(t, 1), :].rearrange("p o d -> p (o d)")
                pool.tensor_tensor(xt, xt, bo[:], ALU.add).then_inc(bo_done, 1)

            with pool.Fori(0, B) as b:
                pool.wait_ge(mm_done, b * TB + 1)
                pool.tensor_copy(cshift[:], g.shift[0:M, bass.ds(b, 1)]).then_inc(vc_done, 1)
                pool.tensor_copy(v[0:M, TB, :], g.vctx[:, bass.ds(b, 1), :].rearrange("p o d -> p (o d)")).then_inc(vc_done, 1)
                with pool.Fori(0, TB // 2) as n:
                    for i in range(2):
                        root(b * TB + 2 * n + i, i)
                for n in range(STEPS):
                    sum_up(pool, acc1, 1, b, n)

        @block.vector
        def _(dve):
            def center(first, l):
                t, i = first + l, l % 2
                if l >= 2:
                    dve.wait_ge(t1_done, t - 1)
                dve.tensor_scalar(z[:, i:i + 1, :], g.x[:, bass.ds(t, 1), :], g.mean[:, bass.ds(t, 1)],
                                  g.rstd[:, bass.ds(t, 1)], ALU.subtract, ALU.mult).then_inc(z_done, 1)

            def sums(first, l):
                t, i = first + l, l % 2
                dve.wait_ge(sq_done, t + 1)
                dve.tensor_reduce(ss[:, i, :], sq[:, i, :].rearrange("p (h d) -> p h d", d=HD0), AX.X,
                                  ALU.add).then_inc(ss_done, 1)
                dve.wait_ge(ss_done, 2 * t + 1)
                dve.tensor_scalar(ss[:, i, :], ss[:, i, :], 1.0 / HD0, RMS_EPS ** 2, ALU.mult, ALU.max).then_inc(ss_done, 1)

            def norm(first, l):
                t, i = first + l, l % 2
                dve.wait_ge(rn_done, t + 1)
                if l >= 2:
                    dve.wait_ge(hi_done, t - 1)
                dve.tensor_tensor(qk[:, i], pqk[i].rearrange("p (h d) -> p h d", d=HD0),
                                  rn[:, i, :].rearrange("p (h o) -> p h o", o=1).to_broadcast([P, 2 * H0, HD0]),
                                  ALU.mult).then_inc(qk_done, 1)
                dve.wait_ge(qk_done, t + 1)
                dve.tensor_tensor(qk[:, i, 0:H0, :], qk[:, i, 0:H0, :],
                                  g.gain[:].rearrange("p (o d) -> p o d", o=1).to_broadcast([P, H0, HD0]),
                                  ALU.mult).then_inc(n_done, 1)

            def low(first, l):
                t, i = first + l, l % 2
                dve.wait_ge(hi_done, t + 1)
                dve.tensor_tensor(hl[:, i, :, 1, :], qk[:, i], hl[:, i, :, 0, :], ALU.subtract).then_inc(lo_done, 1)

            def queries_out(first, l):
                dve.wait_ge(t3_done, first + l + 1)
                dve.tensor_copy(qT[:, :, l * P:(l + 1) * P], t3[:, 0, 0:H0, :]).then_inc(e3_dve, 1)

            def normalise(b, u):
                half, pair = divmod(u, 2)
                dve.wait_ge(den_done, UNITS * b + u + 1)
                dve.reciprocal(rden[:], pden).then_inc(r_done, 1)
                dve.wait_ge(r_done, UNITS * b + u + 1)
                dve.wait_ge(pv_done, STEPS * b + KT * (u + 1))
                dve.tensor_tensor(oT[:, pair, :], po[u % 2], rden[:], ALU.mult).then_inc(o_done, 1)

            def residual(b, half):
                for r in range(2):
                    i = 2 * half + r
                    dve.wait_ge(y_done, UNITS * b + i + 1)
                    xt = g.x[:, bass.ds(b * TB + 2 * i, 2), :]
                    dve.tensor_tensor(xt, xt, py, ALU.add).then_inc(x_done, 1)
                    dve.wait_ge(x_done, UNITS * b + i + 1)
                    for c in range(2):
                        t = bass.ds(b * TB + 2 * i + c, 1)
                        dve.bn_stats(g.stats[:, t, :], g.x[:, t, :]).then_inc(st_done, 1)

            with dve.Fori(0, B) as b:
                first = b * TB
                pipeline([(lambda l: low(first, l), 3), (lambda l: norm(first, l), 2), (lambda l: center(first, l), -1),
                          (lambda l: sums(first, l), 1), (lambda l: queries_out(first, l), 4)])
                for n in range(STEPS):
                    u, k = divmod(n, KT)
                    sum_up(dve, acc0, 0, b, n)
                    if u > 0 and k == 2:
                        normalise(b, u - 1)
                    if u == 2 and k == 7:
                        residual(b, 0)
                normalise(b, UNITS - 1)
                residual(b, 1)
            dve.wait_ge(st_done, T)


def hold(eng, g, sem, value):
    eng.wait_ge(sem, value)
    eng.wait_ge(g.consts, 4)


C = 2
NT = (2 * B * S + E * (C * P - 1)) // (C * P)
NT += NT % 2
SLOTS = NT * C * P
PIECE = 1024


def route(nc, g, gate, first_pieces, last_pieces):
    R = 4
    GROUP = T // (E // 2)
    assert len(first_pieces) == 2
    late = [(src, dst, e) for src, dst in last_pieces for e in range(E)]
    EACH = T // len(late)
    NP = 2 * E
    with ExitStack() as st:
        m = Mem(nc, st)
        nm = g.name
        z = m.sb(nm("z"), [P, 4, D])
        zr = m.sb(nm("zr"), [P, R, D])
        zhl = m.sb(nm("zhl"), [P, R, 2 * D], F16)
        stage = m.sb(nm("stage"), [P, 4, PIECE])
        zTs = m.sb(nm("zTs"), [P, 2, 2, P])
        gw = m.sb(nm("gw"), [P, 2, E])
        upper = m.sb(nm("upper"), [P, P])
        rev = m.sb(nm("rev"), [P, E])
        tiles = m.sb(nm("tiles"), [1, NT, E])
        lg, l2, oh0, oh1, wk, wk2, ex = (m.sb(nm(f"r{i}"), [P, T, E]) for i in range(7))
        m0, m1, r0, e1, sm, den, pf = (m.sb(nm(f"c{i}"), [P, T]) for i in range(7))
        cnt, cumt, base = (m.sb(nm(f"e{i}"), [P, E]) for i in range(3))
        cnti, cntj = (m.sb(nm(f"ei{i}"), [P, E], I32) for i in range(2))
        tef = m.sb(nm("tef"), [1, NT])
        pz = [m.ps(nm(f"pz{i}"), [P, 4, P]) for i in range(2)]
        plg = m.ps(nm("plg"), [P, 512])
        prk = m.ps(nm("prk"), [P, 512])
        ptot = m.ps(nm("ptot"), [P, 512])

        ld, z_done, hi_done, lo_done = m.sem(nm("ld")), m.sem(nm("z_")), m.sem(nm("hi")), m.sem(nm("lo"))
        t_done, ev, lg_done, p_step = m.sem(nm("t")), m.sem(nm("ev")), m.sem(nm("lg")), m.sem(nm("p"))
        v_step, ex_done, rk_done = m.sem(nm("v")), m.sem(nm("ex")), m.sem(nm("rk"))
        w_ld = [m.sem(nm(f"w_ld{i}")) for i in range(4)]
        w_hi, w_lo, zr_done = m.sem(nm("w_hi")), m.sem(nm("w_lo")), m.sem(nm("zr_"))
        sc = [m.sem(nm(f"sc{i}")) for i in range(R)]
        block = st.enter_context(nc.Block())

        @block.sync
        def _(sp):
            sp.dma_start(gw[:], gate.rearrange("(k p) e -> p k e", p=P)).then_inc(ld, 16)

            def fetch(n, early):
                for r in range(4):
                    src = first_pieces[r % 2][0]
                    if not early:
                        sp.wait_ge(w_lo, 4 * n - 4 + r + 1)
                    sp.dma_start(stage[:, r:r + 1, :].rearrange("p o (k n) -> p (o k) n", k=src(0).shape[1]),
                                 src(2 * n + r // 2)).then_inc(w_ld[r], 16)

            fetch(0, True)
            with sp.Fori(1, E // 2) as n:
                fetch(n, False)
            for j, (src, _, e) in enumerate(late):
                r = j % 4
                sp.wait_ge(w_lo, NP + j - 3)
                sp.dma_start(stage[:, r:r + 1, :].rearrange("p o (k n) -> p (o k) n", k=src(0).shape[1]), src(e)
                             ).then_inc(w_ld[r], 16)

        @block.gpsimd
        def _(pool):
            pool.affine_select(out=upper[:], in_=g.ones[:], compare_op=ALU.is_gt, fill=0.0, base=0,
                               pattern=[[1, P]], channel_multiplier=-1).then_inc(p_step, 1)
            pool.iota(rev[:], pattern=[[-1, E]], base=E, channel_multiplier=0,
                      allow_small_or_imprecise_dtypes=True).then_inc(p_step, 1)
            pool.iota(tiles[:], pattern=[[1, NT], [0, E]], base=0, channel_multiplier=0,
                      allow_small_or_imprecise_dtypes=True).then_inc(p_step, 1)
            pool.wait_ge(v_step, ROUTED)
            for t in range(T):
                pool.wait_ge(lo_done, t + 1)
                for pos in g.pos:
                    pool.indirect_dma_start(g.zs, bass.IndirectOffsetOnAxis(ap=pos[:, t:t + 1], axis=0),
                                            zhl[:, t % R, :], None).then_inc(sc[t % R], 16)
            for i in range(R):
                pool.wait_ge(sc[i], 32 * (T // R))

        @block.tensor
        def _(pe):
            pe.wait_ge(ld, 16)

            def turn(t, i, early):
                pe.wait_ge(z_done, t + 1)
                if not early:
                    pe.wait_ge(ev, t - 1)
                for k in range(2):
                    last = pe.transpose(pz[i % 2][:, k, :], z[:, i, k * P:(k + 1) * P], g.ident[:])
                last.then_inc(t_done, 1)

            def logits(t, i):
                pe.wait_ge(ev, t + 1)
                for k in range(2):
                    last = pe.matmul(plg[:, bass.ds(t * E, E)], zTs[:, i, k, :], gw[:, k, :],
                                     start=(k == 0), stop=(k == 1))
                last.then_inc(lg_done, 1)

            turn(0, 0, True)
            for i in range(1, 4):
                turn(i, i, i == 1)
                logits(i - 1, (i - 1) % 2)
            with pe.Fori(1, T // 4) as n:
                for i in range(4):
                    turn(4 * n + i, i, False)
                    logits(4 * n + i - 1, (i - 1) % 2)
            logits(T - 1, 1)
            pe.wait_ge(p_step, 3)
            pe.wait_ge(v_step, CHOSEN)
            sel = wk[:].rearrange("p t e -> p (t e)")
            pe.matmul(prk[:, 0:T * E], upper[:], sel, start=True, stop=True)
            pe.matmul(ptot[:, 0:T * E], g.ones[:], sel, start=True, stop=True).then_inc(rk_done, 1)

        @block.scalar
        def _(act):
            def copy_out(t, i, early):
                act.wait_ge(t_done, t + 1)
                if not early:
                    act.wait_ge(lg_done, t - 1)
                act.copy(zTs[:, i], pz[i][:, 0:2, :]).then_inc(ev, 1)

            def high(r, loads, dst, e):
                hold(act, g, w_ld[r], 16 * loads)
                act.mul(dst(0, e), stage[:, r:r + 1, :], WS).then_inc(w_hi, 1)

            def group(n, early):
                for r in range(GROUP):
                    copy_out(GROUP * n + r, r % 2, early and r < 2)
                    if r % 2 == 0:
                        high(r // 2, n + 1, first_pieces[r // 2 % 2][1], 2 * n + r // 4)

            group(0, True)
            with act.Fori(1, E // 2) as n:
                group(n, False)
            act.wait_ge(v_step, SHIFTED)
            act.activation(ex[:], l2[:], ACT.Exp).then_inc(ex_done, 1)
            act.activation(e1[:], sm[:], ACT.Exp).then_inc(ex_done, 1)
            for t in range(T):
                act.wait_ge(zr_done, t + 1)
                if t >= R:
                    act.wait_ge(sc[t % R], 32 * (t // R))
                act.copy(zhl[:, t % R, 0:D], zr[:, t % R, :]).then_inc(hi_done, 1)
                if t % EACH == 0:
                    j = t // EACH
                    high(j % 4, E // 2 + j // 4 + 1, late[j][1], late[j][2])

        def over_e(x):
            return x.rearrange("p (t o) -> p t o", o=1).to_broadcast([P, T, E])

        def over_t(x, n=T, p=P):
            return x.rearrange("p (o e) -> p o e", o=1).to_broadcast([p, n, E])

        @block.vector
        def _(dve):
            def center(t, i, early):
                if not early:
                    dve.wait_ge(t_done, t - 3)
                dve.tensor_scalar(z[:, i:i + 1, :], g.x[:, bass.ds(t, 1), :], g.mean[:, bass.ds(t, 1)],
                                  g.rstd[:, bass.ds(t, 1)], ALU.subtract, ALU.mult).then_inc(z_done, 1)

            def weight_low(r, before, dst, e):
                hold(dve, g, w_hi, before + 1)
                dve.scalar_tensor_tensor(dst(1, e), stage[:, r:r + 1, :], WS, dst(0, e), ALU.mult, ALU.subtract
                                         ).then_inc(w_lo, 1)

            def group(n, final):
                for r in range(0, GROUP, 2):
                    weight_low(r // 2, 4 * n + r // 2, first_pieces[r // 2 % 2][1], 2 * n + r // 4)
                    for i in range(4, 6):
                        if not (final and r + i >= GROUP):
                            center(GROUP * n + r + i, (r + i) % 4, False)

            for t in range(4):
                center(t, t, True)
            with dve.Fori(0, E // 2 - 1) as n:
                group(n, False)
            group(E // 2 - 1, True)

            def low(t):
                dve.wait_ge(hi_done, t + 1)
                dve.tensor_tensor(zhl[:, t % R, D:], zr[:, t % R, :], zhl[:, t % R, 0:D], ALU.subtract
                                  ).then_inc(lo_done, 1)

            n = [0]

            def step(ins):
                n[0] += 1
                ins.then_inc(v_step, 1)
                dve.wait_ge(v_step, n[0])

            dve.wait_ge(lg_done, T)
            dve.wait_ge(p_step, 3)
            step(dve.tensor_copy(lg[:].rearrange("p t e -> p (t e)"), plg[:, 0:T * E]))
            for src, top, oh in ((lg, m0, oh0), (l2, m1, oh1)):
                step(dve.tensor_reduce(top[:], src[:], AX.X, ALU.max))
                step(dve.tensor_tensor(wk[:], src[:], over_e(top[:]), ALU.is_equal))
                step(dve.tensor_tensor(wk2[:], wk[:], over_t(rev[:]), ALU.mult))
                step(dve.tensor_reduce(r0[:], wk2[:], AX.X, ALU.max))
                step(dve.tensor_tensor(oh[:], over_t(rev[:]), over_e(r0[:]), ALU.is_equal))
                if src is lg:
                    step(dve.scalar_tensor_tensor(l2[:].rearrange("p t e -> p (t e)"), oh0[:].rearrange("p t e -> p (t e)"),
                                                  MASKED, lg[:].rearrange("p t e -> p (t e)"), ALU.mult, ALU.add))
            step(dve.tensor_tensor(wk[:], oh0[:], oh1[:], ALU.add))
            assert n[0] == CHOSEN
            step(dve.tensor_tensor(l2[:], lg[:], over_e(m0[:]), ALU.subtract))
            step(dve.tensor_tensor(sm[:], m1[:], m0[:], ALU.subtract))
            assert n[0] == SHIFTED
            dve.wait_ge(ex_done, 2)
            step(dve.tensor_reduce(den[:], ex[:], AX.X, ALU.add))
            step(dve.tensor_scalar(den[:], den[:], 1e-9, 1.0, ALU.mult, ALU.add))
            step(dve.tensor_tensor(den[:], den[:], e1[:], ALU.add))
            step(dve.reciprocal(g.wt[:, 0, :], den[:]))
            step(dve.tensor_tensor(g.wt[:, 1, :], g.wt[:, 0, :], e1[:], ALU.mult))
            dve.wait_ge(rk_done, 1)
            tot = ptot[:, 0:T * E].rearrange("p (t e) -> p t e", e=E)
            step(dve.tensor_copy(ex[:], tot))
            step(dve.tensor_scalar(wk2[:], ex[:], 0.0, 1.0, ALU.mult, ALU.add))
            for e in range(E):
                last = dve.tensor_tensor_scan(l2[:, :, e], wk2[:, :, e], ex[:, :, e], 0.0, ALU.mult, ALU.add)
                n[0] += 1
                last.then_inc(v_step, 1)
            dve.wait_ge(v_step, n[0])
            step(dve.tensor_scalar(cnti[:], l2[:, T - 1, :], float(C * P - 1), None, ALU.add))
            step(dve.tensor_scalar(cntj[:], cnti[:], (C * P).bit_length() - 1, None, ALU.logical_shift_right))
            step(dve.tensor_copy(cnt[:], cntj[:]))
            step(dve.tensor_tensor_scan(cumt[:], wk2[:, 0, :], cnt[:], 0.0, ALU.mult, ALU.add))
            step(dve.tensor_tensor(base[:], cumt[:], cnt[:], ALU.subtract))
            step(dve.tensor_scalar(base[:], base[:], float(C * P), None, ALU.mult))
            step(dve.tensor_tensor(l2[:], l2[:], ex[:], ALU.subtract))
            step(dve.tensor_tensor(l2[:], l2[:], prk[:, 0:T * E].rearrange("p (t e) -> p t e", e=E), ALU.add))
            step(dve.tensor_tensor(l2[:], l2[:], over_t(base[:]), ALU.add))
            for oh, pos in zip((oh0, oh1), g.pos):
                step(dve.tensor_tensor(wk2[:], oh[:], l2[:], ALU.mult))
                step(dve.tensor_reduce(pf[:], wk2[:], AX.X, ALU.add))
                step(dve.tensor_copy(pos[:], pf[:]))
            step(dve.tensor_tensor(tiles[:], tiles[:], over_t(cumt[0:1, :], NT, 1), ALU.is_ge))
            step(dve.tensor_reduce(tef[:], tiles[:], AX.X, ALU.add))
            step(dve.tensor_scalar(tef[:], tef[:], float(E - 1), None, ALU.min))
            step(dve.tensor_copy(g.expert[:], tef[:]))
            assert n[0] == ROUTED, n[0]
            for t in range(T):
                if t >= R:
                    dve.wait_ge(lo_done, t - R + 1)
                dve.tensor_scalar(zr[:, t % R, :], g.x[:, t, :], g.mean[:, t:t + 1], g.rstd[:, t:t + 1],
                                  ALU.subtract, ALU.mult).then_inc(zr_done, 1)
                if t >= 1:
                    low(t - 1)
                if t % EACH == EACH - 1:
                    j = t // EACH
                    weight_low(j % 4, NP + j, late[j][1], late[j][2])
            low(T - 1)
            dve.wait_ge(lo_done, T)


CHOSEN = 13
SHIFTED = 15
ROUTED = 49


def experts(nc, g, a, layer):
    F = F0 if layer == 0 else F1
    NF = F // P
    NU = 8
    Q = 4
    HQ = NF // 2
    with ExitStack() as st:
        m = Mem(nc, st)
        nm = g.name
        zt = m.sb(nm("zt"), [P, 2, C, 2 * D], F16)
        zTs = m.sb(nm("zTt"), [P, 2, 4, C * P], F16)
        h32 = m.sb(nm("h32"), [P, 2, 2, C * P])
        gt = m.sb(nm("g32"), [P, 2, 2, C * P]) if layer else None
        hh = m.sb(nm("hh"), [P, 2, NF, C * P], F16)
        hl = m.sb(nm("hl"), [P, 2, NF, C * P], F16)
        ysb = m.sb(nm("ysb"), [P, 2, C, D])
        if layer == 0:
            b1 = m.sb(nm("b1"), [P, E, NF])
            b2 = m.sb(nm("b2"), [P, E, D])
        pz = [m.ps(nm(f"pzt{i}"), [P, 4, C * P], F16) for i in range(2)]
        ph = m.ps(nm("ph"), [P, Q, 2, C * P])
        py = [m.ps(nm(f"pyt{i}"), [P, 2, D]) for i in range(C)]

        ld = [m.sem(nm(f"zld{i}")) for i in range(2)]
        sto = [m.sem(nm(f"yst{i}")) for i in range(2)]
        bld, t_done, zev = m.sem(nm("bld")), m.sem(nm("tt")), m.sem(nm("zev"))
        up_done, act_done, g_done = m.sem(nm("up")), m.sem(nm("act")), m.sem(nm("gd"))
        hi_done, lo_done, dn_done, yev = m.sem(nm("hid")), m.sem(nm("lod")), m.sem(nm("dn")), m.sem(nm("yev"))
        block = st.enter_context(nc.Block())
        up_w, down_w = g.up_w, g.down_w

        def expert_of(eng, i):
            return eng.value_load(g.expert[0:1, bass.ds(i, 1)], min_val=0, max_val=E - 1)

        @block.sync
        def _(sp):
            if layer == 0:
                sp.dma_start(b1[:], a["b1"].rearrange("e (f p) -> p e f", p=P), allow_slow_non_contiguous=True
                             ).then_inc(bld, 16)
                sp.dma_start(b2[:], a["b2"].partition_broadcast(P)).then_inc(bld, 16)
            zs = g.zs.rearrange("(i c p) d -> p i c d", p=P, c=C)
            ys = g.ys.rearrange("(i c p) d -> p i c d", p=P, c=C)

            def load(i, s, early):
                if not early:
                    sp.wait_ge(t_done, i - 1)
                sp.dma_start(zt[:, s:s + 1], zs[:, bass.ds(i, 1)]).then_inc(ld[s], 16)

            for i in range(4):
                load(i, i % 2, i < 2)
            with sp.Fori(2, NT // 2) as n:
                for s in range(2):
                    load(2 * n + s, s, False)
                    sp.wait_ge(yev, C * (2 * n + s - 3))
                    sp.dma_start(ys[:, bass.ds(2 * n + s - 4, 1)], ysb[:, s:s + 1]).then_inc(sto[s], 16)
            for i in range(NT - 4, NT):
                sp.wait_ge(yev, C * (i + 1))
                sp.dma_start(ys[:, i], ysb[:, i % 2]).then_inc(sto[i % 2], 16)
            for i in range(2):
                sp.wait_ge(sto[i], 16 * (NT // 2))

        @block.tensor
        def _(pe):
            def turn(i, s, half, early):
                pe.wait_ge(ld[s], 16 * half + 16)
                if not early:
                    pe.wait_ge(zev, i - 1)
                for c in range(C):
                    for k in range(4):
                        last = pe.transpose(pz[s][:, k, c * P:(c + 1) * P], zt[:, s, c, k * P:(k + 1) * P], g.ident16[:])
                last.then_inc(t_done, 1)

            def up(i, s, e, early):
                hold(pe, g, zev, i + 1)
                for q in range(Q):
                    if not early:
                        if layer == 0:
                            hold(pe, g, act_done, Q * i - Q + q + 1)
                        else:
                            hold(pe, g, act_done if q < HQ else g_done, HQ * i - HQ + q % HQ + 1)
                    for f in range(2):
                        n = 0
                        for k in range(2):
                            for wp, zp in ((0, 0), (0, 1), (1, 0)):
                                last = pe.matmul(ph[:, q, f, :], up_w(wp, e, k, 2 * q + f), zTs[:, s, 2 * zp + k, :],
                                                 start=(n == 0), stop=(n == 5))
                                n += 1
                    last.then_inc(up_done, 1)

            def down(i, s, e, early):
                pe.wait_ge(hi_done, HQ * i + HQ)
                hold(pe, g, lo_done, HQ * i + HQ)
                for c in range(C):
                    if not early:
                        hold(pe, g, yev, C * i - C + c + 1)
                    n = 0
                    for f in range(NF):
                        for wp, hp in ((0, hh), (0, hl), (1, hh)):
                            last = pe.matmul(py[c][:, 0, :], hp[:, s, f, c * P:(c + 1) * P], down_w(wp, e, f),
                                             start=(n == 0), stop=(n == 3 * NF - 1))
                            n += 1
                    last.then_inc(dn_done, 1)

            if layer == 0:
                pe.wait_ge(bld, 32)
            e = [expert_of(pe, i) for i in range(3)]
            turn(0, 0, 0, True)
            turn(1, 1, 0, True)
            up(0, 0, e[0], True)
            up(1, 1, e[1], False)
            turn(2, 0, 1, False)
            down(0, 0, e[0], True)
            up(2, 0, e[2], False)
            turn(3, 1, 1, False)
            down(1, 1, e[1], False)
            with pe.Fori(1, NT // 2 - 1) as n:
                e = [expert_of(pe, 2 * n + i) for i in range(3)]
                for s in range(2):
                    i = 2 * n + s
                    up(i + 1, 1 - s, e[s + 1], False)
                    turn(i + 2, s, n + 1, False)
                    down(i, s, e[s], False)
            e = [expert_of(pe, NT - 2 + i) for i in range(2)]
            up(NT - 1, 1, e[1], False)
            down(NT - 2, 0, e[0], False)
            down(NT - 1, 1, e[1], False)

        def steps(eng, body):
            body(0, 0, True)
            body(1, 1, True)
            with eng.Fori(1, NT // 2) as n:
                body(2 * n, 0, False)
                body(2 * n + 1, 1, False)

        @block.scalar
        def _(act):
            if layer == 0:
                act.wait_ge(bld, 32)

            def body(i, s, early):
                if layer == 0:
                    e = expert_of(act, i)

                def units(q):
                    if not (early and s == 0 and q < 2):
                        if layer == 0:
                            act.wait_ge(lo_done, HQ * i + q - 1)
                        else:
                            act.wait_ge(g_done, HQ * i + q - 1)
                    hold(act, g, up_done, Q * i + q + 1)
                    if layer == 0:
                        for f in range(2):
                            last = act.activation(h32[:, q % 2, f, :], ph[:, q, f, :], ACT.Relu,
                                                  bias=b1[:, bass.ds(e, 1), 2 * q + f], scale=1.0 / WS)
                    else:
                        last = act.activation(h32[:, q], ph[:, q], ACT.Silu, scale=1.0 / WS)
                    last.then_inc(act_done, 1)

                def high(q):
                    if layer == 0:
                        act.wait_ge(act_done, HQ * i + q + 1)
                    else:
                        act.wait_ge(g_done, HQ * i + q + 1)
                    if not early and q == 0:
                        act.wait_ge(dn_done, C * i - C)
                    src = gt if layer else h32
                    act.copy(hh[:, s, 2 * q:2 * q + 2, :], src[:, q % 2]).then_inc(hi_done, 1)

                units(0)
                for q in range(1, HQ):
                    units(q)
                    high(q - 1)
                high(HQ - 1)

            steps(act, body)

        @block.vector
        def _(dve):
            if layer == 0:
                dve.wait_ge(bld, 32)

            def evacuate(i, s, early):
                dve.wait_ge(t_done, i + 1)
                if not early:
                    dve.wait_ge(up_done, Q * i - Q)
                dve.tensor_copy(zTs[:, s], pz[s][:]).then_inc(zev, 1)

            def hidden(i, s, early):
                if layer:
                    for q in range(HQ):
                        if not (early and s == 0):
                            dve.wait_ge(lo_done, HQ * i + q - 1)
                        dve.wait_ge(act_done, HQ * i + q + 1)
                        dve.wait_ge(up_done, Q * i + HQ + q + 1)
                        dve.scalar_tensor_tensor(gt[:, q].rearrange("p f t -> p (f t)"),
                                                 ph[:, HQ + q].rearrange("p f t -> p (f t)"), 1.0 / WS,
                                                 h32[:, q].rearrange("p f t -> p (f t)"), ALU.mult, ALU.mult
                                                 ).then_inc(g_done, 1)
                if not early:
                    dve.wait_ge(dn_done, C * i - C)
                src = gt if layer else h32
                for q in range(HQ):
                    dve.wait_ge(hi_done, HQ * i + q + 1)
                    dve.tensor_tensor(hl[:, s, 2 * q:2 * q + 2, :], src[:, q % 2], hh[:, s, 2 * q:2 * q + 2, :],
                                      ALU.subtract).then_inc(lo_done, 1)

            def result(i, s, half, early):
                if layer == 0:
                    e = expert_of(dve, i)
                if not early:
                    dve.wait_ge(sto[s], 16 * half)
                for c in range(C):
                    if layer == 0:
                        hold(dve, g, dn_done, C * i + c + 1)
                        dve.scalar_tensor_tensor(ysb[:, s, c:c + 1, :], py[c][:, 0:1, :], 1.0 / WS,
                                                 b2[:, bass.ds(e, 1), :], ALU.mult, ALU.add).then_inc(yev, 1)
                    else:
                        dve.wait_ge(dn_done, C * i + c + 1)
                        dve.tensor_scalar(ysb[:, s, c, :], py[c][:, 0, :], 1.0 / WS, None, ALU.mult).then_inc(yev, 1)

            evacuate(0, 0, True)
            evacuate(1, 1, True)
            hidden(0, 0, True)
            hidden(1, 1, True)
            evacuate(2, 0, False)
            result(0, 0, 0, True)
            hidden(2, 0, False)
            evacuate(3, 1, False)
            result(1, 1, 0, True)
            with dve.Fori(1, NT // 2 - 1) as n:
                for s in range(2):
                    i = 2 * n + s
                    hidden(i + 1, 1 - s, False)
                    evacuate(i + 2, s, False)
                    result(i, s, n, False)
            hidden(NT - 1, 1, False)
            result(NT - 2, 0, NT // 2 - 1, False)
            result(NT - 1, 1, NT // 2 - 1, False)
            dve.wait_ge(yev, C * NT)


def combine(nc, g, out=None):
    with ExitStack() as st:
        m = Mem(nc, st)
        nm = g.name
        R = 4
        rows = m.sb(nm("rows"), [P, R, 2, D])
        got = [m.sem(nm(f"got{i}")) for i in range(R)]
        added = m.sem(nm("added"))
        block = st.enter_context(nc.Block())

        if out is not None:
            @block.sync
            def _(sp):
                G = 4
                for i in range(T // G):
                    sp.wait_ge(added, 3 * G * (i + 1))
                    sp.dma_start(out[i * G * P:(i + 1) * G * P, :].rearrange("(t p) d -> p t d", p=P),
                                 g.x[:, i * G:(i + 1) * G, :]).then_inc(g.x_in, 16)
                sp.wait_ge(g.x_in, 16 * (B + T // G))

        @block.gpsimd
        def _(pool):
            for t in range(T):
                if t >= R:
                    pool.wait_ge(added, 3 * (t - R) + 2)
                for k in range(2):
                    pool.indirect_dma_start(rows[:, t % R, k, :], None, g.ys,
                                            bass.IndirectOffsetOnAxis(ap=g.pos[k][:, t:t + 1], axis=0)
                                            ).then_inc(got[t % R], 16)

        @block.vector
        def _(dve):
            for t in range(T):
                dve.wait_ge(got[t % R], 32 * (t // R + 1))
                for k in range(2):
                    if k:
                        dve.wait_ge(added, 3 * t + 1)
                    dve.scalar_tensor_tensor(g.x[:, t, :], rows[:, t % R, k, :], g.wt[:, k, t:t + 1], g.x[:, t, :],
                                             ALU.mult, ALU.add).then_inc(added, 1)
                dve.wait_ge(added, 3 * t + 2)
                dve.bn_stats(g.stats[:, t, :], g.x[:, t, :]).then_inc(added, 1)
            dve.wait_ge(added, 3 * T)


def attention1_context(nc, g, a, at):
    with ExitStack() as st:
        m = Mem(nc, st)
        wk = m.sb("wk1", [P, 2, D])
        wv = m.sb("wv1", [P, 2, D])
        mask8 = m.sb("mask8", [P, B, M], U8)
        mask = m.sb("mask1f", [P, B, M])
        own = m.sb("own", [P, 8])
        own2 = m.sb("own2", [P, 8])
        kT = m.sb("kT1", [P, 2, B, M])
        pk = m.ps("pk1", [P, 2, 512])
        pv = m.ps("pv1", [M, B, 512])
        ld, pool_done, mm_done, v_step, v_ev = m.sem("k_ld"), m.sem("k_pool"), m.sem("k_mm"), m.sem("k_v"), m.sem("k_vev")
        kbd_done, wo_ld = m.sem("k_bd"), m.sem("k_wo")
        block = st.enter_context(nc.Block())

        @block.sync
        def _(sp):
            for w, src in ((wk, a["Wk1"]), (wv, a["Wv1"])):
                sp.dma_start(w[:, 0, :], src[0:P, :]).then_inc(ld, 16)
                sp.dma_start(w[0:DC - P, 1, :], src[P:DC, :]).then_inc(ld, 16)
            sp.dma_start(mask8[:], a["mask1"].partition_broadcast(P)).then_inc(ld, 16)
            sp.dma_start(at.wq[:], a["Wq1"].rearrange("(k p) n -> p k n", p=P)).then_inc(ld, 16)
            sp.dma_start(at.wo[:], a["Wo1"].rearrange("(k p) n -> p k n", p=P)).then_inc(wo_ld, 16)
            sp.wait_ge(wo_ld, 16)

        @block.gpsimd
        def _(pool):
            pool.memset(at.v[:], 0.0).then_inc(pool_done, 1)
            pool.affine_select(out=own2[:], in_=g.ones[:, 0:8], compare_op=ALU.is_ge, fill=0.0, base=0,
                               pattern=[[-HD1, 8]], channel_multiplier=1).then_inc(pool_done, 1)
            pool.wait_ge(pool_done, 2)
            pool.affine_select(out=own[:], in_=own2[:], compare_op=ALU.is_ge, fill=0.0, base=HD1 - 1,
                               pattern=[[HD1, 8]], channel_multiplier=-1).then_inc(pool_done, 1)

        @block.tensor
        def _(pe):
            pe.wait_ge(ld, 16 * 6)
            for hg in range(2):
                for k, r in ((0, P), (1, DC - P)):
                    pe.matmul(pk[:, hg, 0:B * M], wk[0:r, k, hg * P:(hg + 1) * P], g.ctxT[0:r, k, :, 0:M],
                              start=(k == 0), stop=(k == 1))
            for b in range(B):
                for k, r in ((0, P), (1, DC - P)):
                    last = pe.matmul(pv[:, b, 0:D], g.ctxT[0:r, k, b, 0:M], wv[0:r, k, :],
                                     start=(k == 0), stop=(k == 1))
            last.then_inc(mm_done, 1)

        @block.scalar
        def _(act):
            act.wait_ge(mm_done, 1)
            act.wait_ge(pool_done, 1)
            for b in range(B):
                own_v = pv[:, b, 0:D].rearrange("p (h o d) -> p h o d", o=2, d=HD1)
                for o in range(2):
                    act.copy(at.v[:, b, o:H1:2, o * HD1:(o + 1) * HD1], own_v[:, :, o, :]).then_inc(v_ev, 1)
            act.wait_ge(v_ev, 2 * B)

        @block.vector
        def _(dve):
            dve.wait_ge(ld, 16 * 6)
            dve.tensor_copy(mask[:], mask8[:]).then_inc(v_step, 1)
            dve.wait_ge(v_step, 1)
            dve.tensor_scalar(at.bias[:], mask[:], 1.0, -MASKED, ALU.subtract, ALU.mult).then_inc(v_step, 1)
            dve.wait_ge(mm_done, 1)
            for hg in range(2):
                dve.scalar_tensor_tensor(kT[:, hg].rearrange("p b m -> p (b m)"), pk[:, hg, 0:B * M], SCALE1,
                                         mask[:].rearrange("p b m -> p (b m)"), ALU.mult, ALU.mult).then_inc(v_step, 1)
            dve.wait_ge(v_step, 4)
            dve.wait_ge(pool_done, 3)
            for b in range(B):
                for hg in range(2):
                    dve.tensor_tensor(at.k[:, b, hg], kT[:, hg, b:b + 1, :].to_broadcast([P, 8, M]),
                                      own[:].rearrange("p (j o) -> p j o", o=1).to_broadcast([P, 8, M]),
                                      ALU.mult).then_inc(kbd_done, 1)
            dve.wait_ge(kbd_done, 2 * B)


def attention1(nc, g, a, at):
    LAG = 4
    SLOT = 4
    C = 4
    with ExitStack() as st:
        m = Mem(nc, st)
        z = m.sb("z1", [P, 2, D])
        zT = m.sb("zT1", [P, 2, P])
        qT = m.sb("qT1", [P, 2, P])
        s = m.sb("s1", [P, SLOT, H1, M])
        mx = m.sb("mx1", [P, SLOT, H1])
        sm = m.sb("sm1", [P, SLOT, H1])
        rs = m.sb("rs1", [P, SLOT, H1])
        pT = m.sb("pT1", [M, 2, H1, P])
        oT = m.sb("oT1", [P, 2, P])
        v = m.sb("vcur", [M, H1, 32])
        psc = m.ps("psc1", [P, C, 512])
        pt = m.ps("pt1", [M, 2, 4, P])
        front = m.ps("front1", [P, 4, P])
        back = m.ps("back1", [P, 512])

        z_done, t_done, zT_ev, q_done, q_ev = (m.sem("b_" + n) for n in ("z", "t", "zTev", "q", "qev"))
        s_done, add_done, max_done, sub_done, e_done = (m.sem("b_" + n) for n in ("s", "add", "max", "sub", "e"))
        sum_done, r_done, n_done = (m.sem("b_" + n) for n in ("sum", "r", "n"))
        pt_done, pt_ev, v_done, o_done, o_ev, y_done, x_done, st_done = (
            m.sem("b_" + n) for n in ("pt", "ptev", "v", "o", "oev", "y", "x", "st"))
        block = st.enter_context(nc.Block())

        def steps(eng, body):
            head = LAG + 1
            for c in range(head):
                body(0, 0, c, lambda x: 0 <= x)
            with eng.Fori(0, B - 1) as n:
                for r in range(TB):
                    body(n * TB, n, head + r, lambda x: True)
            last = (B - 1) * TB
            for c in range(head, TB + LAG + 1):
                body(last, B - 1, c, lambda x: x < TB)

        @block.tensor
        def _(pe):
            def body(base, b0, c, live):
                if live(c):
                    t = base + c
                    if c > 0:
                        pe.wait_ge(q_ev, t)
                    pe.wait_ge(z_done, t + 1)
                    for k in range(2):
                        last = pe.transpose(front[:, k, :], z[:, c % 2, k * P:(k + 1) * P], g.ident[:])
                    last.then_inc(t_done, 1)
                d = c - LAG
                if live(d):
                    t = base + d
                    pe.wait_ge(n_done, t + 1)
                    for n in range(4):
                        if d > 0 or n >= 2:
                            pe.wait_ge(pt_ev, 4 * t + n - 1)
                        for h in range(4 * n, 4 * n + 4):
                            last = pe.transpose(pt[:, n % 2, h % 4, :], s[:, d % SLOT, h, :], g.ident[:])
                        last.then_inc(pt_done, 1)
                if live(c):
                    t = base + c
                    pe.wait_ge(zT_ev, t + 1)
                    for hg in range(2):
                        for k in range(2):
                            last = pe.matmul(front[:, 2 + hg, :], at.wq[:, k, hg * P:(hg + 1) * P], zT[:, k, :],
                                             start=(k == 0), stop=(k == 1))
                    last.then_inc(q_done, 1)
                if live(d):
                    t = base + d
                    if d % TB == 0:
                        pe.wait_ge(v_done, b0 + d // TB + 1)
                    if d > 0:
                        pe.wait_ge(x_done, t)
                    pe.wait_ge(pt_ev, 4 * t + 4)
                    for hg in range(2):
                        for o in range(2):
                            for r in range(4):
                                h = 8 * hg + 2 * r + o
                                last = pe.matmul(back[32 * r:32 * r + 32, hg * P:(hg + 1) * P], v[:, h, :],
                                                 pT[:, d % 2, h, :], start=(o == 0), stop=(o == 1))
                    last.then_inc(o_done, 1)
                if live(c):
                    t = base + c
                    if c > 0:
                        pe.wait_ge(add_done, t)
                    pe.wait_ge(q_ev, t + 1)
                    for n in range(C):
                        last = pe.matmul(psc[:, n, 0:4 * M], qT[:, n // 2, :],
                                         at.k[:, bass.ds(b0 + c // TB, 1), n // 2, 4 * (n % 2):4 * (n % 2) + 4, :]
                                         .rearrange("p o j m -> p (o j m)"), start=True, stop=True)
                    last.then_inc(s_done, 1)
                if live(d):
                    pe.wait_ge(o_ev, base + d + 1)
                    for hg in range(2):
                        last = pe.matmul(back[:, 0:D], oT[:, hg, :], at.wo[:, hg, :], start=(hg == 0), stop=(hg == 1))
                    last.then_inc(y_done, 1)

            steps(pe, body)

        @block.scalar
        def _(act):
            def body(base, b0, c, live):
                if live(c):
                    t = base + c
                    act.wait_ge(t_done, t + 1)
                    act.copy(zT[:], front[:, 0:2, :]).then_inc(zT_ev, 1)
                d = c - LAG
                if live(d):
                    t = base + d
                    for n in range(4):
                        act.wait_ge(pt_done, 4 * t + n + 1)
                        act.copy(pT[:, d % 2, 4 * n:4 * n + 4, :], pt[:, n % 2]).then_inc(pt_ev, 1)
                if live(c):
                    t = base + c
                    act.wait_ge(q_done, t + 1)
                    act.copy(qT[:], front[:, 2:4, :]).then_inc(q_ev, 1)
                if live(d):
                    act.wait_ge(o_done, base + d + 1)
                    act.copy(oT[:].rearrange("p n t -> p (n t)"), back[:, 0:2 * P]).then_inc(o_ev, 1)
                if live(c - 2):
                    i, t = (c - 2) % SLOT, base + c - 2
                    act.wait_ge(sub_done, t + 1)
                    act.activation(s[:, i], s[:, i], ACT.Exp).then_inc(e_done, 1)

            steps(act, body)

        def per_key(x):
            return x.rearrange("p (h o) -> p h o", o=1).to_broadcast([P, H1, M])

        @block.gpsimd
        def _(pool):
            def body(base, b0, c, live):
                d = c - LAG
                if live(d) and d % TB == 0:
                    b = b0 + d // TB
                    if d > 0:
                        pool.wait_ge(o_done, base + d)
                    pool.tensor_copy(v[:].rearrange("p (o h) d -> p o h d", o=1), at.v[:, bass.ds(b, 1)]
                                     ).then_inc(v_done, 1)
                if live(c - 3):
                    i = (c - 3) % SLOT
                    pool.wait_ge(r_done, base + c - 2)
                    pool.tensor_tensor(s[:, i], s[:, i], per_key(rs[:, i, :]), ALU.mult).then_inc(n_done, 1)
                if live(c - 1):
                    i = (c - 1) % SLOT
                    pool.wait_ge(max_done, base + c)
                    pool.tensor_tensor(s[:, i], s[:, i], per_key(mx[:, i, :]), ALU.subtract).then_inc(sub_done, 1)

            steps(pool, body)

        @block.vector
        def _(dve):
            def center(base, c):
                t = base + c
                if c > 1:
                    dve.wait_ge(t_done, t - 1)
                dve.tensor_scalar(z[:, c % 2:c % 2 + 1, :], g.x[:, bass.ds(t, 1), :], g.mean[:, bass.ds(t, 1)],
                                  g.rstd[:, bass.ds(t, 1)], ALU.subtract, ALU.mult).then_inc(z_done, 1)

            def body(base, b0, c, live):
                if c == 0:
                    center(base, 0)
                if live(c - 3):
                    i, t = (c - 3) % SLOT, base + c - 3
                    dve.wait_ge(e_done, t + 1)
                    dve.tensor_reduce(sm[:, i, :], s[:, i], AX.X, ALU.add).then_inc(sum_done, 1)
                    dve.wait_ge(sum_done, t + 1)
                    dve.reciprocal(rs[:, i, :], sm[:, i, :]).then_inc(r_done, 1)
                if live(c - 1):
                    i, t = (c - 1) % SLOT, base + c - 1
                    if c - 1 >= SLOT:
                        dve.wait_ge(pt_done, 4 * (t - SLOT) + 4)
                    dve.wait_ge(s_done, t + 1)
                    dve.tensor_tensor(s[:, i].rearrange("p (n j) m -> p n j m", n=C),
                                      psc[:, :, 0:4 * M].rearrange("p n (j m) -> p n j m", m=M),
                                      at.bias[:, bass.ds(b0 + (c - 1) // TB, 1), :].rearrange("p (n o) m -> p n o m", n=1)
                                      .to_broadcast([P, C, 4, M]), ALU.add).then_inc(add_done, 1)
                    dve.wait_ge(add_done, t + 1)
                    dve.tensor_reduce(mx[:, i, :], s[:, i], AX.X, ALU.max).then_inc(max_done, 1)
                if live(c + 1):
                    center(base, c + 1)
                d = c - LAG
                if live(d):
                    t = base + d
                    dve.wait_ge(y_done, t + 1)
                    xt = g.x[:, bass.ds(t, 1), :]
                    dve.tensor_tensor(xt, xt, back[:, 0:D].rearrange("p (o d) -> p o d", o=1), ALU.add).then_inc(x_done, 1)
                    dve.wait_ge(x_done, t + 1)
                    dve.bn_stats(g.stats[:, bass.ds(t, 1), :], xt).then_inc(st_done, 1)

            steps(dve, body)
            dve.wait_ge(st_done, T)


def host_arrays(i):
    import numpy as np

    n = {k: np.asarray(v) for k, v in i.items()}
    c = np.ascontiguousarray
    return {
        "x": n["x"].reshape(B * S, D),
        "ctx": n["ctx_768"],
        "mask0": n["mask_BxS2_bk0"],
        "mask1": n["mask_BxS2_bf1"],
        "ln_x_g": n["L0_xattn_ln_x_g"], "ln_x_b": n["L0_xattn_ln_x_b"],
        "ln_l_g": n["L0_xattn_ln_l_g"], "ln_l_b": n["L0_xattn_ln_l_b"],
        "qn_g": n["L0_xattn_qn_g"], "kn_g": n["L0_xattn_kn_g"],
        "WqkvT": c(np.concatenate([n["L0_xattn_Wq"].T, n["L0_xattn_Wlkv"].T], axis=1)),
        "WkvT": c(n["L0_xattn_Wkv"].T),
        "WoT": c(n["L0_xattn_Wo"].T), "bo": n["L0_xattn_bo"],
        "routerT": c(n["L0_ffn_router_w"].T),
        "w1T": c(n["L0_ffn_w1"].transpose(0, 2, 1)), "b1": n["L0_ffn_b1"],
        "w2T": c(n["L0_ffn_w2"].transpose(0, 2, 1)), "b2": n["L0_ffn_b2"],
        "Wq1": n["L1_xattn_Wq"], "Wk1": n["L1_xattn_Wk"], "Wv1": n["L1_xattn_Wv"], "Wo1": n["L1_xattn_Wo"],
        "gate": n["L1_ffn_gate_w"],
        "u1": n["L1_ffn_w1"], "u2": n["L1_ffn_w2"], "u3": n["L1_ffn_w3"],
    }


def program(nc, a, out, start=0, stages=4):
    g = Names()
    g.phase = "e0_"
    g.name = lambda x: g.phase + x
    g.zs = nc.dram_tensor("sorted_tokens", [SLOTS, 2 * D], F16, kind="Internal").ap()
    g.ys = nc.dram_tensor("sorted_results", [SLOTS, D], F32, kind="Internal").ap()
    with ExitStack() as whole:
        mem = Mem(nc, whole)
        setup(nc, mem, g, a)
        with ExitStack() as st:
            m = Mem(nc, st)
            g.kctx = m.sb("kctx", [P, 2, B * H0, MP], F16)
            g.vctx = m.sb("vctx", [M, B, D])
            g.zeros = m.sb("zeros", [P, 2 * D], F16)
            attention0_inputs(nc, g, a)
            if start < 1 <= stages:
                token_stats(nc, g, "n0", False, twice=True)
                attention0(nc, g, a)
        wA = mem.sb("weights_a", [P, 2, E, 2 * F0], F16)

        def blocks(w, offset):
            return lambda part, e: w[:, part, bass.ds(e, 1), offset:offset + PIECE]

        def block_of(w, part, e, offset, n):
            return w[:, part, bass.ds(e, 1), offset:offset + n].rearrange("p o n -> p (o n)")

        def rows_of(w, k0, k):
            return lambda e: w[bass.ds(e, 1), k0 * P:(k0 + k) * P, :].rearrange("o (k p) f -> p (o k) f", p=P)

        if start < 2 <= stages:
            token_stats(nc, g, "n1", start == 1)
            with ExitStack() as st:
                wB = Mem(nc, st).sb("weights_b", [P, 2, E, (F0 // P) * D], F16)
                route(nc, g, a["routerT"],
                      [(rows_of(a["w1T"], k, 1), blocks(wA, k * F0)) for k in range(2)],
                      [(rows_of(a["w2T"], 4 * k, 4), blocks(wB, k * PIECE)) for k in range(2)])
                g.up_w = lambda part, e, k, f: block_of(wA, part, e, k * F0 + f * P, P)
                g.down_w = lambda part, e, f: block_of(wB, part, e, f * D, D)
                experts(nc, g, a, 0)
            combine(nc, g)
        if start < 3 <= stages:
            with ExitStack() as st:
                m = Mem(nc, st)
                at = Names()
                at.k = m.sb("kbd", [P, B, 2, 8, M])
                at.v = m.sb("vpad", [M, B, H1, 32])
                at.bias = m.sb("bias1", [P, B, M])
                at.wq = m.sb("wq1", [P, 2, D])
                at.wo = m.sb("wo1", [P, 2, D])
                attention1_context(nc, g, a, at)
                token_stats(nc, g, "n2", start == 2)
                attention1(nc, g, a, at)
        if start < 4 <= stages:
            g.phase = "e1_"
            token_stats(nc, g, "n3", start == 3)
            with ExitStack() as st:
                w3 = Mem(nc, st).sb("weights_3", [P, 2, E, (F1 // P) * D], F16)
                route(nc, g, a["gate"],
                      [(rows_of(a["u1"], 0, 2), blocks(wA, 0)), (rows_of(a["u2"], 0, 2), blocks(wA, PIECE))],
                      [(rows_of(a["u3"], 0, 4), blocks(w3, 0))])
                g.up_w = lambda part, e, k, f: block_of(wA, part, e, f // 4 * PIECE + k * F1 + f % 4 * P, P)
                g.down_w = lambda part, e, f: block_of(w3, part, e, f * D, D)
                experts(nc, g, a, 1)
            combine(nc, g, out)
        else:
            finish(nc, g, out)


def finish(nc, g, out):
    with ExitStack() as st:
        block = st.enter_context(nc.Block())

        @block.sync
        def _(sp):
            sp.dma_start(out.rearrange("(t p) d -> p t d", p=P), g.x[:]).then_inc(g.x_in, 16)
            sp.wait_ge(g.x_in, 16 * (B + 1))


def kernel(**inputs):
    import concourse.bacc as bacc
    from concourse.bass_utils import run_bass_kernel_spmd
    nc = bacc.Bacc("TRN2", target_bir_lowering=False, num_devices=1)
    arrays = {f"in_{name}": array for name, array in host_arrays(inputs).items()}
    views = {name[3:]: nc.dram_tensor(name, array.shape, mybir.dt.from_np(array.dtype), kind="ExternalInput").ap()
             for name, array in arrays.items()}
    out = nc.dram_tensor("out_dram", (B, S, D), F32, kind="ExternalOutput").ap()
    program(nc, views, out.rearrange("b s d -> (b s) d"))
    return run_bass_kernel_spmd(nc, [arrays], core_ids=[0]).results[0]["out_dram"]
```

```python
from contextlib import ExitStack

import concourse.bass as bass
from concourse import mybir

F32 = mybir.dt.float32
F16 = mybir.dt.float16
I32 = mybir.dt.int32
U32 = mybir.dt.uint32
U8 = mybir.dt.uint8
ALU = mybir.AluOpType
ACT = mybir.ActivationFunctionType
AX = mybir.AxisListType

P = 128
B = 4
S = 1024
T = B * S // P
TB = S // P
D = 256
DC = 192
M = 77
MP = 80
LN_EPS = 1e-5
RMS_EPS = 1e-8
MASKED = -1e30

H0, HD0 = 4, 64
SCALE0 = HD0 ** -0.5
H1, HD1 = 16, 16
SCALE1 = HD1 ** -0.5

E = 8
F0, F1 = 1024, 512
WS = 64.0


class Names:
    pass


class Mem:

    def __init__(self, nc, stack):
        self.nc, self.stack = nc, stack

    def sb(self, name, shape, dt=F32):
        return self.stack.enter_context(self.nc.sbuf_tensor(name, shape, dt))

    def ps(self, name, shape, dt=F32):
        return self.stack.enter_context(self.nc.psum_tensor(name, shape, dt))

    def sem(self, name):
        return self.stack.enter_context(self.nc.semaphore(name))


def setup(nc, mem, g):
    g.x = mem.sb("x_sb", [P, T, D])
    g.ident = mem.sb("ident", [P, P])
    g.ident16 = mem.sb("ident16", [P, P], F16)
    g.ones = mem.sb("ones", [P, P])
    g.neghalf = mem.sb("neghalf", [P, 64])
    g.ctxT = mem.sb("ctxT", [P, 2, B, MP])
    g.stats = mem.sb("stats", [P, T, 6])
    g.mean = mem.sb("mean", [P, T])
    g.rstd = mem.sb("rstd", [P, T])
    g.gain = mem.sb("gain", [P, HD0])
    g.shift = mem.sb("shift", [P, B + 1])
    g.pos = mem.sb("pos", [P, T, 2], U32)
    g.wt = mem.sb("wt", [P, 2, T])
    g.expert = mem.sb("expert", [1, NT], I32)
    g.cleared = mem.sem("cleared")
    g.x_in = mem.sem("x_in")
    g.consts = mem.sem("consts")
    g.stat_steps, g.stat_roots = mem.sem("stat_steps"), mem.sem("stat_roots")
    g.stat_seen, g.stat_runs = 0, 1
    g.moved = [mem.sem(f"moved{i}") for i in range(4)]
    g.moved_before = 0


def attention0_inputs(nc, g, a):
    with ExitStack() as st:
        m = Mem(nc, st)
        ctx = m.sb("ctx", [M, B, DC])
        tmp = m.sb("tok_tmp", [P, 4, T])
        tok_ve = m.sb("tok_ve", [P, T])
        zc = m.sb("zc", [M, B, DC])
        stats = m.sb("stats_c", [M, B, 6])
        mv = m.sb("mv_c", [M, B, 2])
        ve = m.sb("ve_c", [M, B])
        rstd = m.sb("rstd_c", [M, B])
        lnT = m.sb("lnT_c", [P, 2, B, M])
        gx = m.sb("gx", [P, 2])
        bx = m.sb("bx", [P, 2])
        wkv = m.sb("wkv", [P, 2, 2 * D])
        sq = m.sb("sq_c", [M, B, D])
        ss = m.sb("ss_c", [M, B * H0])
        rn = m.sb("rn_c", [M, B * H0])
        kn = m.sb("kn_c", [M, B * H0, HD0])
        khl = m.sb("khl_c", [M, B * H0, 3, HD0], F16)
        mask = m.sb("mask_c", [M, B], U8)
        gq = m.sb("gq_row", [P, HD0])
        gk = m.sb("gk_row", [P, HD0])
        gabs = m.sb("gabs", [P, 1])
        kv = m.ps("kv_c", [M, B, 2 * D])
        tr = m.ps("tr_c", [P, 4, 512])

        ld_ctx, ld_w, ld_g = m.sem("ld_ctx"), m.sem("ld_wkv"), m.sem("ld_g")
        v_step, p_step = m.sem("c_v_step"), m.sem("c_p_step")
        t_done, ev, kv_done, sq_done = m.sem("c_t_done"), m.sem("c_ev"), m.sem("c_kv"), m.sem("c_sq")
        x_step, ld_next = m.sem("c_x"), m.sem("ld_next")
        hi_done, kt_done, kt_ev = m.sem("c_hi"), m.sem("c_ktd"), m.sem("c_ktev")
        block = st.enter_context(nc.Block())

        @block.sync
        def _(sp):
            sp.dma_start(ctx[:], a["ctx"].rearrange("b m d -> m b d")).then_inc(ld_ctx, 16)
            sp.wait_ge(ld_w, 32)
            for i in range(B):
                sp.dma_start(g.x[:, i * TB:(i + 1) * TB, :],
                             a["x"][i * S:(i + 1) * S, :].rearrange("(t p) d -> p t d", p=P)).then_inc(g.x_in, 16)
            sp.dma_start(g.wqkv[:], a["WqkvT"].rearrange("(k p) n -> p k n", p=P)).then_inc(ld_next, 16)
            sp.dma_start(g.wo[:], a["WoT"].rearrange("(k p) n -> p k n", p=P)).then_inc(ld_next, 16)
            sp.dma_start(g.gl[:], a["ln_l_g"].rearrange("(k p) -> p k", p=P), allow_slow_non_contiguous=True).then_inc(ld_next, 16)
            sp.dma_start(g.bl[:], a["ln_l_b"].rearrange("(k p) -> p k", p=P), allow_slow_non_contiguous=True).then_inc(ld_next, 16)
            sp.dma_start(g.bo[:], a["bo"].partition_broadcast(P)).then_inc(ld_next, 16)
            sp.wait_ge(ld_next, 16 * 5)
            sp.wait_ge(p_step, 1)
            sp.wait_ge(g.x_in, 16 * B)
            sp.dma_start(g.zs.rearrange("(n p) d -> p n d", p=P),
                         g.zeros[:].rearrange("p (o d) -> p o d", o=1).to_broadcast([P, C * NT, 2 * D])).then_inc(g.cleared, 16)

        @block.scalar
        def _(act):
            act.preload_act_table_set("natural_log_exp_and_others")
            act.dma_start(wkv[:, 0, :], a["WkvT"][0:P, :]).then_inc(ld_w, 16)
            act.dma_start(wkv[0:DC - P, 1, :], a["WkvT"][P:DC, :]).then_inc(ld_w, 16)
            for v, dst in ((a["ln_x_g"], gx), (a["ln_x_b"], bx)):
                act.dma_start(dst[:, 0:1], v[0:P].rearrange("(p o) -> p o", o=1)).then_inc(ld_g, 16)
                act.dma_start(dst[0:DC - P, 1:2], v[P:DC].rearrange("(p o) -> p o", o=1)).then_inc(ld_g, 16)
            act.dma_start(mask[:], a["mask0"].rearrange("b m -> m b"), allow_slow_non_contiguous=True).then_inc(ld_g, 16)
            act.dma_start(gq[:], a["qn_g"].partition_broadcast(P)).then_inc(ld_g, 16)
            act.dma_start(gk[:], a["kn_g"].partition_broadcast(P)).then_inc(ld_g, 16)
            act.wait_ge(t_done, 1)
            act.copy(g.ctxT[:, 0, :, 0:M], tr[:, 0, 0:B * M].rearrange("p (b m) -> p b m", b=B)).then_inc(ev, 1)
            act.copy(g.ctxT[0:DC - P, 1, :, 0:M],
                     tr[0:DC - P, 1, 0:B * M].rearrange("p (b m) -> p b m", b=B)).then_inc(ev, 1)
            act.wait_ge(t_done, 2)
            act.wait_ge(ld_g, 16 * 7)
            act.activation(lnT[:, 0], tr[:, 2, 0:B * M].rearrange("p (b m) -> p b m", b=B), ACT.Identity,
                           bias=bx[:, 0:1], scale=gx[:, 0:1]).then_inc(ev, 1)
            act.activation(lnT[0:DC - P, 1], tr[0:DC - P, 3, 0:B * M].rearrange("p (b m) -> p b m", b=B),
                           ACT.Identity, bias=bx[0:DC - P, 1:2], scale=gx[0:DC - P, 1:2]).then_inc(ev, 1)
            act.wait_ge(kv_done, 1)
            act.activation(sq[:], kv[:, :, 0:D], ACT.Square).then_inc(sq_done, 1)
            act.copy(g.vctx[:], kv[:, :, D:2 * D]).then_inc(sq_done, 1)
            act.wait_ge(v_step, 16)
            act.copy(khl[:, :, 0:3:2, :], kn[:].rearrange("p (h o) d -> p h o d", o=1).to_broadcast([M, B * H0, 2, HD0])
                     ).then_inc(hi_done, 1)
            act.wait_ge(kt_done, 1)
            t16 = tr[:].bitcast(F16)
            for n in range(4):
                act.copy(g.kctx[:, n // 2, (n % 2) * 8:(n % 2) * 8 + 8, 0:M],
                         t16[:, n, 0:8 * MP].rearrange("p (h m) -> p h m", h=8)[:, :, 0:M]).then_inc(kt_ev, 1)
            act.wait_ge(kt_ev, 4)

        @block.gpsimd
        def _(pool):
            pool.memset(g.zeros[:], 0.0).then_inc(p_step, 1)
            pool.memset(g.ident[:], 0.0).then_inc(p_step, 1)
            pool.memset(g.ident16[:], 0.0).then_inc(p_step, 1)
            pool.memset(g.ones[:], 1.0).then_inc(g.consts, 1)
            pool.memset(g.neghalf[:], -0.5).then_inc(g.consts, 1)
            pool.wait_ge(p_step, 3)
            for t in (g.ident, g.ident16):
                pool.affine_select(out=t[:], in_=t[:], compare_op=ALU.not_equal, fill=1.0, base=0,
                                   pattern=[[-1, P]], channel_multiplier=1).then_inc(g.consts, 1)
            pool.wait_ge(g.consts, 4)
            pool.wait_ge(v_step, 9)
            pool.tensor_tensor(rstd[:], ve[:], g.neghalf[0:M, 0:B], ALU.pow).then_inc(p_step, 1)
            pool.wait_ge(v_step, 15)
            pool.tensor_tensor(rn[:], ss[:], g.neghalf[0:M, 0:B * H0], ALU.pow).then_inc(p_step, 1)
            pool.wait_ge(g.stat_steps, 7)
            pool.tensor_tensor(g.rstd[:], tok_ve[:], g.neghalf[:, 0:T], ALU.pow).then_inc(g.stat_roots, 1)
            pool.wait_ge(g.stat_roots, 1)
            pool.wait_ge(p_step, 5)

        @block.vector
        def _(dve):
            def token_rows(t0, t1):
                if t0 == 0:
                    dve.wait_ge(g.x_in, 16 * B)
                for t in range(t0, t1):
                    dve.bn_stats(g.stats[:, t, :], g.x[:, t, :]).then_inc(x_step, 1)

            dve.wait_ge(ld_ctx, 16)
            for b in range(B):
                dve.bn_stats(stats[:, b, :], ctx[:, b, :]).then_inc(v_step, 1)
            dve.wait_ge(v_step, 4)
            for b in range(B):
                dve.bn_aggr(mv[:, b, :], stats[:, b, :]).then_inc(v_step, 1)
            dve.wait_ge(v_step, 8)
            dve.tensor_scalar(ve[:], mv[:, :, 1], LN_EPS, None, ALU.add).then_inc(v_step, 1)
            dve.wait_ge(p_step, 4)
            for b in range(B):
                dve.tensor_scalar(zc[:, b, :], ctx[:, b, :], mv[:, b, 0:1], rstd[:, b:b + 1],
                                  ALU.subtract, ALU.mult).then_inc(v_step, 1)
            token_rows(0, T // 2)
            dve.wait_ge(sq_done, 1)
            dve.tensor_reduce(ss[:], sq[:].rearrange("p b (h d) -> p (b h) d", d=HD0), AX.X,
                              ALU.add).then_inc(v_step, 1)
            dve.wait_ge(v_step, 14)
            dve.tensor_scalar(ss[:], ss[:], 1.0 / HD0, RMS_EPS ** 2, ALU.mult, ALU.max).then_inc(v_step, 1)
            token_rows(T // 2, T)
            dve.wait_ge(x_step, T)
            summarise(dve, g, tmp, tok_ve, True)
            dve.wait_ge(p_step, 5)
            dve.wait_ge(sq_done, 2)
            dve.tensor_tensor(kn[:].rearrange("p (b h) d -> p b h d", b=B),
                              kv[:, :, 0:D].rearrange("p b (h d) -> p b h d", d=HD0),
                              rn[:].rearrange("p (b h o) -> p b h o", b=B, o=1).to_broadcast([M, B, H0, HD0]),
                              ALU.mult).then_inc(v_step, 1)
            dve.wait_ge(ld_g, 16 * 7)
            dve.scalar_tensor_tensor(g.gain[:], gq[:], SCALE0, gk[:], ALU.mult, ALU.mult).then_inc(v_step, 1)
            dve.wait_ge(v_step, 17)
            dve.tensor_reduce(gabs[:], g.gain[:], AX.X, ALU.max, apply_absolute_value=True).then_inc(v_step, 1)
            dve.wait_ge(v_step, 18)
            dve.tensor_scalar(g.shift[:, B:B + 1], gabs[:], -float(HD0), None, ALU.mult).then_inc(v_step, 1)
            dve.tensor_scalar(g.shift[0:M, 0:B], mask[:], 1.0, -MASKED, ALU.subtract, ALU.mult).then_inc(v_step, 1)
            dve.wait_ge(v_step, 20)
            dve.tensor_scalar(g.shift[0:M, 0:B], g.shift[0:M, 0:B], g.shift[0:M, B:B + 1], None,
                              ALU.add).then_inc(v_step, 1)
            dve.wait_ge(hi_done, 1)
            dve.tensor_tensor(khl[:, :, 1, :], kn[:], khl[:, :, 0, :], ALU.subtract).then_inc(v_step, 1)
            dve.wait_ge(v_step, 22)

        @block.tensor
        def _(pe):
            pe.wait_ge(ld_ctx, 16)
            pe.wait_ge(g.consts, 4)

            def turn(src, k0):
                for b in range(B):
                    pe.transpose(tr[:, k0, b * M:(b + 1) * M], src[:, b, 0:P], g.ident[0:M, 0:M])
                    last = pe.transpose(tr[0:DC - P, k0 + 1, b * M:(b + 1) * M], src[:, b, P:DC],
                                        g.ident[0:M, 0:M])
                last.then_inc(t_done, 1)

            turn(ctx, 0)
            pe.wait_ge(v_step, 13)
            turn(zc, 2)
            pe.wait_ge(ev, 4)
            pe.wait_ge(ld_w, 32)
            for b in range(B):
                pe.matmul(kv[:, b, :], lnT[:, 0, b, :], wkv[:, 0, :], start=True, stop=False)
                last = pe.matmul(kv[:, b, :], lnT[0:DC - P, 1, b, :], wkv[0:DC - P, 1, :], start=False, stop=True)
            last.then_inc(kv_done, 1)
            pe.wait_ge(hi_done, 1)
            pe.wait_ge(v_step, 22)
            t16 = tr[:].bitcast(F16)
            for n in range(2):
                for h in range(B * H0):
                    last = pe.transpose(t16[:, 2 * n + h // 8, (h % 8) * MP:(h % 8) * MP + M],
                                        khl[:, h, n:n + 2, :].rearrange("p o d -> p (o d)"), g.ident16[0:M, 0:M])
            last.then_inc(kt_done, 1)


def summarise(dve, g, tmp, ve, twice):
    seen = g.stat_seen
    g.stat_seen += 7
    stats, steps = g.stats, g.stat_steps
    dve.tensor_tensor(tmp[:, 0, :], stats[:, :, 1], stats[:, :, 4], ALU.add).then_inc(steps, 1)
    dve.tensor_tensor(tmp[:, 1, :], stats[:, :, 1], stats[:, :, 4], ALU.subtract).then_inc(steps, 1)
    dve.tensor_tensor(tmp[:, 2, :], stats[:, :, 2], stats[:, :, 5], ALU.add).then_inc(steps, 1)
    dve.wait_ge(steps, seen + 3)
    dve.tensor_scalar(g.mean[:], tmp[:, 0, :], 0.5, None, ALU.mult).then_inc(steps, 1)
    dve.tensor_tensor(tmp[:, 3, :], tmp[:, 1, :], tmp[:, 1, :], ALU.mult).then_inc(steps, 1)
    dve.wait_ge(steps, seen + 5)
    dve.scalar_tensor_tensor(tmp[:, 0, :], tmp[:, 3, :], D / 4, tmp[:, 2, :], ALU.mult, ALU.add).then_inc(steps, 1)
    dve.wait_ge(steps, seen + 6)
    grow, eps = (1.0 + LN_EPS, LN_EPS ** 2) if twice else (1.0, LN_EPS)
    dve.tensor_scalar(ve[:], tmp[:, 0, :], grow / D, eps, ALU.mult, ALU.add).then_inc(steps, 1)


def attention0(nc, g):
    HALF = S // 2
    KT = TB + 1
    UNITS = 4
    STEPS = UNITS * KT
    with ExitStack() as st:
        m = Mem(nc, st)
        z = m.sb("z0", [P, 2, D])
        lnT = m.sb("lnT0", [P, 2, 2, P])
        w, gl, bl, bo, wo = g.wqkv, g.gl, g.bl, g.bo, g.wo
        sq = m.sb("sq0", [P, 2, 2 * D])
        ss = m.sb("ss0", [P, 2, 2 * H0])
        rn = m.sb("rn0", [P, 2, 2 * H0])
        qk = m.sb("qk0", [P, 2, 2 * H0, HD0])
        hl = m.sb("hl0", [P, 2, 2 * H0, 3, HD0], F16)
        qT = m.sb("qT", [P, H0, S], F16)
        kT = m.sb("kT", [P, 2, H0, S], F16)
        v = m.sb("v0", [P, KT, D])
        pr = m.sb("probs", [P, 4, 2, HALF])
        acc = m.sb("acc", [P, 2, 2, HALF])
        oT = m.sb("oT0", [P, 2, HALF])
        rden = m.sb("rden", [P, HALF])
        cshift = m.sb("cshift", [M, 1])
        lo = m.ps("lower_banks", [P, 4, 512])
        mid = m.ps("middle_banks", [P, 2, 512])
        hi = m.ps("upper_banks", [P, 2, 512])
        zT = [lo[:, i, 0:2 * P].rearrange("p (k t) -> p k t", k=2) for i in range(2)]
        pqk = [lo[:, 2 + i, :] for i in range(2)]
        pv = [mid[:, i, 0:D] for i in range(2)]
        t3 = hi[:].bitcast(F16).rearrange("p a (h t) -> p a h t", t=P)
        sc = lo[:].rearrange("p (s j) q -> p s j q", s=2)
        po = [mid[:, i, :] for i in range(2)]
        pden = hi[:, 0, :]
        py = hi[:, 1, :].rearrange("p (c d) -> p c d", c=2)

        def y_bank(i):
            return py if i < 3 else pden.rearrange("p (c d) -> p c d", c=2)


        z_done, t1_done, e1_done, mm_done = m.sem("l_z"), m.sem("l_t1"), m.sem("l_e1"), m.sem("l_mm")
        sq_done, v_ev, ss_done, rn_done, qk_done = m.sem("l_sq"), m.sem("l_v"), m.sem("l_ss"), m.sem("l_rn"), m.sem("l_qk")
        hi_done, lo_done, t3_done, e3_act, e3_dve = m.sem("l_hi"), m.sem("l_lo"), m.sem("l_t3"), m.sem("l_e3a"), m.sem("l_e3v")
        n_done, bo_done, vc_done = m.sem("l_n"), m.sem("l_bo"), m.sem("l_vc")
        s_done, e_done, pv_done = m.sem("a_s"), m.sem("a_e"), m.sem("a_pv")
        acc0, acc1, den_done, r_done = m.sem("a_acc0"), m.sem("a_acc1"), m.sem("a_den"), m.sem("a_r")
        o_done, y_done, x_done, st_done = m.sem("a_o"), m.sem("a_y"), m.sem("a_x"), m.sem("a_st")
        block = st.enter_context(nc.Block())

        @block.sync
        def _(sp):
            sp.wait_ge(g.cleared, 16)
        def rows(k):
            return P if k < TB else M

        LAG = 4

        def pipeline(stages):
            for s in range(-1, TB + LAG):
                for stage, lag, start in stages:
                    if start <= s - lag < TB:
                        stage(s - lag)

        def batches(eng, body):
            with eng.Fori(0, B - 1) as b:
                body(b, True)
            body(B - 1, False)

        @block.tensor
        def _(pe):

            def turn_z(first, l):
                t, i = first + l, l % 2
                pe.wait_ge(z_done, t + 1)
                if l >= 2:
                    pe.wait_ge(e1_done, t - 1)
                for k in range(2):
                    last = pe.transpose(zT[i][:, k, :], z[:, i, k * P:(k + 1) * P], g.ident[:])
                last.then_inc(t1_done, 1)

            def project(first, l):
                t, i = first + l, l % 2
                if l >= 2:
                    pe.wait_ge(qk_done, t - 1)
                    pe.wait_ge(v_ev, t - 1)
                    pe.wait_ge(sq_done, t - 1)
                pe.wait_ge(e1_done, t + 1)
                for k in range(2):
                    pe.matmul(pqk[i], lnT[:, i, k, :], w[:, k, 0:2 * D], start=(k == 0), stop=(k == 1))
                for k in range(2):
                    last = pe.matmul(pv[i], lnT[:, i, k, :], w[:, k, 2 * D:], start=(k == 0), stop=(k == 1))
                last.then_inc(mm_done, 1)

            def turn_parts(first, l):
                t, i = first + l, l % 2
                pe.wait_ge(hi_done, t + 1)
                pe.wait_ge(lo_done, t + 1)
                if l >= 1:
                    pe.wait_ge(e3_act, t)
                    pe.wait_ge(e3_dve, t)
                for h in range(H0):
                    pe.transpose(t3[:, 0, h, :], hl[:, i, h, 0:2, :].rearrange("p o d -> p (o d)"), g.ident16[:])
                for form in range(2):
                    for h in range(H0):
                        last = pe.transpose(t3[:, 1, form * H0 + h, :],
                                            hl[:, i, H0 + h, form:form + 2, :].rearrange("p o d -> p (o d)"), g.ident16[:])
                last.then_inc(t3_done, 1)

            def scores(b, n, fresh):
                u, k = divmod(n, KT)
                half, pair = divmod(u, 2)
                if not fresh:
                    pe.wait_ge(e_done, STEPS * b + n - 1)
                for j in range(2):
                    h = 2 * pair + j
                    q = qT[:, h, half * HALF:(half + 1) * HALF]
                    for form in range(2):
                        if k < TB:
                            kk = kT[:, form, h, k * P:(k + 1) * P]
                        else:
                            kk = g.kctx[:, form, bass.ds(b * H0 + h, 1), 0:M]
                            kk = kk.rearrange("p o m -> p (o m)")
                        last = pe.matmul(sc[0:rows(k), n % 2, j, :], kk, q, start=(form == 0), stop=(form == 1))
                last.then_inc(s_done, 1)

            def values(b, n):
                u, k = divmod(n, KT)
                pair = u % 2
                pe.wait_ge(e_done, STEPS * b + n + 1)
                if k == 0 and u >= 2:
                    pe.wait_ge(o_done, UNITS * b + u - 1)
                for j in range(2):
                    h = 2 * pair + j
                    last = pe.matmul(po[u % 2][j * HD0:(j + 1) * HD0, :], v[0:rows(k), k, h * HD0:(h + 1) * HD0],
                                     pr[0:rows(k), n % 4, j, :], start=(k == 0), stop=(k == KT - 1))
                last.then_inc(pv_done, 1)

            def denominators(b, u):
                pe.wait_ge(acc0, TB * (UNITS * b + u + 1))
                pe.wait_ge(acc1, TB * (UNITS * b + u + 1))
                if u > 0:
                    pe.wait_ge(r_done, UNITS * b + u)
                for j in range(2):
                    last = pe.matmul(pden[j * HD0:(j + 1) * HD0, :], g.ones[:, 0:HD0], acc[:, u % 2, j, :],
                                     start=True, stop=True)
                last.then_inc(den_done, 1)

            def output(b, half):
                pe.wait_ge(o_done, UNITS * b + 2 * half + 2)
                for r in range(2):
                    i = 2 * half + r
                    if 0 < i < 3:
                        pe.wait_ge(x_done, UNITS * b + i)
                    for c in range(2):
                        tok = (2 * r + c) * P
                        for pair in range(2):
                            last = pe.matmul(y_bank(i)[:, c, :], oT[:, pair, tok:tok + P], wo[:, pair, :],
                                             start=(pair == 0), stop=(pair == 1))
                    last.then_inc(y_done, 1)

            def body(b, more):
                first = b * TB
                pipeline([(lambda l: turn_z(first, l), 0, 2), (lambda l: project(first, l), 1, 2),
                          (lambda l: turn_parts(first, l), 4, 0)])
                pe.wait_ge(e3_act, first + TB)
                pe.wait_ge(e3_dve, first + TB)
                pe.wait_ge(vc_done, 2 * b + 2)
                for n in range(STEPS):
                    if n == 0:
                        scores(b, 0, True)
                    if n < STEPS - 1:
                        scores(b, n + 1, n == 0)
                    values(b, n)
                    u, k = divmod(n, KT)
                    if u > 0 and k == 1:
                        denominators(b, u - 1)
                    if u == 2 and k == 6:
                        output(b, 0)
                if more:
                    turn_z(first + TB, 0)
                denominators(b, UNITS - 1)
                if more:
                    turn_z(first + TB, 1)
                    pe.wait_ge(o_done, UNITS * b + UNITS - 1)
                    project(first + TB, 0)
                output(b, 1)
                if more:
                    project(first + TB, 1)
                pe.wait_ge(x_done, UNITS * b + UNITS)

            turn_z(0, 0)
            turn_z(0, 1)
            project(0, 0)
            project(0, 1)
            batches(pe, body)

        @block.scalar
        def _(act):

            def gain_and_shift(first, l):
                t, i = first + l, l % 2
                act.wait_ge(t1_done, t + 1)
                if l >= 2:
                    act.wait_ge(mm_done, t - 1)
                for k in range(2):
                    last = act.activation(lnT[:, i, k, :], zT[i][:, k, :], ACT.Identity, bias=bl[:, k:k + 1],
                                          scale=gl[:, k:k + 1])
                last.then_inc(e1_done, 1)

            def squares(first, l):
                t, i = first + l, l % 2
                act.wait_ge(mm_done, t + 1)
                if l >= 2:
                    act.wait_ge(ss_done, 2 * t - 2)
                act.activation(sq[:, i, :], pqk[i], ACT.Square).then_inc(sq_done, 1)
                act.copy(v[:, l, :], pv[i]).then_inc(v_ev, 1)

            def high(first, l):
                t, i = first + l, l % 2
                act.wait_ge(n_done, t + 1)
                if l >= 2:
                    act.wait_ge(t3_done, t - 1)
                act.copy(hl[:, i, :, 0:3:2, :],
                         qk[:, i].rearrange("p (h o) d -> p h o d", o=1).to_broadcast([P, 2 * H0, 2, HD0])).then_inc(hi_done, 1)

            def keys_out(first, l):
                act.wait_ge(t3_done, first + l + 1)
                act.copy(kT[:, :, :, l * P:(l + 1) * P], t3[:, 1].rearrange("p (f h) t -> p f h t", f=2)
                         ).then_inc(e3_act, 1)

            def head(first):
                gain_and_shift(first, 0)
                gain_and_shift(first, 1)
                squares(first, 0)
                squares(first, 1)

            def body(b, more):
                first = b * TB
                pipeline([(lambda l: high(first, l), 3, 0), (lambda l: gain_and_shift(first, l), 0, 2),
                          (lambda l: squares(first, l), 1, 2), (lambda l: keys_out(first, l), 4, 0)])
                for n in range(STEPS):
                    k = n % KT
                    act.wait_ge(s_done, STEPS * b + n + 1)
                    if n >= 4:
                        u4, k4 = divmod(n - 4, KT)
                        act.wait_ge(pv_done, STEPS * b + n - 3)
                        act.wait_ge(acc0, TB * (UNITS * b + u4) + max(k4, 1))
                        act.wait_ge(acc1, TB * (UNITS * b + u4) + max(k4, 1))
                    r = rows(k)
                    if n == TB:
                        act.wait_ge(vc_done, 2 * b + 2)
                    bias = g.shift[:, B:B + 1] if k < TB else cshift[:]
                    act.activation(pr[0:r, n % 4], sc[0:r, n % 2], ACT.Exp, bias=bias).then_inc(e_done, 1)
                if more:
                    head(first + TB)

            head(0)
            batches(act, body)

        def sum_up(eng, sem, j, b, n):
            u, k = divmod(n, KT)
            if k == 0:
                return
            eng.wait_ge(e_done, STEPS * b + n + 1)
            if k == 1:
                if u >= 2:
                    eng.wait_ge(den_done, UNITS * b + u - 1)
                eng.tensor_tensor(acc[:, u % 2, j, :], pr[:, (n - 1) % 4, j, :], pr[:, n % 4, j, :],
                                  ALU.add).then_inc(sem, 1)
            else:
                eng.wait_ge(sem, TB * (UNITS * b + u) + k - 1)
                r = rows(k)
                eng.tensor_tensor(acc[0:r, u % 2, j, :], acc[0:r, u % 2, j, :], pr[0:r, n % 4, j, :],
                                  ALU.add).then_inc(sem, 1)

        @block.gpsimd
        def _(pool):

            def root(t, i):
                pool.wait_ge(ss_done, 2 * t + 2)
                pool.tensor_tensor(rn[:, i, :], ss[:, i, :], g.neghalf[:, 0:2 * H0], ALU.pow).then_inc(rn_done, 1)
                pool.wait_ge(z_done, t + 1)
                xt = g.x[:, bass.ds(t, 1), :].rearrange("p o d -> p (o d)")
                pool.tensor_tensor(xt, xt, bo[:], ALU.add).then_inc(bo_done, 1)

            with pool.Fori(0, B) as b:
                pool.wait_ge(mm_done, b * TB + 1)
                pool.tensor_copy(cshift[:], g.shift[0:M, bass.ds(b, 1)]).then_inc(vc_done, 1)
                pool.tensor_copy(v[0:M, TB, :], g.vctx[:, bass.ds(b, 1), :].rearrange("p o d -> p (o d)")).then_inc(vc_done, 1)
                with pool.Fori(0, TB // 2) as n:
                    for i in range(2):
                        root(b * TB + 2 * n + i, i)
                for n in range(STEPS):
                    sum_up(pool, acc1, 1, b, n)

        @block.vector
        def _(dve):
            def center(first, l):
                t, i = first + l, l % 2
                if l >= 2:
                    dve.wait_ge(t1_done, t - 1)
                dve.tensor_scalar(z[:, i:i + 1, :], g.x[:, bass.ds(t, 1), :], g.mean[:, bass.ds(t, 1)],
                                  g.rstd[:, bass.ds(t, 1)], ALU.subtract, ALU.mult).then_inc(z_done, 1)

            def sums(first, l):
                t, i = first + l, l % 2
                dve.wait_ge(sq_done, t + 1)
                dve.tensor_reduce(ss[:, i, :], sq[:, i, :].rearrange("p (h d) -> p h d", d=HD0), AX.X,
                                  ALU.add).then_inc(ss_done, 1)
                dve.wait_ge(ss_done, 2 * t + 1)
                dve.tensor_scalar(ss[:, i, :], ss[:, i, :], 1.0 / HD0, RMS_EPS ** 2, ALU.mult, ALU.max).then_inc(ss_done, 1)

            def norm(first, l):
                t, i = first + l, l % 2
                dve.wait_ge(rn_done, t + 1)
                if l >= 2:
                    dve.wait_ge(hi_done, t - 1)
                dve.tensor_tensor(qk[:, i], pqk[i].rearrange("p (h d) -> p h d", d=HD0),
                                  rn[:, i, :].rearrange("p (h o) -> p h o", o=1).to_broadcast([P, 2 * H0, HD0]),
                                  ALU.mult).then_inc(qk_done, 1)
                dve.wait_ge(qk_done, t + 1)
                dve.tensor_tensor(qk[:, i, 0:H0, :], qk[:, i, 0:H0, :],
                                  g.gain[:].rearrange("p (o d) -> p o d", o=1).to_broadcast([P, H0, HD0]),
                                  ALU.mult).then_inc(n_done, 1)

            def low(first, l):
                t, i = first + l, l % 2
                dve.wait_ge(hi_done, t + 1)
                dve.tensor_tensor(hl[:, i, :, 1, :], qk[:, i], hl[:, i, :, 0, :], ALU.subtract).then_inc(lo_done, 1)

            def queries_out(first, l):
                dve.wait_ge(t3_done, first + l + 1)
                dve.tensor_copy(qT[:, :, l * P:(l + 1) * P], t3[:, 0, 0:H0, :]).then_inc(e3_dve, 1)

            def normalise(b, u):
                half, pair = divmod(u, 2)
                dve.wait_ge(den_done, UNITS * b + u + 1)
                dve.reciprocal(rden[:], pden).then_inc(r_done, 1)
                dve.wait_ge(r_done, UNITS * b + u + 1)
                dve.wait_ge(pv_done, STEPS * b + KT * (u + 1))
                dve.tensor_tensor(oT[:, pair, :], po[u % 2], rden[:], ALU.mult).then_inc(o_done, 1)

            def residual(b, half):
                for r in range(2):
                    i = 2 * half + r
                    dve.wait_ge(y_done, UNITS * b + i + 1)
                    xt = g.x[:, bass.ds(b * TB + 2 * i, 2), :]
                    dve.tensor_tensor(xt, xt, y_bank(i), ALU.add).then_inc(x_done, 1)
                    dve.wait_ge(x_done, UNITS * b + i + 1)
                    for c in range(2):
                        t = bass.ds(b * TB + 2 * i + c, 1)
                        dve.bn_stats(g.stats[:, t, :], g.x[:, t, :]).then_inc(st_done, 1)

            def body(b, more):
                first = b * TB
                pipeline([(lambda l: center(first, l), -1, 2), (lambda l: low(first, l), 3, 0),
                          (lambda l: norm(first, l), 2, 0), (lambda l: sums(first, l), 1, 0),
                          (lambda l: queries_out(first, l), 4, 0)])
                for n in range(STEPS):
                    u, k = divmod(n, KT)
                    sum_up(dve, acc0, 0, b, n)
                    if u > 0 and k == 2:
                        normalise(b, u - 1)
                    if u == 2 and k == 7:
                        residual(b, 0)
                if more:
                    center(first + TB, 0)
                    center(first + TB, 1)
                normalise(b, UNITS - 1)
                residual(b, 1)

            center(0, 0)
            center(0, 1)
            batches(dve, body)
            dve.wait_ge(st_done, T)


def hold(eng, g, sem, value):
    eng.wait_ge(sem, value)
    eng.wait_ge(g.consts, 4)


C = 2
NT = (2 * B * S + E * (C * P - 1)) // (C * P)
SLOTS = NT * C * P
PIECE = 1024


def route(nc, g, gate, first_pieces, last_pieces):
    R = 4
    GROUP = T // (E // 2)
    assert len(first_pieces) == 2
    late = [(src, dst, e) for src, dst in last_pieces for e in range(E)]
    EACH = T // len(late)
    NP = 2 * E
    with ExitStack() as st:
        m = Mem(nc, st)
        nm = g.name
        stat_tmp = m.sb(nm("stat_tmp"), [P, 4, T])
        stat_ve = m.sb(nm("stat_ve"), [P, T])
        z = m.sb(nm("z"), [P, 4, D])
        zr = m.sb(nm("zr"), [P, R, D])
        zhl = m.sb(nm("zhl"), [P, R, 2 * D], F16)
        stage = m.sb(nm("stage"), [P, 4, PIECE])
        zTs = m.sb(nm("zTs"), [P, 2, 2, P])
        gw = m.sb(nm("gw"), [P, 2, E])
        upper = m.sb(nm("upper"), [P, P])
        rev = m.sb(nm("rev"), [P, E])
        tiles = m.sb(nm("tiles"), [1, NT, E])
        lg, l2, oh0, oh1, wk, wk2, ex = (m.sb(nm(f"r{i}"), [P, T, E]) for i in range(7))
        m0, m1, r0, e1, sm, den, pf = (m.sb(nm(f"c{i}"), [P, T]) for i in range(7))
        cnt, cumt, base = (m.sb(nm(f"e{i}"), [P, E]) for i in range(3))
        cnti, cntj = (m.sb(nm(f"ei{i}"), [P, E], I32) for i in range(2))
        tef = m.sb(nm("tef"), [1, NT])
        pz = [m.ps(nm(f"pz{i}"), [P, 4, P]) for i in range(2)]
        plg = m.ps(nm("plg"), [P, 512])
        prk = m.ps(nm("prk"), [P, 512])
        ptot = m.ps(nm("ptot"), [P, 512])

        ld, z_done, hi_done, lo_done = m.sem(nm("ld")), m.sem(nm("z_")), m.sem(nm("hi")), m.sem(nm("lo"))
        t_done, ev, lg_done, p_step = m.sem(nm("t")), m.sem(nm("ev")), m.sem(nm("lg")), m.sem(nm("p"))
        v_step, ex_done, rk_done = m.sem(nm("v")), m.sem(nm("ex")), m.sem(nm("rk"))
        w_ld = [m.sem(nm(f"w_ld{i}")) for i in range(4)]
        w_hi, w_lo, zr_done = m.sem(nm("w_hi")), m.sem(nm("w_lo")), m.sem(nm("zr_"))
        summed, roots = g.stat_seen + 7, g.stat_runs
        g.stat_runs += 2
        sc, before = g.moved, g.moved_before
        g.moved_before += 32 * (T // R)
        block = st.enter_context(nc.Block())

        @block.sync
        def _(sp):
            sp.dma_start(gw[:], gate.rearrange("(k p) e -> p k e", p=P)).then_inc(ld, 16)

            def fetch(n, early):
                for r in range(4):
                    src = first_pieces[r % 2][0]
                    if not early:
                        sp.wait_ge(w_lo, 4 * n - 4 + r + 1)
                    sp.dma_start(stage[:, r:r + 1, :].rearrange("p o (k n) -> p (o k) n", k=src(0).shape[1]),
                                 src(2 * n + r // 2)).then_inc(w_ld[r], 16)

            fetch(0, True)
            with sp.Fori(1, E // 2) as n:
                fetch(n, False)
            for j, (src, _, e) in enumerate(late):
                r = j % 4
                sp.wait_ge(w_lo, NP + j - 3)
                sp.dma_start(stage[:, r:r + 1, :].rearrange("p o (k n) -> p (o k) n", k=src(0).shape[1]), src(e)
                             ).then_inc(w_ld[r], 16)

        @block.gpsimd
        def _(pool):
            pool.wait_ge(g.stat_steps, summed)
            for t0, t1 in ((0, 4), (4, T)):
                pool.tensor_tensor(g.rstd[:, t0:t1], stat_ve[:, t0:t1], g.neghalf[:, t0:t1], ALU.pow
                                   ).then_inc(g.stat_roots, 1)
            pool.affine_select(out=upper[:], in_=g.ones[:], compare_op=ALU.is_gt, fill=0.0, base=0,
                               pattern=[[1, P]], channel_multiplier=-1).then_inc(p_step, 1)
            pool.iota(rev[:], pattern=[[-1, E]], base=E, channel_multiplier=0,
                      allow_small_or_imprecise_dtypes=True).then_inc(p_step, 1)
            pool.iota(tiles[:], pattern=[[1, NT], [0, E]], base=0, channel_multiplier=0,
                      allow_small_or_imprecise_dtypes=True).then_inc(p_step, 1)
            pool.wait_ge(v_step, PLACED)
            for t in range(T):
                pool.wait_ge(lo_done, t + 1)
                for k in range(2):
                    pool.indirect_dma_start(g.zs, bass.IndirectOffsetOnAxis(ap=g.pos[:, t, k:k + 1], axis=0),
                                            zhl[:, t % R, :], None).then_inc(sc[t % R], 16)
            for i in range(R):
                pool.wait_ge(sc[i], before + 32 * (T // R))

        @block.tensor
        def _(pe):
            pe.wait_ge(ld, 16)

            def turn(t, i, early):
                pe.wait_ge(z_done, t + 1)
                if not early:
                    pe.wait_ge(ev, t - 1)
                for k in range(2):
                    last = pe.transpose(pz[i % 2][:, k, :], z[:, i, k * P:(k + 1) * P], g.ident[:])
                last.then_inc(t_done, 1)

            def logits(t, i):
                pe.wait_ge(ev, t + 1)
                for k in range(2):
                    last = pe.matmul(plg[:, bass.ds(t * E, E)], zTs[:, i, k, :], gw[:, k, :],
                                     start=(k == 0), stop=(k == 1))
                last.then_inc(lg_done, 1)

            turn(0, 0, True)
            for i in range(1, 4):
                turn(i, i, i == 1)
                logits(i - 1, (i - 1) % 2)
            with pe.Fori(1, T // 4) as n:
                for i in range(4):
                    turn(4 * n + i, i, False)
                    logits(4 * n + i - 1, (i - 1) % 2)
            logits(T - 1, 1)
            pe.wait_ge(p_step, 3)
            pe.wait_ge(v_step, CHOSEN)
            sel = wk[:].rearrange("p t e -> p (t e)")
            pe.matmul(prk[:, 0:T * E], upper[:], sel, start=True, stop=True)
            pe.matmul(ptot[:, 0:T * E], g.ones[:], sel, start=True, stop=True).then_inc(rk_done, 1)

        @block.scalar
        def _(act):
            def copy_out(t, i, early):
                act.wait_ge(t_done, t + 1)
                if not early:
                    act.wait_ge(lg_done, t - 1)
                act.copy(zTs[:, i], pz[i][:, 0:2, :]).then_inc(ev, 1)

            def high(r, loads, dst, e):
                hold(act, g, w_ld[r], 16 * loads)
                act.mul(dst(0, e), stage[:, r:r + 1, :], WS).then_inc(w_hi, 1)

            def group(n, early):
                for r in range(GROUP):
                    copy_out(GROUP * n + r, r % 2, early and r < 2)
                    if r % 2 == 0:
                        high(r // 2, n + 1, first_pieces[r // 2 % 2][1], 2 * n + r // 4)

            group(0, True)
            with act.Fori(1, E // 2) as n:
                group(n, False)
            def scatter_high(t):
                act.wait_ge(zr_done, t + 1)
                if t >= R:
                    act.wait_ge(sc[t % R], before + 32 * (t // R))
                act.copy(zhl[:, t % R, 0:D], zr[:, t % R, :]).then_inc(hi_done, 1)

            for t in range(R):
                scatter_high(t)
            for t in range(T):
                if t == R:
                    act.wait_ge(v_step, SHIFTED)
                    act.activation(ex[:], l2[:], ACT.Exp).then_inc(ex_done, 1)
                    act.activation(e1[:], sm[:], ACT.Exp).then_inc(ex_done, 1)
                if t >= R:
                    scatter_high(t)
                if t % EACH == 0:
                    j = t // EACH
                    high(j % 4, E // 2 + j // 4 + 1, late[j][1], late[j][2])

        def over_e(x):
            return x.rearrange("p (t o) -> p t o", o=1).to_broadcast([P, T, E])

        def over_t(x, n=T, p=P):
            return x.rearrange("p (o e) -> p o e", o=1).to_broadcast([p, n, E])

        @block.vector
        def _(dve):
            def center(t, i, early):
                if not early:
                    dve.wait_ge(t_done, t - 3)
                dve.tensor_scalar(z[:, i:i + 1, :], g.x[:, bass.ds(t, 1), :], g.mean[:, bass.ds(t, 1)],
                                  g.rstd[:, bass.ds(t, 1)], ALU.subtract, ALU.mult).then_inc(z_done, 1)

            def weight_low(r, before, dst, e):
                hold(dve, g, w_hi, before + 1)
                dve.scalar_tensor_tensor(dst(1, e), stage[:, r:r + 1, :], WS, dst(0, e), ALU.mult, ALU.subtract
                                         ).then_inc(w_lo, 1)

            def group(n, final):
                for r in range(0, GROUP, 2):
                    weight_low(r // 2, 4 * n + r // 2, first_pieces[r // 2 % 2][1], 2 * n + r // 4)
                    for i in range(4, 6):
                        if not (final and r + i >= GROUP):
                            center(GROUP * n + r + i, (r + i) % 4, False)

            summarise(dve, g, stat_tmp, stat_ve, False)
            dve.wait_ge(g.stat_roots, roots + 1)
            for t in range(4):
                center(t, t, True)
            dve.wait_ge(g.stat_roots, roots + 2)
            with dve.Fori(0, E // 2 - 1) as n:
                group(n, False)
            group(E // 2 - 1, True)

            def low(t):
                dve.wait_ge(hi_done, t + 1)
                dve.tensor_tensor(zhl[:, t % R, D:], zr[:, t % R, :], zhl[:, t % R, 0:D], ALU.subtract
                                  ).then_inc(lo_done, 1)

            def scatter_rows(t):
                if t >= R:
                    dve.wait_ge(lo_done, t - R + 1)
                dve.tensor_scalar(zr[:, t % R, :], g.x[:, t, :], g.mean[:, t:t + 1], g.rstd[:, t:t + 1],
                                  ALU.subtract, ALU.mult).then_inc(zr_done, 1)
                if t >= 1:
                    low(t - 1)

            def late_piece(t):
                if t % EACH == EACH - 1:
                    j = t // EACH
                    weight_low(j % 4, NP + j, late[j][1], late[j][2])

            for t in range(R):
                scatter_rows(t)
            n = [0]

            def step(ins):
                n[0] += 1
                ins.then_inc(v_step, 1)
                dve.wait_ge(v_step, n[0])

            dve.wait_ge(lg_done, T)
            dve.wait_ge(p_step, 3)
            step(dve.tensor_copy(lg[:].rearrange("p t e -> p (t e)"), plg[:, 0:T * E]))
            for src, top, oh in ((lg, m0, oh0), (l2, m1, oh1)):
                step(dve.tensor_reduce(top[:], src[:], AX.X, ALU.max))
                step(dve.tensor_tensor(wk[:], src[:], over_e(top[:]), ALU.is_equal))
                step(dve.tensor_tensor(wk2[:], wk[:], over_t(rev[:]), ALU.mult))
                step(dve.tensor_reduce(r0[:], wk2[:], AX.X, ALU.max))
                step(dve.tensor_tensor(oh[:], over_t(rev[:]), over_e(r0[:]), ALU.is_equal))
                if src is lg:
                    step(dve.scalar_tensor_tensor(l2[:].rearrange("p t e -> p (t e)"), oh0[:].rearrange("p t e -> p (t e)"),
                                                  MASKED, lg[:].rearrange("p t e -> p (t e)"), ALU.mult, ALU.add))
            step(dve.tensor_tensor(wk[:], oh0[:], oh1[:], ALU.add))
            assert n[0] == CHOSEN
            dve.wait_ge(rk_done, 1)
            tot = ptot[:, 0:T * E].rearrange("p (t e) -> p t e", e=E)
            step(dve.tensor_copy(ex[:], tot))
            step(dve.tensor_scalar(wk2[:], ex[:], 0.0, 1.0, ALU.mult, ALU.add))
            for e in range(E):
                last = dve.tensor_tensor_scan(l2[:, :, e], wk2[:, :, e], ex[:, :, e], 0.0, ALU.mult, ALU.add)
                n[0] += 1
                last.then_inc(v_step, 1)
            dve.wait_ge(v_step, n[0])
            step(dve.tensor_scalar(cnti[:], l2[:, T - 1, :], float(C * P - 1), None, ALU.add))
            step(dve.tensor_scalar(cntj[:], cnti[:], (C * P).bit_length() - 1, None, ALU.logical_shift_right))
            step(dve.tensor_copy(cnt[:], cntj[:]))
            step(dve.tensor_tensor_scan(cumt[:], wk2[:, 0, :], cnt[:], 0.0, ALU.mult, ALU.add))
            step(dve.tensor_tensor(base[:], cumt[:], cnt[:], ALU.subtract))
            step(dve.tensor_scalar(base[:], base[:], float(C * P), None, ALU.mult))
            step(dve.tensor_tensor(l2[:], l2[:], ex[:], ALU.subtract))
            step(dve.tensor_tensor(l2[:], l2[:], prk[:, 0:T * E].rearrange("p (t e) -> p t e", e=E), ALU.add))
            step(dve.tensor_tensor(l2[:], l2[:], over_t(base[:]), ALU.add))
            for k, oh in enumerate((oh0, oh1)):
                step(dve.tensor_tensor(wk2[:], oh[:], l2[:], ALU.mult))
                step(dve.tensor_reduce(pf[:], wk2[:], AX.X, ALU.add))
                step(dve.tensor_copy(g.pos[:, :, k], pf[:]))
            assert n[0] == PLACED, n[0]
            step(dve.tensor_tensor(l2[:], lg[:], over_e(m0[:]), ALU.subtract))
            step(dve.tensor_tensor(sm[:], m1[:], m0[:], ALU.subtract))
            assert n[0] == SHIFTED, n[0]
            dve.wait_ge(ex_done, 2)
            step(dve.tensor_reduce(den[:], ex[:], AX.X, ALU.add))
            step(dve.tensor_scalar(den[:], den[:], 1e-9, 1.0, ALU.mult, ALU.add))
            step(dve.tensor_tensor(den[:], den[:], e1[:], ALU.add))
            step(dve.reciprocal(g.wt[:, 0, :], den[:]))
            step(dve.tensor_tensor(g.wt[:, 1, :], g.wt[:, 0, :], e1[:], ALU.mult))
            step(dve.tensor_tensor(tiles[:], tiles[:], over_t(cumt[0:1, :], NT, 1), ALU.is_ge))
            step(dve.tensor_reduce(tef[:], tiles[:], AX.X, ALU.add))
            step(dve.tensor_scalar(tef[:], tef[:], float(E - 1), None, ALU.min))
            step(dve.tensor_copy(g.expert[:], tef[:]))
            for t in range(T):
                if t >= R:
                    scatter_rows(t)
                late_piece(t)
            low(T - 1)
            dve.wait_ge(lo_done, T)


CHOSEN = 13
PLACED = 38
SHIFTED = 40


def experts(nc, g, a, layer):
    F = F0 if layer == 0 else F1
    NF = F // P
    NU = 8
    Q = 4
    HQ = NF // 2
    TAIL = 2 * ((NT - 2) // 2)
    with ExitStack() as st:
        m = Mem(nc, st)
        nm = g.name
        zt = m.sb(nm("zt"), [P, 2, C, 2 * D], F16)
        zTs = m.sb(nm("zTt"), [P, 2, 4, C * P], F16)
        h32 = m.sb(nm("h32"), [P, 2, 2, C * P])
        gt = m.sb(nm("g32"), [P, 2, 2, C * P]) if layer else None
        hh = m.sb(nm("hh"), [P, 2, NF, C * P], F16)
        hl = m.sb(nm("hl"), [P, 2, NF, C * P], F16)
        ysb = m.sb(nm("ysb"), [P, 2, C, D])
        if layer == 0:
            b1 = m.sb(nm("b1"), [P, E, NF])
            b2 = m.sb(nm("b2"), [P, E, D])
        pz = [m.ps(nm(f"pzt{i}"), [P, 4, C * P], F16) for i in range(2)]
        ph = m.ps(nm("ph"), [P, Q, 2, C * P])
        py = [m.ps(nm(f"pyt{i}"), [P, 2, D]) for i in range(C)]

        ld = [m.sem(nm(f"zld{i}")) for i in range(2)]
        sto = [m.sem(nm(f"yst{i}")) for i in range(2)]
        b1_ld, b2_ld, t_done, zev = m.sem(nm("b1_ld")), m.sem(nm("b2_ld")), m.sem(nm("tt")), m.sem(nm("zev"))
        up_done, act_done, g_done = m.sem(nm("up")), m.sem(nm("act")), m.sem(nm("gd"))
        hi_done, lo_done, dn_done, yev = m.sem(nm("hid")), m.sem(nm("lod")), m.sem(nm("dn")), m.sem(nm("yev"))
        block = st.enter_context(nc.Block())
        up_w, down_w = g.up_w, g.down_w

        def expert_of(eng, i):
            return eng.value_load(g.expert[0:1, bass.ds(i, 1)], min_val=0, max_val=E - 1)

        @block.sync
        def _(sp):
            zs = g.zs.rearrange("(i c p) d -> p i c d", p=P, c=C)
            ys = g.ys.rearrange("(i c p) d -> p i c d", p=P, c=C)

            def load(i, s, early):
                if not early:
                    sp.wait_ge(t_done, i - 1)
                sp.dma_start(zt[:, s:s + 1], zs[:, bass.ds(i, 1)]).then_inc(ld[s], 16)

            load(0, 0, True)
            if layer == 0:
                sp.dma_start(b1[:], a["b1"]).then_inc(b1_ld, 16)
            load(1, 1, True)
            if layer == 0:
                sp.dma_start(b2[:], a["b2"].partition_broadcast(P)).then_inc(b2_ld, 16)
            for i in range(2, 4):
                load(i, i % 2, False)
            with sp.Fori(2, NT // 2) as n:
                for s in range(2):
                    load(2 * n + s, s, False)
                    sp.wait_ge(yev, C * (2 * n + s - 3))
                    sp.dma_start(ys[:, bass.ds(2 * n + s - 4, 1)], ysb[:, s:s + 1]).then_inc(sto[s], 16)
            for i in range(2 * (NT // 2), NT):
                load(i, i % 2, False)
            for i in range(2 * (NT // 2) - 4, NT):
                sp.wait_ge(yev, C * (i + 1))
                sp.dma_start(ys[:, i], ysb[:, i % 2]).then_inc(sto[i % 2], 16)
            for i in range(2):
                sp.wait_ge(sto[i], 16 * ((NT - i + 1) // 2))

        @block.tensor
        def _(pe):
            def turn(i, s, half, early):
                pe.wait_ge(ld[s], 16 * half + 16)
                if not early:
                    pe.wait_ge(zev, i - 1)
                for c in range(C):
                    for k in range(4):
                        last = pe.transpose(pz[s][:, k, c * P:(c + 1) * P], zt[:, s, c, k * P:(k + 1) * P], g.ident16[:])
                last.then_inc(t_done, 1)

            def up(i, s, e, early):
                hold(pe, g, zev, i + 1)
                for q in range(Q):
                    if not early:
                        if layer == 0:
                            hold(pe, g, act_done, Q * i - Q + q + 1)
                        else:
                            hold(pe, g, act_done if q < HQ else g_done, HQ * i - HQ + q % HQ + 1)
                    for f in range(2):
                        n = 0
                        for k in range(2):
                            for wp, zp in ((0, 0), (0, 1), (1, 0)):
                                last = pe.matmul(ph[:, q, f, :], up_w(wp, e, k, 2 * q + f), zTs[:, s, 2 * zp + k, :],
                                                 start=(n == 0), stop=(n == 5))
                                n += 1
                    last.then_inc(up_done, 1)

            def down(i, s, e, early):
                pe.wait_ge(hi_done, HQ * i + HQ)
                hold(pe, g, lo_done, HQ * i + HQ)
                for c in range(C):
                    if not early:
                        hold(pe, g, yev, C * i - C + c + 1)
                    n = 0
                    for f in range(NF):
                        for wp, hp in ((0, hh), (0, hl), (1, hh)):
                            last = pe.matmul(py[c][:, 0, :], hp[:, s, f, c * P:(c + 1) * P], down_w(wp, e, f),
                                             start=(n == 0), stop=(n == 3 * NF - 1))
                            n += 1
                    last.then_inc(dn_done, 1)

            e = [expert_of(pe, i) for i in range(3)]
            turn(0, 0, 0, True)
            turn(1, 1, 0, True)
            up(0, 0, e[0], True)
            up(1, 1, e[1], False)
            turn(2, 0, 1, False)
            down(0, 0, e[0], True)
            up(2, 0, e[2], False)
            turn(3, 1, 1, False)
            down(1, 1, e[1], False)
            with pe.Fori(1, TAIL // 2) as n:
                _, e = nc.values_load_multi_w_load_instructions(g.expert[0:1, bass.ds(2 * n, 3)], engines=[mybir.EngineType.PE],
                                                                min_val=0, max_val=E - 1)
                for s in range(2):
                    i = 2 * n + s
                    up(i + 1, 1 - s, e[s + 1], False)
                    turn(i + 2, s, n + 1, False)
                    down(i, s, e[s], False)
            e = [expert_of(pe, i) for i in range(TAIL, NT)]
            for i in range(TAIL, NT):
                if i + 1 < NT:
                    up(i + 1, (i + 1) % 2, e[i + 1 - TAIL], False)
                if i + 2 < NT:
                    turn(i + 2, i % 2, i // 2 + 1, False)
                down(i, i % 2, e[i - TAIL], False)

        def steps(eng, body):
            body(0, 0, True)
            body(1, 1, True)
            with eng.Fori(1, NT // 2) as n:
                body(2 * n, 0, False)
                body(2 * n + 1, 1, False)
            for i in range(2 * (NT // 2), NT):
                body(i, i % 2, False)

        @block.scalar
        def _(act):
            if layer == 0:
                act.wait_ge(b1_ld, 16)

            def body(i, s, early):
                if layer == 0:
                    e = expert_of(act, i)

                def units(q):
                    if not (early and s == 0 and q < 2):
                        if layer == 0:
                            act.wait_ge(lo_done, HQ * i + q - 1)
                        else:
                            act.wait_ge(g_done, HQ * i + q - 1)
                    hold(act, g, up_done, Q * i + q + 1)
                    if layer == 0:
                        for f in range(2):
                            last = act.activation(h32[:, q % 2, f, :], ph[:, q, f, :], ACT.Relu,
                                                  bias=b1[:, bass.ds(e, 1), 2 * q + f], scale=1.0 / WS)
                    else:
                        last = act.activation(h32[:, q], ph[:, q], ACT.Silu, scale=1.0 / WS)
                    last.then_inc(act_done, 1)

                def high(q):
                    if layer == 0:
                        act.wait_ge(act_done, HQ * i + q + 1)
                    else:
                        act.wait_ge(g_done, HQ * i + q + 1)
                    if not early and q == 0:
                        act.wait_ge(dn_done, C * i - C)
                    src = gt if layer else h32
                    act.copy(hh[:, s, 2 * q:2 * q + 2, :], src[:, q % 2]).then_inc(hi_done, 1)

                units(0)
                for q in range(1, HQ):
                    units(q)
                    high(q - 1)
                high(HQ - 1)

            steps(act, body)

        @block.vector
        def _(dve):
            def evacuate(i, s, early):
                dve.wait_ge(t_done, i + 1)
                if not early:
                    dve.wait_ge(up_done, Q * i - Q)
                dve.tensor_copy(zTs[:, s], pz[s][:]).then_inc(zev, 1)

            def hidden(i, s, early):
                if layer:
                    for q in range(HQ):
                        if not (early and s == 0):
                            dve.wait_ge(lo_done, HQ * i + q - 1)
                        dve.wait_ge(act_done, HQ * i + q + 1)
                        dve.wait_ge(up_done, Q * i + HQ + q + 1)
                        dve.scalar_tensor_tensor(gt[:, q].rearrange("p f t -> p (f t)"),
                                                 ph[:, HQ + q].rearrange("p f t -> p (f t)"), 1.0 / WS,
                                                 h32[:, q].rearrange("p f t -> p (f t)"), ALU.mult, ALU.mult
                                                 ).then_inc(g_done, 1)
                if not early:
                    dve.wait_ge(dn_done, C * i - C)
                src = gt if layer else h32
                for q in range(HQ):
                    dve.wait_ge(hi_done, HQ * i + q + 1)
                    dve.tensor_tensor(hl[:, s, 2 * q:2 * q + 2, :], src[:, q % 2], hh[:, s, 2 * q:2 * q + 2, :],
                                      ALU.subtract).then_inc(lo_done, 1)

            def result(i, s, half, early):
                if layer == 0:
                    if early:
                        dve.wait_ge(b2_ld, 16)
                    e = expert_of(dve, i)
                if not early:
                    dve.wait_ge(sto[s], 16 * half)
                for c in range(C):
                    if layer == 0:
                        hold(dve, g, dn_done, C * i + c + 1)
                        dve.scalar_tensor_tensor(ysb[:, s, c:c + 1, :], py[c][:, 0:1, :], 1.0 / WS,
                                                 b2[:, bass.ds(e, 1), :], ALU.mult, ALU.add).then_inc(yev, 1)
                    else:
                        dve.wait_ge(dn_done, C * i + c + 1)
                        dve.tensor_scalar(ysb[:, s, c, :], py[c][:, 0, :], 1.0 / WS, None, ALU.mult).then_inc(yev, 1)

            evacuate(0, 0, True)
            evacuate(1, 1, True)
            hidden(0, 0, True)
            hidden(1, 1, True)
            evacuate(2, 0, False)
            result(0, 0, 0, True)
            hidden(2, 0, False)
            evacuate(3, 1, False)
            result(1, 1, 0, True)
            with dve.Fori(1, TAIL // 2) as n:
                for s in range(2):
                    i = 2 * n + s
                    hidden(i + 1, 1 - s, False)
                    evacuate(i + 2, s, False)
                    result(i, s, n, False)
            for i in range(TAIL, NT):
                if i + 1 < NT:
                    hidden(i + 1, (i + 1) % 2, False)
                if i + 2 < NT:
                    evacuate(i + 2, i % 2, False)
                result(i, i % 2, i // 2, False)
            dve.wait_ge(yev, C * NT)


def combine(nc, g, out):
    with ExitStack() as st:
        m = Mem(nc, st)
        nm = g.name
        R = 4
        rows = m.sb(nm("rows"), [P, R, 2, D])
        got, before = g.moved, g.moved_before
        added = m.sem(nm("added"))
        block = st.enter_context(nc.Block())

        @block.sync
        def _(sp):
            G = 4
            for i in range(T // G):
                sp.wait_ge(added, 2 * G * (i + 1))
                sp.dma_start(out[i * G * P:(i + 1) * G * P, :].rearrange("(t p) d -> p t d", p=P),
                             g.x[:, i * G:(i + 1) * G, :]).then_inc(g.x_in, 16)
            sp.wait_ge(g.x_in, 16 * (B + T // G))

        @block.gpsimd
        def _(pool):
            for t in range(T):
                if t >= R:
                    pool.wait_ge(added, 2 * (t - R) + 2)
                for k in range(2):
                    pool.indirect_dma_start(rows[:, t % R, k, :], None, g.ys,
                                            bass.IndirectOffsetOnAxis(ap=g.pos[:, t, k:k + 1], axis=0)
                                            ).then_inc(got[t % R], 16)

        @block.vector
        def _(dve):
            for t in range(T):
                dve.wait_ge(got[t % R], before + 32 * (t // R + 1))
                for k in range(2):
                    if k:
                        dve.wait_ge(added, 2 * t + 1)
                    dve.scalar_tensor_tensor(g.x[:, t, :], rows[:, t % R, k, :], g.wt[:, k, t:t + 1], g.x[:, t, :],
                                             ALU.mult, ALU.add).then_inc(added, 1)
            dve.wait_ge(added, 2 * T)


def attention1_context(nc, g, a, at):
    with ExitStack() as st:
        m = Mem(nc, st)
        wk = m.sb("wk1", [P, 2, D])
        wv = m.sb("wv1", [P, 2, D])
        mask8 = m.sb("mask8", [P, B, M], U8)
        mask = m.sb("mask1f", [P, B, M])
        own = m.sb("own", [P, 8])
        own2 = m.sb("own2", [P, 8])
        kT = m.sb("kT1", [P, 2, B, M])
        pk = m.ps("pk1", [P, 2, 512])
        pv = m.ps("pv1", [M, B, 512])
        ld, pool_done, mm_done, v_step, v_ev = m.sem("k_ld"), m.sem("k_pool"), m.sem("k_mm"), m.sem("k_v"), m.sem("k_vev")
        kbd_done, wo_ld = m.sem("k_bd"), m.sem("k_wo")
        block = st.enter_context(nc.Block())

        @block.sync
        def _(sp):
            for w, src in ((wk, a["Wk1"]), (wv, a["Wv1"])):
                sp.dma_start(w[:, 0, :], src[0:P, :]).then_inc(ld, 16)
                sp.dma_start(w[0:DC - P, 1, :], src[P:DC, :]).then_inc(ld, 16)
            sp.dma_start(mask8[:], a["mask1"].partition_broadcast(P)).then_inc(ld, 16)
            sp.dma_start(at.wq[:], a["Wq1"].rearrange("(k p) n -> p k n", p=P)).then_inc(ld, 16)
            sp.dma_start(at.wo[:], a["Wo1"].rearrange("(k p) n -> p k n", p=P)).then_inc(wo_ld, 16)
            sp.wait_ge(wo_ld, 16)

        @block.gpsimd
        def _(pool):
            pool.memset(at.v[:], 0.0).then_inc(pool_done, 1)
            pool.affine_select(out=own2[:], in_=g.ones[:, 0:8], compare_op=ALU.is_ge, fill=0.0, base=0,
                               pattern=[[-HD1, 8]], channel_multiplier=1).then_inc(pool_done, 1)
            pool.wait_ge(pool_done, 2)
            pool.affine_select(out=own[:], in_=own2[:], compare_op=ALU.is_ge, fill=0.0, base=HD1 - 1,
                               pattern=[[HD1, 8]], channel_multiplier=-1).then_inc(pool_done, 1)

        @block.tensor
        def _(pe):
            pe.wait_ge(ld, 16 * 6)
            for hg in range(2):
                for k, r in ((0, P), (1, DC - P)):
                    pe.matmul(pk[:, hg, 0:B * M], wk[0:r, k, hg * P:(hg + 1) * P], g.ctxT[0:r, k, :, 0:M],
                              start=(k == 0), stop=(k == 1))
            for b in range(B):
                for k, r in ((0, P), (1, DC - P)):
                    last = pe.matmul(pv[:, b, 0:D], g.ctxT[0:r, k, b, 0:M], wv[0:r, k, :],
                                     start=(k == 0), stop=(k == 1))
            last.then_inc(mm_done, 1)

        @block.scalar
        def _(act):
            act.wait_ge(mm_done, 1)
            act.wait_ge(pool_done, 1)
            for b in range(B):
                own_v = pv[:, b, 0:D].rearrange("p (h o d) -> p h o d", o=2, d=HD1)
                for o in range(2):
                    act.copy(at.v[:, b, o:H1:2, o * HD1:(o + 1) * HD1], own_v[:, :, o, :]).then_inc(v_ev, 1)
            act.wait_ge(v_ev, 2 * B)

        @block.vector
        def _(dve):
            dve.wait_ge(ld, 16 * 6)
            dve.tensor_copy(mask[:], mask8[:]).then_inc(v_step, 1)
            dve.wait_ge(v_step, 1)
            dve.tensor_scalar(at.bias[:], mask[:], 1.0, -MASKED, ALU.subtract, ALU.mult).then_inc(v_step, 1)
            dve.wait_ge(mm_done, 1)
            for hg in range(2):
                dve.scalar_tensor_tensor(kT[:, hg].rearrange("p b m -> p (b m)"), pk[:, hg, 0:B * M], SCALE1,
                                         mask[:].rearrange("p b m -> p (b m)"), ALU.mult, ALU.mult).then_inc(v_step, 1)
            dve.wait_ge(v_step, 4)
            dve.wait_ge(pool_done, 3)
            for b in range(B):
                for hg in range(2):
                    dve.tensor_tensor(at.k[:, b, hg], kT[:, hg, b:b + 1, :].to_broadcast([P, 8, M]),
                                      own[:].rearrange("p (j o) -> p j o", o=1).to_broadcast([P, 8, M]),
                                      ALU.mult).then_inc(kbd_done, 1)
            dve.wait_ge(kbd_done, 2 * B)


def attention1(nc, g, at):
    R = 4
    LEAD = 5
    LAG = 4
    SLOT = 4
    C = 4
    with ExitStack() as st:
        m = Mem(nc, st)
        z = m.sb("z1", [P, 2, D])
        zT = m.sb("zT1", [P, 2, P])
        qT = m.sb("qT1", [P, 2, P])
        s = m.sb("s1", [P, SLOT, H1, M])
        mx = m.sb("mx1", [P, SLOT, H1])
        sm = m.sb("sm1", [P, SLOT, H1])
        rs = m.sb("rs1", [P, SLOT, H1])
        pT = m.sb("pT1", [M, 2, H1, P])
        oT = m.sb("oT1", [P, 2, P])
        v = m.sb("vcur", [M, H1, 32])
        rows = m.sb("rows1", [P, R, 2, D])
        xs = m.sb("xs1", [P, TB, D])
        idx = m.sb("idx1", [P, R, 2], U32)
        stats = m.sb("stats1", [P, R, 6])
        mv = m.sb("mv1", [P, R, 2])
        ve = m.sb("ve1", [P, R])
        rstd = m.sb("rstd1", [P, R])
        psc = m.ps("psc1", [P, C, 512])
        pt = m.ps("pt1", [M, 2, 4, P])
        front = m.ps("front1", [P, 4, P])
        back = m.ps("back1", [P, 512])

        z_done, t_done, zT_ev, q_done, q_ev = (m.sem("b_" + n) for n in ("z", "t", "zTev", "q", "qev"))
        s_done, add_done, max_done, sub_done, e_done = (m.sem("b_" + n) for n in ("s", "add", "max", "sub", "e"))
        sum_done, r_done, n_done = (m.sem("b_" + n) for n in ("sum", "r", "n"))
        pt_done, pt_ev, v_done, o_done, o_ev, y_done, x_done, st_done = (
            m.sem("b_" + n) for n in ("pt", "ptev", "v", "o", "oev", "y", "x", "st"))
        idx_done, comb, agg_done, ve_done, root_done = (m.sem("b_" + n) for n in ("idx", "comb", "agg", "ve", "root"))
        got, before = g.moved, g.moved_before
        g.moved_before += 32 * (T // R)
        block = st.enter_context(nc.Block())

        def steps(eng, body):
            head = LAG + 1
            for c in range(-LEAD, head):
                body(0, 0, c, lambda x: 0 <= x)
            with eng.Fori(0, B - 2) as n:
                for r in range(TB):
                    body(n * TB, n, head + r, lambda x: True)
            for c in range(head, 2 * TB + LAG + 2):
                body((B - 2) * TB, B - 2, c, lambda x: x < 2 * TB)

        @block.tensor
        def _(pe):
            def body(base, b0, c, live):
                if live(c):
                    t = base + c
                    if c > 0:
                        pe.wait_ge(q_ev, t)
                    pe.wait_ge(z_done, t + 1)
                    for k in range(2):
                        last = pe.transpose(front[:, k, :], z[:, c % 2, k * P:(k + 1) * P], g.ident[:])
                    last.then_inc(t_done, 1)
                d = c - LAG
                if live(d):
                    t = base + d
                    pe.wait_ge(n_done, t + 1)
                    for n in range(4):
                        if d > 0 or n >= 2:
                            pe.wait_ge(pt_ev, 4 * t + n - 1)
                        for h in range(4 * n, 4 * n + 4):
                            last = pe.transpose(pt[:, n % 2, h % 4, :], s[:, d % SLOT, h, :], g.ident[:])
                        last.then_inc(pt_done, 1)
                if live(c):
                    t = base + c
                    pe.wait_ge(zT_ev, t + 1)
                    for hg in range(2):
                        for k in range(2):
                            last = pe.matmul(front[:, 2 + hg, :], at.wq[:, k, hg * P:(hg + 1) * P], zT[:, k, :],
                                             start=(k == 0), stop=(k == 1))
                    last.then_inc(q_done, 1)
                if live(d):
                    t = base + d
                    if d % TB == 0:
                        pe.wait_ge(v_done, b0 + d // TB + 1)
                    if d > 0:
                        pe.wait_ge(x_done, t)
                    pe.wait_ge(pt_ev, 4 * t + 4)
                    for hg in range(2):
                        for o in range(2):
                            for r in range(4):
                                h = 8 * hg + 2 * r + o
                                last = pe.matmul(back[32 * r:32 * r + 32, hg * P:(hg + 1) * P], v[:, h, :],
                                                 pT[:, d % 2, h, :], start=(o == 0), stop=(o == 1))
                    last.then_inc(o_done, 1)
                if live(c):
                    t = base + c
                    if c > 0:
                        pe.wait_ge(add_done, t)
                    pe.wait_ge(q_ev, t + 1)
                    for n in range(C):
                        last = pe.matmul(psc[:, n, 0:4 * M], qT[:, n // 2, :],
                                         at.k[:, bass.ds(b0 + c // TB, 1), n // 2, 4 * (n % 2):4 * (n % 2) + 4, :]
                                         .rearrange("p o j m -> p (o j m)"), start=True, stop=True)
                    last.then_inc(s_done, 1)
                if live(d):
                    pe.wait_ge(o_ev, base + d + 1)
                    for hg in range(2):
                        last = pe.matmul(back[:, 0:D], oT[:, hg, :], at.wo[:, hg, :], start=(hg == 0), stop=(hg == 1))
                    last.then_inc(y_done, 1)

            steps(pe, body)

        @block.scalar
        def _(act):
            def body(base, b0, c, live):
                if live(c):
                    t = base + c
                    act.wait_ge(t_done, t + 1)
                    act.copy(zT[:], front[:, 0:2, :]).then_inc(zT_ev, 1)
                d = c - LAG
                if live(d):
                    t = base + d
                    for n in range(4):
                        act.wait_ge(pt_done, 4 * t + n + 1)
                        act.copy(pT[:, d % 2, 4 * n:4 * n + 4, :], pt[:, n % 2]).then_inc(pt_ev, 1)
                if live(c):
                    t = base + c
                    act.wait_ge(q_done, t + 1)
                    act.copy(qT[:], front[:, 2:4, :]).then_inc(q_ev, 1)
                if live(d):
                    act.wait_ge(o_done, base + d + 1)
                    act.copy(oT[:].rearrange("p n t -> p (n t)"), back[:, 0:2 * P]).then_inc(o_ev, 1)
                if live(d + 1) and (d + 1) % TB == 0:
                    act.copy(v[:].rearrange("p (o h) d -> p o h d", o=1), at.v[:, bass.ds(b0 + (d + 1) // TB, 1)]
                             ).then_inc(v_done, 1)
                if live(c - 2):
                    i, t = (c - 2) % SLOT, base + c - 2
                    act.wait_ge(sub_done, t + 1)
                    act.activation(s[:, i], s[:, i], ACT.Exp).then_inc(e_done, 1)

            steps(act, body)

        def per_key(x):
            return x.rearrange("p (h o) -> p h o", o=1).to_broadcast([P, H1, M])

        @block.gpsimd
        def _(pool):
            def gather(c, known):
                i = c % R
                if not known:
                    pool.wait_ge(idx_done, c + 1)
                    if c >= R:
                        pool.wait_ge(comb, 3 * (c - R) + 2)
                for k in range(2):
                    pool.indirect_dma_start(rows[:, i, k, :], None, g.ys,
                                            bass.IndirectOffsetOnAxis(ap=idx[:, i, k:k + 1], axis=0)
                                            ).then_inc(got[i], 16)

            def body(base, b0, c, live):
                if live(c + 1):
                    i = (c + 1) % R
                    pool.wait_ge(ve_done, base + c + 2)
                    pool.tensor_tensor(rstd[:, i:i + 1], ve[:, i:i + 1], g.neghalf[:, 0:1], ALU.pow).then_inc(root_done, 1)
                d = c - LAG
                if live(c - 3):
                    i = (c - 3) % SLOT
                    pool.wait_ge(r_done, base + c - 2)
                    pool.tensor_tensor(s[:, i], s[:, i], per_key(rs[:, i, :]), ALU.mult).then_inc(n_done, 1)
                if live(c - 1):
                    i = (c - 1) % SLOT
                    pool.wait_ge(max_done, base + c)
                    pool.tensor_tensor(s[:, i], s[:, i], per_key(mx[:, i, :]), ALU.subtract).then_inc(sub_done, 1)
                if live(c + LEAD):
                    gather(c + LEAD, live(c - 3))

            steps(pool, body)

        @block.vector
        def _(dve):
            def center(base, c):
                t = base + c
                if c > 1:
                    dve.wait_ge(t_done, t - 1)
                i = c % R
                dve.wait_ge(root_done, t + 1)
                dve.tensor_scalar(z[:, c % 2, :], xs[:, c % TB, :], mv[:, i, 0:1],
                                  rstd[:, i:i + 1], ALU.subtract, ALU.mult).then_inc(z_done, 1)

            def add_first(base, b0, c):
                t, i = base + c, c % R
                dve.wait_ge(got[i], before + 32 * (TB // R * b0 + c // R + 1))
                dve.scalar_tensor_tensor(xs[:, c % TB:c % TB + 1, :], rows[:, i, 0:1, :], g.wt[:, 0, bass.ds(t, 1)],
                                         g.x[:, bass.ds(t, 1), :], ALU.mult, ALU.add).then_inc(comb, 1)

            def add_second(base, c):
                t, i = base + c, c % R
                dve.wait_ge(comb, 3 * t + 1)
                dve.scalar_tensor_tensor(xs[:, c % TB, :], rows[:, i, 1, :], g.wt[:, 1, bass.ds(t, 1)],
                                         xs[:, c % TB, :], ALU.mult, ALU.add).then_inc(comb, 1)

            def variance(base, c):
                t, i = base + c, c % R
                dve.bn_aggr(mv[:, i, :], stats[:, i, :]).then_inc(agg_done, 1)

            def with_eps(base, c):
                t, i = base + c, c % R
                dve.wait_ge(agg_done, t + 1)
                dve.tensor_scalar(ve[:, i:i + 1], mv[:, i, 1:2], LN_EPS, None, ALU.add).then_inc(ve_done, 1)

            def tile_stats(base, c):
                dve.wait_ge(comb, 3 * (base + c) + 2)
                dve.bn_stats(stats[:, c % R, :], xs[:, c % TB, :]).then_inc(comb, 1)

            def body(base, b0, c, live):
                if live(c + LEAD):
                    t, i = base + c + LEAD, (c + LEAD) % R
                    dve.tensor_copy(idx[:, i:i + 1, :], g.pos[:, bass.ds(t, 1), :]).then_inc(idx_done, 1)
                if live(c - 1):
                    i, t = (c - 1) % SLOT, base + c - 1
                    if c - 1 >= SLOT:
                        dve.wait_ge(pt_done, 4 * (t - SLOT) + 4)
                    dve.wait_ge(s_done, t + 1)
                    dve.tensor_tensor(s[:, i].rearrange("p (n j) m -> p n j m", n=C),
                                      psc[:, :, 0:4 * M].rearrange("p n (j m) -> p n j m", m=M),
                                      at.bias[:, bass.ds(b0 + (c - 1) // TB, 1), :].rearrange("p (n o) m -> p n o m", n=1)
                                      .to_broadcast([P, C, 4, M]), ALU.add).then_inc(add_done, 1)
                d = c - LAG - 1
                if live(d):
                    t = base + d
                    dve.wait_ge(y_done, t + 1)
                    xt = g.x[:, bass.ds(t, 1), :]
                    dve.tensor_tensor(xt, xs[:, d % TB:d % TB + 1, :], back[:, 0:D].rearrange("p (o d) -> p o d", o=1), ALU.add).then_inc(x_done, 1)
                    dve.wait_ge(x_done, t + 1)
                    dve.bn_stats(g.stats[:, bass.ds(t, 1), :], xt).then_inc(st_done, 1)
                if live(c - 3):
                    i, t = (c - 3) % SLOT, base + c - 3
                    dve.wait_ge(e_done, t + 1)
                    dve.tensor_reduce(sm[:, i, :], s[:, i], AX.X, ALU.add).then_inc(sum_done, 1)
                if live(c - 1):
                    i, t = (c - 1) % SLOT, base + c - 1
                    dve.wait_ge(add_done, t + 1)
                    dve.tensor_reduce(mx[:, i, :], s[:, i], AX.X, ALU.max).then_inc(max_done, 1)
                if live(c - 3):
                    i, t = (c - 3) % SLOT, base + c - 3
                    dve.wait_ge(sum_done, t + 1)
                    dve.reciprocal(rs[:, i, :], sm[:, i, :]).then_inc(r_done, 1)
                if live(c + 3):
                    add_first(base, b0, c + 3)
                if live(c + 1):
                    center(base, c + 1)
                if live(c + 3):
                    add_second(base, c + 3)
                if live(c + 2):
                    if not live(c + 3):
                        dve.wait_ge(comb, 3 * (base + c + 2) + 3)
                    variance(base, c + 2)
                if live(c + 3):
                    tile_stats(base, c + 3)
                if live(c + 2):
                    with_eps(base, c + 2)
            steps(dve, body)
            dve.wait_ge(st_done, T)


def host_arrays(i):
    import numpy as np

    n = {k: np.asarray(v) for k, v in i.items()}
    c = np.ascontiguousarray
    return {
        "x": n["x"].reshape(B * S, D),
        "ctx": n["ctx_768"],
        "mask0": n["mask_BxS2_bk0"],
        "mask1": n["mask_BxS2_bf1"],
        "ln_x_g": n["L0_xattn_ln_x_g"], "ln_x_b": n["L0_xattn_ln_x_b"],
        "ln_l_g": n["L0_xattn_ln_l_g"], "ln_l_b": n["L0_xattn_ln_l_b"],
        "qn_g": n["L0_xattn_qn_g"], "kn_g": n["L0_xattn_kn_g"],
        "WqkvT": c(np.concatenate([n["L0_xattn_Wq"].T, n["L0_xattn_Wlkv"].T], axis=1)),
        "WkvT": c(n["L0_xattn_Wkv"].T),
        "WoT": c(n["L0_xattn_Wo"].T), "bo": n["L0_xattn_bo"],
        "routerT": c(n["L0_ffn_router_w"].T),
        "w1T": c(n["L0_ffn_w1"].transpose(0, 2, 1)), "b1": c(n["L0_ffn_b1"].reshape(E, F0 // P, P).transpose(2, 0, 1)),
        "w2T": c(n["L0_ffn_w2"].transpose(0, 2, 1)), "b2": n["L0_ffn_b2"],
        "Wq1": n["L1_xattn_Wq"], "Wk1": n["L1_xattn_Wk"], "Wv1": n["L1_xattn_Wv"], "Wo1": n["L1_xattn_Wo"],
        "gate": n["L1_ffn_gate_w"],
        "u1": n["L1_ffn_w1"], "u2": n["L1_ffn_w2"], "u3": n["L1_ffn_w3"],
    }


def program(nc, a, out):
    g = Names()
    g.phase = "e0_"
    g.name = lambda x: g.phase + x
    g.zs = nc.dram_tensor("sorted_tokens", [SLOTS, 2 * D], F16, kind="Internal").ap()
    g.ys = nc.dram_tensor("sorted_results", [SLOTS, D], F32, kind="Internal").ap()
    with ExitStack() as whole:
        mem = Mem(nc, whole)
        setup(nc, mem, g)
        with ExitStack() as st:
            m = Mem(nc, st)
            g.kctx = m.sb("kctx", [P, 2, B * H0, MP], F16)
            g.vctx = m.sb("vctx", [M, B, D])
            g.zeros = m.sb("zeros", [P, 2 * D], F16)
            g.wqkv = m.sb("wqkv", [P, 2, 3 * D])
            g.gl = m.sb("gl", [P, 2])
            g.bl = m.sb("bl", [P, 2])
            g.bo = m.sb("bo_row", [P, D])
            g.wo = m.sb("wo0", [P, 2, D])
            attention0_inputs(nc, g, a)
            attention0(nc, g)
        wA = mem.sb("weights_a", [P, 2, E, 2 * F0], F16)

        def blocks(w, offset):
            return lambda part, e: w[:, part, bass.ds(e, 1), offset:offset + PIECE]

        def block_of(w, part, e, offset, n):
            return w[:, part, bass.ds(e, 1), offset:offset + n].rearrange("p o n -> p (o n)")

        def rows_of(w, k0, k):
            return lambda e: w[bass.ds(e, 1), k0 * P:(k0 + k) * P, :].rearrange("o (k p) f -> p (o k) f", p=P)

        with ExitStack() as st:
            wB = Mem(nc, st).sb("weights_b", [P, 2, E, (F0 // P) * D], F16)
            route(nc, g, a["routerT"],
                  [(rows_of(a["w1T"], k, 1), blocks(wA, k * F0)) for k in range(2)],
                  [(rows_of(a["w2T"], 4 * k, 4), blocks(wB, k * PIECE)) for k in range(2)])
            g.up_w = lambda part, e, k, f: block_of(wA, part, e, k * F0 + f * P, P)
            g.down_w = lambda part, e, f: block_of(wB, part, e, f * D, D)
            experts(nc, g, a, 0)
        with ExitStack() as st:
            m = Mem(nc, st)
            at = Names()
            at.k = m.sb("kbd", [P, B, 2, 8, M])
            at.v = m.sb("vpad", [M, B, H1, 32])
            at.bias = m.sb("bias1", [P, B, M])
            at.wq = m.sb("wq1", [P, 2, D])
            at.wo = m.sb("wo1", [P, 2, D])
            attention1_context(nc, g, a, at)
            attention1(nc, g, at)
        g.phase = "e1_"
        with ExitStack() as st:
            w3 = Mem(nc, st).sb("weights_3", [P, 2, E, (F1 // P) * D], F16)
            route(nc, g, a["gate"],
                  [(rows_of(a["u1"], 0, 2), blocks(wA, 0)), (rows_of(a["u2"], 0, 2), blocks(wA, PIECE))],
                  [(rows_of(a["u3"], 0, 4), blocks(w3, 0))])
            g.up_w = lambda part, e, k, f: block_of(wA, part, e, f // 4 * PIECE + k * F1 + f % 4 * P, P)
            g.down_w = lambda part, e, f: block_of(w3, part, e, f * D, D)
            experts(nc, g, a, 1)
        combine(nc, g, out)


def kernel(**inputs):
    import concourse.bacc as bacc
    from concourse.bass_utils import run_bass_kernel_spmd
    nc = bacc.Bacc("TRN2", target_bir_lowering=False, num_devices=1)
    arrays = {f"in_{name}": array for name, array in host_arrays(inputs).items()}
    views = {name[3:]: nc.dram_tensor(name, array.shape, mybir.dt.from_np(array.dtype), kind="ExternalInput").ap()
             for name, array in arrays.items()}
    out = nc.dram_tensor("out_dram", (B, S, D), F32, kind="ExternalOutput").ap()
    program(nc, views, out.rearrange("b s d -> (b s) d"))
    return run_bass_kernel_spmd(nc, [arrays], core_ids=[0]).results[0]["out_dram"]
```
